# Optimizing a Trainium2 kernel written in Bass

```python
import numpy as np
import jax
import jax.numpy as jnp

def _softmax(x, axis=-1):
    return jax.nn.softmax(x, axis=axis)

def _gelu(x):
    return jax.nn.gelu(x, approximate=True)

def _silu(x):
    return jax.nn.silu(x)

def _sigmoid(x):
    return jax.nn.sigmoid(x)

def _layernorm(x, axis=-1, eps=1e-05):
    m = jnp.mean(x, axis=axis, keepdims=True)
    v = jnp.var(x, axis=axis, keepdims=True)
    return (x - m) / jnp.sqrt(v + eps)

def _scatter_add(tgt, idx, src, axis=0):
    return tgt.at[idx].add(src)

def _segment_sum(src, seg, n):
    return jax.ops.segment_sum(src, seg, n)
kernel_name = 'mk_flamingo_gated_d4_seqx_r8_815973'

def setup_inputs(seed: int=0):
    np.random.seed(seed)
    _w = jnp.asarray

    def _rec_inputs():
        import jax
        import jax.numpy as jnp
        _rk = jax.random.key(seed)
        x = 7.22e-05 + 1 * jax.random.normal(jax.random.fold_in(_rk, 1), (32, 128, 128), jnp.float32)
        _lenS = 128 - jax.random.randint(jax.random.fold_in(_rk, 7), (32,), 0, max(1, 128 // 4) + 1, jnp.int32)
        _lenS2 = 128 - jax.random.randint(jax.random.fold_in(_rk, 8), (32,), 0, max(1, 128 // 4) + 1, jnp.int32)
        _ctx_1024P = jax.random.normal(jax.random.fold_in(_rk, 11), (32, 16, 128), jnp.float32)
        _ctx_1024c = jax.random.dirichlet(jax.random.fold_in(_rk, 511), 0.3 * jnp.ones((16,), jnp.float32), (32, 128))
        _ctx_1024t = jnp.einsum('bsk,bkd->bsd', _ctx_1024c, _ctx_1024P)
        _ctx_1024t = _ctx_1024t * jax.lax.rsqrt(jnp.mean(jnp.square(_ctx_1024t)) + 1e-12) * 0.953939
        ctx_1024 = 4.13588e-05 + 0.999923 * (_ctx_1024t + 0.3 * jax.random.normal(jax.random.fold_in(_rk, 611), (32, 128, 128), jnp.float32))
        _g = jax.random.normal(jax.random.fold_in(_rk, 9001), (2, 4), jnp.float32)
        _g = jnp.sign(_g) * jnp.maximum(jnp.abs(_g), 1.0) + (_g == 0) * 1.0
        g_xattn = _g[0]
        g_ffn = _g[1]
        return (x, ctx_1024, g_xattn, g_ffn)
    x, ctx_1024, g_xattn, g_ffn = _rec_inputs()

    def _L0_xattn_setup():
        import jax, jax.numpy as jnp
        import numpy as np
        B, S, D = (4, 256, 128)
        H = 16
        DH = D // H
        THETA = 10000.0

        def _rope_tables(seq_len, d_head, theta, dtype):
            inv_freq = 1.0 / theta ** (jnp.arange(0, d_head, 2, dtype=jnp.float32) / d_head)
            ang = jnp.arange(seq_len, dtype=jnp.float32)[:, None] * inv_freq[None, :]
            return (jnp.sin(ang).astype(dtype), jnp.cos(ang).astype(dtype))

        def _apply_rope(x, sin, cos):
            x1 = x[..., 0::2]
            x2 = x[..., 1::2]
            x1r = x1 * cos - x2 * sin
            x2r = x1 * sin + x2 * cos
            return jnp.stack([x1r, x2r], axis=-1).reshape(x.shape)
        key = jax.random.key(seed)
        ks = jax.random.split(key, 7)
        scale = 1.0 / np.sqrt(D)
        return {'Q': jax.random.normal(ks[0], (B, S, D), dtype=jnp.float32), 'K': jax.random.normal(ks[1], (B, S, D), dtype=jnp.float32), 'V': jax.random.normal(ks[2], (B, S, D), dtype=jnp.float32), 'Wq': jax.random.normal(ks[3], (D, D), dtype=jnp.float32) * scale, 'Wk': jax.random.normal(ks[4], (D, D), dtype=jnp.float32) * scale, 'Wv': jax.random.normal(ks[5], (D, D), dtype=jnp.float32) * scale, 'Wo': jax.random.normal(ks[6], (D, D), dtype=jnp.float32) * scale}
    _L0_xattn_all = _L0_xattn_setup()
    _L0_xattn_in = {k: v for k, v in _L0_xattn_all.items() if k in ('Wq', 'Wk', 'Wv', 'Wo')}
    del _L0_xattn_all

    def _L0_ffn_setup():
        import jax, jax.numpy as jnp
        import numpy as np
        B, S, D = (4, 256, 128)
        E, K = (8, 2)
        H = 176
        key = jax.random.key(seed)
        kx, kr, k1, k2, k3 = jax.random.split(key, 5)
        s = 0.02
        return {'x': jax.random.normal(kx, (B, S, D), dtype=jnp.float32), 'w_router': jax.random.normal(kr, (E, D), dtype=jnp.float32) * s, 'w1': jax.random.normal(k1, (E, D, H), dtype=jnp.float32) * s, 'w2': jax.random.normal(k2, (E, H, D), dtype=jnp.float32) * s, 'w3': jax.random.normal(k3, (E, D, H), dtype=jnp.float32) * s}
    _L0_ffn_all = _L0_ffn_setup()
    _L0_ffn_in = {k: v for k, v in _L0_ffn_all.items() if k in ('w_router', 'w1', 'w2', 'w3')}
    del _L0_ffn_all

    def _L1_xattn_setup():
        import jax, jax.numpy as jnp
        import numpy as np
        B, S, D, H = (4, 256, 128, 16)
        DH = D // H

        def _split_heads(x):
            b, s, _ = x.shape
            return x.reshape(b, s, H, DH).transpose(0, 2, 1, 3)
        key = jax.random.key(seed)
        ks = jax.random.split(key, 11)
        s = 1.0 / np.sqrt(D)
        return {'q': jax.random.normal(ks[0], (B, S, D), jnp.float32), 'k': jax.random.normal(ks[1], (B, S, D), jnp.float32), 'v': jax.random.normal(ks[2], (B, S, D), jnp.float32), 'Wq': jax.random.normal(ks[3], (D, D), jnp.float32) * s, 'bq': jnp.zeros((D,), jnp.float32), 'Wk': jax.random.normal(ks[4], (D, D), jnp.float32) * s, 'bk': jnp.zeros((D,), jnp.float32), 'Wv': jax.random.normal(ks[5], (D, D), jnp.float32) * s, 'bv': jnp.zeros((D,), jnp.float32), 'Wo': jax.random.normal(ks[6], (D, D), jnp.float32) * s, 'bo': jnp.zeros((D,), jnp.float32)}
    _L1_xattn_all = _L1_xattn_setup()
    _L1_xattn_in = {k: v for k, v in _L1_xattn_all.items() if k in ('Wq', 'bq', 'Wk', 'bk', 'Wv', 'bv', 'Wo', 'bo')}
    del _L1_xattn_all

    def _L1_ffn_setup():
        import jax, jax.numpy as jnp
        import numpy as np
        H_DIM, E_DIM = (128, 64)
        N_SHARED, N_ROUTED, TOP_K = (2, 16, 4)
        B, S = (4, 256)
        key = jax.random.key(seed)
        ks = jax.random.split(key, 6)
        sc = 1.0 / np.sqrt(H_DIM)
        ec = 1.0 / np.sqrt(E_DIM)
        return {'x': jax.random.normal(ks[0], (B, S, H_DIM), dtype=jnp.float32), 'shared_up': jax.random.uniform(ks[1], (N_SHARED, E_DIM, H_DIM), jnp.float32, -sc, sc), 'shared_down': jax.random.uniform(ks[2], (N_SHARED, H_DIM, E_DIM), jnp.float32, -ec, ec), 'routed_up': jax.random.uniform(ks[3], (N_ROUTED, E_DIM, H_DIM), jnp.float32, -sc, sc), 'routed_down': jax.random.uniform(ks[4], (N_ROUTED, H_DIM, E_DIM), jnp.float32, -ec, ec), 'router_w': jax.random.uniform(ks[5], (N_ROUTED, H_DIM), jnp.float32, -sc, sc)}
    _L1_ffn_all = _L1_ffn_setup()
    _L1_ffn_in = {k: v for k, v in _L1_ffn_all.items() if k in ('shared_up', 'shared_down', 'routed_up', 'routed_down', 'router_w')}
    del _L1_ffn_all

    def _L2_xattn_setup():
        import jax, jax.numpy as jnp
        import numpy as np
        DIM = 128
        NUM_HEADS = 16
        DIM_HEAD = 64
        INNER = NUM_HEADS * DIM_HEAD
        SCALE = DIM_HEAD ** (-0.5)

        def _layernorm(x, gamma, beta, eps=1e-05):
            mu = jnp.mean(x, axis=-1, keepdims=True)
            var = jnp.mean(jnp.square(x - mu), axis=-1, keepdims=True)
            return (x - mu) * jax.lax.rsqrt(var + eps) * gamma + beta
        key = jax.random.key(seed)
        ks = jax.random.split(key, 8)
        B, SQ, SK = (2, 256, 512)
        x = jax.random.normal(ks[0], (B, SQ, DIM), dtype=jnp.float32)
        context = jax.random.normal(ks[1], (B, SK, DIM), dtype=jnp.float32)
        ln_gamma = jnp.ones((DIM,), jnp.float32)
        ln_beta = jnp.zeros((DIM,), jnp.float32)
        w_q = jax.random.normal(ks[2], (DIM, INNER), dtype=jnp.float32) / np.sqrt(DIM)
        w_kv = jax.random.normal(ks[3], (DIM, 2 * INNER), dtype=jnp.float32) / np.sqrt(DIM)
        w_out = jax.random.normal(ks[4], (INNER, DIM), dtype=jnp.float32) / np.sqrt(INNER)
        b_out = jnp.zeros((DIM,), jnp.float32)
        gate = jnp.array([0.5], jnp.float32)
        return {'x': x, 'context': context, 'ln_gamma': ln_gamma, 'ln_beta': ln_beta, 'w_q': w_q, 'w_kv': w_kv, 'w_out': w_out, 'b_out': b_out, 'gate': gate}
    _L2_xattn_all = _L2_xattn_setup()
    _L2_xattn_in = {k: v for k, v in _L2_xattn_all.items() if k in ('ln_gamma', 'ln_beta', 'w_q', 'w_kv', 'w_out', 'b_out', 'gate')}
    del _L2_xattn_all

    def _L2_ffn_setup():
        import jax, jax.numpy as jnp
        import numpy as np
        DIM = 128

        def _reference_tuple_inner(x, W_r, W_k, W_v, mu_r, mu_k):
            B, T, C = x.shape
            x_prev = jnp.concatenate([jnp.zeros((B, 1, C), x.dtype), x[:, :-1, :]], axis=1)
            xr = mu_r * x + (1.0 - mu_r) * x_prev
            xk = mu_k * x + (1.0 - mu_k) * x_prev
            r = jax.nn.sigmoid(jnp.einsum('btc,dc->btd', xr, W_r))
            k = jnp.einsum('btc,dc->btd', xk, W_k)
            k_act = jnp.square(jax.nn.relu(k))
            out = r * jnp.einsum('btc,dc->btd', k_act, W_v)
            new_state = x[:, -1, :]
            return (out, new_state)
        key = jax.random.key(seed)
        ks = jax.random.split(key, 6)
        B, T, C = (8, 256, DIM)
        x = jax.random.normal(ks[0], (B, T, C), dtype=jnp.float32)
        s = 1.0 / np.sqrt(C)
        W_r = jax.random.uniform(ks[1], (C, C), jnp.float32, -s, s)
        W_k = jax.random.uniform(ks[2], (C, C), jnp.float32, -s, s)
        W_v = jax.random.uniform(ks[3], (C, C), jnp.float32, -s, s)
        mu_r = jax.random.uniform(ks[4], (C,), jnp.float32)
        mu_k = jax.random.uniform(ks[5], (C,), jnp.float32)
        return {'x': x, 'W_r': W_r, 'W_k': W_k, 'W_v': W_v, 'mu_r': mu_r, 'mu_k': mu_k}
    _L2_ffn_all = _L2_ffn_setup()
    _L2_ffn_in = {k: v for k, v in _L2_ffn_all.items() if k in ('W_r', 'W_k', 'W_v', 'mu_r', 'mu_k')}
    del _L2_ffn_all

    def _L3_xattn_setup():
        import jax, jax.numpy as jnp
        import numpy as np
        EMBED_DIM = 128
        NUM_HEADS = 16
        HEAD_DIM = EMBED_DIM // NUM_HEADS
        B, T, S = (2, 256, 256)
        key = jax.random.key(seed)
        ks = jax.random.split(key, 5)
        scale_w = 1.0 / np.sqrt(EMBED_DIM)
        return {'q': jax.random.normal(ks[0], (B, T, EMBED_DIM), dtype=jnp.float32), 'k': jax.random.normal(ks[1], (B, S, EMBED_DIM), dtype=jnp.float32), 'v': jax.random.normal(ks[2], (B, S, EMBED_DIM), dtype=jnp.float32), 'in_proj_weight': jax.random.normal(ks[3], (3 * EMBED_DIM, EMBED_DIM), dtype=jnp.float32) * scale_w, 'in_proj_bias': jnp.zeros((3 * EMBED_DIM,), dtype=jnp.float32), 'out_w': jax.random.normal(ks[4], (EMBED_DIM, EMBED_DIM), dtype=jnp.float32) * scale_w, 'out_b': jnp.zeros((EMBED_DIM,), dtype=jnp.float32)}
    _L3_xattn_all = _L3_xattn_setup()
    _L3_xattn_in = {k: v for k, v in _L3_xattn_all.items() if k in ('in_proj_weight', 'in_proj_bias', 'out_w', 'out_b')}
    del _L3_xattn_all

    def _L3_ffn_setup():
        import jax, jax.numpy as jnp
        import numpy as np
        B, S, D, F, E = (4, 256, 128, 512, 8)
        key = jax.random.key(seed)
        ks = jax.random.split(key, 7)
        s1 = 1.0 / np.sqrt(D)
        s2 = 1.0 / np.sqrt(F)
        x = jax.random.normal(ks[0], (B, S, D), dtype=jnp.float32)
        W1 = jax.random.uniform(ks[1], (E, D, F), jnp.float32, -s1, s1)
        b1 = jax.random.uniform(ks[2], (E, F), jnp.float32, -s1, s1)
        W2 = jax.random.uniform(ks[3], (E, F, D), jnp.float32, -s2, s2)
        b2 = jax.random.uniform(ks[4], (E, D), jnp.float32, -s2, s2)
        Wr = jax.random.uniform(ks[5], (D, E), jnp.float32, -s1, s1)
        br = jax.random.uniform(ks[6], (E,), jnp.float32, -s1, s1)
        return {'x': x, 'W1': W1, 'b1': b1, 'W2': W2, 'b2': b2, 'Wr': Wr, 'br': br}
    _L3_ffn_all = _L3_ffn_setup()
    _L3_ffn_in = {k: v for k, v in _L3_ffn_all.items() if k in ('W1', 'b1', 'W2', 'b2', 'Wr', 'br')}
    del _L3_ffn_all
    return {'x': x, 'ctx_1024': ctx_1024, 'g_xattn': g_xattn, 'g_ffn': g_ffn, 'L0_xattn_Wq': _L0_xattn_in['Wq'], 'L0_xattn_Wk': _L0_xattn_in['Wk'], 'L0_xattn_Wv': _L0_xattn_in['Wv'], 'L0_xattn_Wo': _L0_xattn_in['Wo'], 'L0_ffn_w_router': _L0_ffn_in['w_router'], 'L0_ffn_w1': _L0_ffn_in['w1'], 'L0_ffn_w2': _L0_ffn_in['w2'], 'L0_ffn_w3': _L0_ffn_in['w3'], 'L1_xattn_Wq': _L1_xattn_in['Wq'], 'L1_xattn_bq': _L1_xattn_in['bq'], 'L1_xattn_Wk': _L1_xattn_in['Wk'], 'L1_xattn_bk': _L1_xattn_in['bk'], 'L1_xattn_Wv': _L1_xattn_in['Wv'], 'L1_xattn_bv': _L1_xattn_in['bv'], 'L1_xattn_Wo': _L1_xattn_in['Wo'], 'L1_xattn_bo': _L1_xattn_in['bo'], 'L1_ffn_shared_up': _L1_ffn_in['shared_up'], 'L1_ffn_shared_down': _L1_ffn_in['shared_down'], 'L1_ffn_routed_up': _L1_ffn_in['routed_up'], 'L1_ffn_routed_down': _L1_ffn_in['routed_down'], 'L1_ffn_router_w': _L1_ffn_in['router_w'], 'L2_xattn_ln_gamma': _L2_xattn_in['ln_gamma'], 'L2_xattn_ln_beta': _L2_xattn_in['ln_beta'], 'L2_xattn_w_q': _L2_xattn_in['w_q'], 'L2_xattn_w_kv': _L2_xattn_in['w_kv'], 'L2_xattn_w_out': _L2_xattn_in['w_out'], 'L2_xattn_b_out': _L2_xattn_in['b_out'], 'L2_xattn_gate': _L2_xattn_in['gate'], 'L2_ffn_W_r': _L2_ffn_in['W_r'], 'L2_ffn_W_k': _L2_ffn_in['W_k'], 'L2_ffn_W_v': _L2_ffn_in['W_v'], 'L2_ffn_mu_r': _L2_ffn_in['mu_r'], 'L2_ffn_mu_k': _L2_ffn_in['mu_k'], 'L3_xattn_in_proj_weight': _L3_xattn_in['in_proj_weight'], 'L3_xattn_in_proj_bias': _L3_xattn_in['in_proj_bias'], 'L3_xattn_out_w': _L3_xattn_in['out_w'], 'L3_xattn_out_b': _L3_xattn_in['out_b'], 'L3_ffn_W1': _L3_ffn_in['W1'], 'L3_ffn_b1': _L3_ffn_in['b1'], 'L3_ffn_W2': _L3_ffn_in['W2'], 'L3_ffn_b2': _L3_ffn_in['b2'], 'L3_ffn_Wr': _L3_ffn_in['Wr'], 'L3_ffn_br': _L3_ffn_in['br']}

def reference(x, ctx_1024, g_xattn, g_ffn, L0_xattn_Wq, L0_xattn_Wk, L0_xattn_Wv, L0_xattn_Wo, L0_ffn_w_router, L0_ffn_w1, L0_ffn_w2, L0_ffn_w3, L1_xattn_Wq, L1_xattn_bq, L1_xattn_Wk, L1_xattn_bk, L1_xattn_Wv, L1_xattn_bv, L1_xattn_Wo, L1_xattn_bo, L1_ffn_shared_up, L1_ffn_shared_down, L1_ffn_routed_up, L1_ffn_routed_down, L1_ffn_router_w, L2_xattn_ln_gamma, L2_xattn_ln_beta, L2_xattn_w_q, L2_xattn_w_kv, L2_xattn_w_out, L2_xattn_b_out, L2_xattn_gate, L2_ffn_W_r, L2_ffn_W_k, L2_ffn_W_v, L2_ffn_mu_r, L2_ffn_mu_k, L3_xattn_in_proj_weight, L3_xattn_in_proj_bias, L3_xattn_out_w, L3_xattn_out_b, L3_ffn_W1, L3_ffn_b1, L3_ffn_W2, L3_ffn_b2, L3_ffn_Wr, L3_ffn_br):
    import jax
    import jax.numpy as jnp

    def _L0_xattn_ref(Q, K, V, Wq, Wk, Wv, Wo):
        import jax, jax.numpy as jnp
        import numpy as np
        B, S, D = (4, 256, 128)
        H = 16
        DH = D // H
        THETA = 10000.0

        def _rope_tables(seq_len, d_head, theta, dtype):
            inv_freq = 1.0 / theta ** (jnp.arange(0, d_head, 2, dtype=jnp.float32) / d_head)
            ang = jnp.arange(seq_len, dtype=jnp.float32)[:, None] * inv_freq[None, :]
            return (jnp.sin(ang).astype(dtype), jnp.cos(ang).astype(dtype))

        def _apply_rope(x, sin, cos):
            x1 = x[..., 0::2]
            x2 = x[..., 1::2]
            x1r = x1 * cos - x2 * sin
            x2r = x1 * sin + x2 * cos
            return jnp.stack([x1r, x2r], axis=-1).reshape(x.shape)
        seq_len = Q.shape[-2]
        q = Q @ Wq.T
        k = K @ Wk.T
        v = V @ Wv.T

        def split(x):
            return x.reshape(x.shape[0], seq_len, H, DH).transpose(0, 2, 1, 3)
        qh, kh, vh = (split(q), split(k), split(v))
        sin, cos = _rope_tables(seq_len, DH, THETA, qh.dtype)
        qh = _apply_rope(qh, sin, cos)
        kh = _apply_rope(kh, sin, cos)
        qf = qh.astype(jnp.float32)
        kf = kh.astype(jnp.float32)
        vf = vh.astype(jnp.float32)
        scale = 1.0 / np.sqrt(DH)
        scores = jnp.einsum('bhqd,bhkd->bhqk', qf, kf) * scale
        causal = jnp.tril(jnp.ones((seq_len, seq_len), dtype=bool))
        scores = jnp.where(causal, scores, -jnp.inf)
        attn = jax.nn.softmax(scores, axis=-1)
        out_h = jnp.einsum('bhqk,bhkd->bhqd', attn, vf).astype(Q.dtype)
        out = out_h.transpose(0, 2, 1, 3).reshape(Q.shape[0], seq_len, D)
        return out @ Wo.T

    def _L0_ffn_ref(x, w_router, w1, w2, w3):
        import jax, jax.numpy as jnp
        import numpy as np
        B, S, D = (4, 256, 128)
        E, K = (8, 2)
        H = 176
        bsz, seqlen, dim = x.shape
        xf = x.reshape(-1, dim)
        scores = jax.nn.softmax(xf @ w_router.T, axis=-1)
        expert_weights, expert_indices = jax.lax.top_k(scores, K)
        h = jax.nn.silu(jnp.einsum('td,edh->eth', xf, w1)) * jnp.einsum('td,edh->eth', xf, w3)
        y = jnp.einsum('eth,ehd->etd', h, w2)
        y_t = jnp.swapaxes(y, 0, 1)
        sel = jnp.take_along_axis(y_t, expert_indices[:, :, None], axis=1)
        out = jnp.sum(expert_weights[:, :, None] * sel, axis=1)
        return out.reshape(bsz, seqlen, dim)

    def _L1_xattn_ref(q, k, v, Wq, bq, Wk, bk, Wv, bv, Wo, bo):
        import jax, jax.numpy as jnp
        import numpy as np
        B, S, D, H = (4, 256, 128, 16)
        DH = D // H

        def _split_heads(x):
            b, s, _ = x.shape
            return x.reshape(b, s, H, DH).transpose(0, 2, 1, 3)
        qh = _split_heads(q @ Wq.T + bq)
        kh = _split_heads(k @ Wk.T + bk)
        vh = _split_heads(v @ Wv.T + bv)
        scale = 1.0 / jnp.sqrt(jnp.asarray(DH, qh.dtype))
        scores = jnp.einsum('bhqd,bhkd->bhqk', qh, kh) * scale
        probs = jax.nn.softmax(scores, axis=-1)
        ctx = jnp.einsum('bhqk,bhkd->bhqd', probs, vh)
        x = ctx.transpose(0, 2, 1, 3).reshape(q.shape[0], -1, D)
        return x @ Wo.T + bo

    def _L1_ffn_ref(x, shared_up, shared_down, routed_up, routed_down, router_w):
        import jax, jax.numpy as jnp
        import numpy as np
        H_DIM, E_DIM = (128, 64)
        N_SHARED, N_ROUTED, TOP_K = (2, 16, 4)
        B, S = (4, 256)
        b, s, h = x.shape
        xt = x.reshape(-1, h)
        up_s = jnp.einsum('th,seh->tse', xt, shared_up)
        shared = jnp.einsum('tse,she->th', jax.nn.gelu(up_s, approximate=False), shared_down)
        probs = jax.nn.softmax(xt @ router_w.T, axis=-1)
        topk_p, topk_i = jax.lax.top_k(probs, TOP_K)
        gate = jnp.zeros_like(probs).at[jnp.arange(xt.shape[0])[:, None], topk_i].add(topk_p)
        up_r = jnp.einsum('th,reh->tre', xt, routed_up)
        act = jax.nn.gelu(up_r, approximate=False) * gate[:, :, None]
        routed = jnp.einsum('tre,rhe->th', act, routed_down)
        return (shared + routed).reshape(b, s, h)

    def _L2_xattn_ref(x, context, ln_gamma, ln_beta, w_q, w_kv, w_out, b_out, gate):
        import jax, jax.numpy as jnp
        import numpy as np
        DIM = 128
        NUM_HEADS = 16
        DIM_HEAD = 64
        INNER = NUM_HEADS * DIM_HEAD
        SCALE = DIM_HEAD ** (-0.5)

        def _layernorm(x, gamma, beta, eps=1e-05):
            mu = jnp.mean(x, axis=-1, keepdims=True)
            var = jnp.mean(jnp.square(x - mu), axis=-1, keepdims=True)
            return (x - mu) * jax.lax.rsqrt(var + eps) * gamma + beta
        B, SQ, _ = x.shape
        SK = context.shape[1]
        xn = _layernorm(x, ln_gamma, ln_beta)
        q = (xn @ w_q).reshape(B, SQ, NUM_HEADS, DIM_HEAD)
        kv = context @ w_kv
        k, v = jnp.split(kv, 2, axis=-1)
        k = k.reshape(B, SK, NUM_HEADS, DIM_HEAD)
        v = v.reshape(B, SK, NUM_HEADS, DIM_HEAD)
        scores = jnp.einsum('bqhd,bkhd->bhqk', q * SCALE, k)
        attn = jax.nn.softmax(scores, axis=-1)
        out = jnp.einsum('bhqk,bkhd->bqhd', attn, v).reshape(B, SQ, INNER)
        out = out @ w_out + b_out
        return out * jnp.tanh(gate[0])

    def _L2_ffn_ref(x, W_r, W_k, W_v, mu_r, mu_k):
        import jax, jax.numpy as jnp
        import numpy as np
        DIM = 128

        def _reference_tuple_inner(x, W_r, W_k, W_v, mu_r, mu_k):
            B, T, C = x.shape
            x_prev = jnp.concatenate([jnp.zeros((B, 1, C), x.dtype), x[:, :-1, :]], axis=1)
            xr = mu_r * x + (1.0 - mu_r) * x_prev
            xk = mu_k * x + (1.0 - mu_k) * x_prev
            r = jax.nn.sigmoid(jnp.einsum('btc,dc->btd', xr, W_r))
            k = jnp.einsum('btc,dc->btd', xk, W_k)
            k_act = jnp.square(jax.nn.relu(k))
            out = r * jnp.einsum('btc,dc->btd', k_act, W_v)
            new_state = x[:, -1, :]
            return (out, new_state)
        return _reference_tuple_inner(x, W_r, W_k, W_v, mu_r, mu_k)[0]

    def _L3_xattn_ref(q, k, v, in_proj_weight, in_proj_bias, out_w, out_b):
        import jax, jax.numpy as jnp
        import numpy as np
        EMBED_DIM = 128
        NUM_HEADS = 16
        HEAD_DIM = EMBED_DIM // NUM_HEADS
        B, T, S = (2, 256, 256)
        H, D = (NUM_HEADS, HEAD_DIM)
        w_q, w_k, w_v = jnp.split(in_proj_weight, 3, axis=0)
        b_q, b_k, b_v = jnp.split(in_proj_bias, 3, axis=0)
        qp = q @ w_q.T + b_q
        kp = k @ w_k.T + b_k
        vp = v @ w_v.T + b_v
        bsz, t, _ = qp.shape
        s = kp.shape[1]
        qh = qp.reshape(bsz, t, H, D).transpose(0, 2, 1, 3)
        kh = kp.reshape(bsz, s, H, D).transpose(0, 2, 1, 3)
        vh = vp.reshape(bsz, s, H, D).transpose(0, 2, 1, 3)
        scale = D ** (-0.5)
        attn = jnp.einsum('bhtd,bhsd->bhts', qh, kh) * scale
        attn = jax.nn.softmax(attn, axis=-1)
        ctx = jnp.einsum('bhts,bhsd->bhtd', attn, vh)
        ctx = ctx.transpose(0, 2, 1, 3).reshape(bsz, t, H * D)
        out = ctx @ out_w.T + out_b
        return out

    def _L3_ffn_ref(x, W1, b1, W2, b2, Wr, br):
        import jax, jax.numpy as jnp
        import numpy as np
        B, S, D, F, E = (4, 256, 128, 512, 8)
        b, s, d = x.shape
        e = Wr.shape[1]
        logits = x @ Wr + br
        idx = jnp.argmax(logits, axis=-1)
        probs = jax.nn.softmax(logits, axis=-1)
        gates = jnp.take_along_axis(probs, idx[..., None], axis=-1)[..., 0]
        xf = x.reshape(-1, d)
        idxf = idx.reshape(-1)
        gf = gates.reshape(-1)
        out = jnp.zeros_like(xf)
        for ei in range(e):
            h = jax.nn.gelu(xf @ W1[ei] + b1[ei], approximate=False)
            y = h @ W2[ei] + b2[ei]
            mask = (idxf == ei).astype(xf.dtype)
            out = out + y * (gf * mask)[:, None]
        return out.reshape(b, s, d)
    x = x + jnp.tanh(g_xattn[0]) * _L0_xattn_ref(_layernorm(x, axis=-1), ctx_1024, ctx_1024, L0_xattn_Wq, L0_xattn_Wk, L0_xattn_Wv, L0_xattn_Wo)
    x = x + jnp.tanh(g_ffn[0]) * _L0_ffn_ref(_layernorm(x, axis=-1), L0_ffn_w_router, L0_ffn_w1, L0_ffn_w2, L0_ffn_w3)
    x = x + jnp.tanh(g_xattn[1]) * _L1_xattn_ref(_layernorm(x, axis=-1), ctx_1024, ctx_1024, L1_xattn_Wq, L1_xattn_bq, L1_xattn_Wk, L1_xattn_bk, L1_xattn_Wv, L1_xattn_bv, L1_xattn_Wo, L1_xattn_bo)
    x = x + jnp.tanh(g_ffn[1]) * _L1_ffn_ref(_layernorm(x, axis=-1), L1_ffn_shared_up, L1_ffn_shared_down, L1_ffn_routed_up, L1_ffn_routed_down, L1_ffn_router_w)
    x = x + jnp.tanh(g_xattn[2]) * _L2_xattn_ref(_layernorm(x, axis=-1), ctx_1024, L2_xattn_ln_gamma, L2_xattn_ln_beta, L2_xattn_w_q, L2_xattn_w_kv, L2_xattn_w_out, L2_xattn_b_out, L2_xattn_gate)
    x = x + jnp.tanh(g_ffn[2]) * _L2_ffn_ref(_layernorm(x, axis=-1), L2_ffn_W_r, L2_ffn_W_k, L2_ffn_W_v, L2_ffn_mu_r, L2_ffn_mu_k)
    x = x + jnp.tanh(g_xattn[3]) * _L3_xattn_ref(_layernorm(x, axis=-1), ctx_1024, ctx_1024, L3_xattn_in_proj_weight, L3_xattn_in_proj_bias, L3_xattn_out_w, L3_xattn_out_b)
    x = x + jnp.tanh(g_ffn[3]) * _L3_ffn_ref(_layernorm(x, axis=-1), L3_ffn_W1, L3_ffn_b1, L3_ffn_W2, L3_ffn_b2, L3_ffn_Wr, L3_ffn_br)
    return x

_drawn_inputs = setup_inputs


def setup_inputs(seed=0):
    import zlib

    import numpy as np

    out = dict(_drawn_inputs(seed))
    spreads = {'L1_xattn_bq': (0.0, 1.101),
     'L1_xattn_bk': (0.0, 2.0),
     'L1_xattn_bv': (0.0, 0.317),
     'L1_xattn_bo': (0.0, 0.1),
     'L2_xattn_ln_gamma': (1.0, 0.6),
     'L2_xattn_ln_beta': (0.0, 2.0),
     'L2_xattn_b_out': (0.0, 0.647),
     'L3_xattn_in_proj_bias': (0.0, 0.32),
     'L3_xattn_out_b': (0.0, 0.341)}
    factors = {'g_ffn': 45.504,
     'L0_ffn_w_router': 8.0,
     'L0_ffn_w1': 8.0,
     'L0_ffn_w2': 8.0,
     'L0_ffn_w3': 8.0,
     'L2_ffn_W_r': 4.342,
     'L2_ffn_mu_r': 80.057,
     'L3_ffn_b1': 32.59,
     'L3_ffn_b2': 24.648,
     'L3_ffn_br': 15.202,
     'L1_ffn_routed_up': 3.812,
     'L1_ffn_routed_down': 3.516,
     'L1_ffn_router_w': 3.916,
     'L3_ffn_W1': 3.088,
     'L2_ffn_mu_k': 2.787}
    for name, (base, spread) in spreads.items():
        noise = np.random.default_rng([zlib.crc32(name.encode()), seed]).standard_normal(out[name].shape)
        drawn = base * np.exp(spread * noise) if base else spread * noise
        out[name] = jnp.asarray(drawn.astype(out[name].dtype))
    for name, factor in factors.items():
        out[name] = (out[name] * factor).astype(out[name].dtype)
    return out
```

```python
from contextlib import ExitStack

import numpy as np

import concourse.bass as bass
from concourse import mybir

F32, BF16, FP16 = mybir.dt.float32, mybir.dt.bfloat16, mybir.dt.float16
ALU = mybir.AluOpType
ACT = mybir.ActivationFunctionType
AX = mybir.AxisListType.X

S = 128
D = 128
H = 16
LN_EPS = 1e-5
MASKED = -1e30
HEAD_DIMS = (8, 8, 64, 8)
ROW_TILE = 32


def wait(eng, sem, count):
    if isinstance(count, int) and count <= 0:
        return
    eng.wait_ge(sem, count)


def shape_constants(B):
    c = {}
    c["ident"] = np.eye(128, dtype=np.float32)
    sel = np.zeros((128, 2, 2, 4, 128), np.float32)
    for t, order in enumerate(((0, 0, 1, 1), (0, 1, 0, 1))):
        for j in range(4):
            for cc in range(4):
                for r, part in enumerate(order):
                    for d in range(8):
                        sel[8 * (4 * j + cc) + d, t, part, cc, 32 * j + 8 * r + d] = 1.0
    c["stack_sel"] = sel.reshape(128, -1).astype(np.float16)
    small = np.zeros((128, 4, 128), np.float32)
    for j in range(4):
        for k in range(4):
            small[32 * j + k, k, :] = 1.0
            small[32 * j + 4 + k, k, :] = 1.0
    wide = np.zeros((128, 8, 128), np.float32)
    for j in range(2):
        for u in range(2):
            for k in range(4):
                wide[64 * j + 4 * u + k, 4 * u + k, :] = 1.0
                wide[64 * j + 8 + 4 * u + k, 4 * u + k, :] = 1.0
    c["max_rows"] = np.concatenate([small, wide], 1).reshape(128, -1)
    q, k = np.meshgrid(np.arange(S), np.arange(S), indexing="ij")
    hidden = np.where(k > q, MASKED, 0.0).astype(np.float32)
    c["causal"] = np.concatenate([hidden, hidden.T], 1)
    freq = (1.0 / np.float32(10000.0) ** (np.arange(0, 8, 2, dtype=np.float32) / np.float32(8))).astype(np.float32)
    ang = np.arange(S, dtype=np.float32)[:, None] * freq[None, :]
    cos, sin = np.cos(ang).astype(np.float32), np.sin(ang).astype(np.float32)
    i = (np.arange(D) % 8) // 2
    sign = np.where(np.arange(D) % 2 == 0, -1.0, 1.0).astype(np.float32)
    c["rope"] = np.concatenate([cos[:, i].T, sin[:, i].T * sign[:, None]], 1)
    c["zero_cols"] = np.zeros((128, 4), np.float32)
    c["zero_row"] = np.zeros((1, 128), np.float32)
    c["gate_sel0"] = gate_rows(8, [[(e, r) for r in range(128) for e in [(128 * t + r) // 176]] for t in range(11)], 11)
    c["gate_sel1"] = gate_rows(16, [[(2 * t + r // 64, r) for r in range(128)] for t in range(8)], 8)
    c["gate_sel3"] = gate_rows(8, [[(e, r) for r in range(128)] for e in range(8)], 8)
    return c


def gate_rows(E, tiles, n):
    g = np.zeros((128, n, 128), np.float32)
    for t, pairs in enumerate(tiles):
        for e, r in pairs:
            for part in range(3):
                g[part * E + e, t, r] = 1.0
    return g.reshape(128, n * 128).astype(mybir.dt.np(BF16))


class Region:

    def __init__(self, tile, size):
        self.tile, self.size, self.at = tile, size, 0

    def restart(self, at=0):
        self.at = at

    def take(self, dims, dtype, rows=128):
        width = 4 if dtype == F32 else 2
        n = int(np.prod(dims)) * width
        n = (n + 3) // 4 * 4
        assert self.at + n <= self.size, (self.at, n, self.size)
        ap = self.tile[0:rows, self.at // 4:(self.at + n) // 4]
        self.at += (n + 31) // 32 * 32
        if dtype != F32:
            ap = ap.bitcast(dtype)
        if len(dims) > 1:
            names = "abcdef"[:len(dims)]
            ap = ap.rearrange(f"p ({' '.join(names)}) -> p {' '.join(names)}",
                              **{x: d for x, d in zip(names[1:], dims[1:])})
        return ap


def program(nc, A, out, B, upto=8):
    ctx = ExitStack()
    with ctx:
        body(nc, A, out, B, upto, ctx)


def body(nc, A, out, B, upto, ctx):
    def sb(name, shape, dt):
        return ctx.enter_context(nc.sbuf_tensor(name, shape, dt))

    def sem(name):
        return ctx.enter_context(nc.semaphore(name))

    shared = {}

    def phase_sem(kind, name):
        if (kind, name) not in shared:
            shared[kind, name] = sem(f"{kind}_{name}")
        return shared[kind, name]

    def clear(kind):
        def sync(sp):
            for (k, _), handle in shared.items():
                if k == kind:
                    sp.sem_clear(handle)
        return dict(sync=sync)

    NT = B * S

    X = sb("X", [128, B, D], F32)
    ctxT = sb("ctxT", [128, NT], F32)
    xnT = sb("xnT", [128, NT], F32)
    ident = sb("ident_f", [128, 128], F32)
    ident_b = sb("ident_b", [128, 128], BF16)
    stack_sel = sb("stack_sel", [128, 2, 2, 4, 128], FP16)
    max_rows = sb("max_rows", [128, 12, 128], BF16)
    causal = sb("causal", [128, 2, 128], BF16)
    rope = sb("rope", [128, 2, 128], F32)
    gates = sb("gates", [128, 12], F32)
    stats = sb("stats", [128, B, 6], F32)
    stats2 = sb("stats2", [128, B, 6], F32)
    ln_small = sb("ln_small", [128, 10, B], F32)
    minus_half = sb("minus_half", [128, B], F32)
    cols = sb("cols", [128, 4, 8], F32)
    bv_row = sb("bv_row", [128, 128], F32)
    gate_sel = sb("gate_sel", [128, 11 * 128], BF16)
    gateT = sb("gateT", [128, NT], BF16)
    b2_rows = sb("b2_rows", [128, 128], F32)
    b2_rest = sb("b2_rest", [128, 128], F32)
    b2_part = sb("b2_part", [128, 3, 128], BF16)
    br_row = sb("br_row", [128, 8], F32)
    W_att = Region(sb("W_att", [128, 4096], F32), 4096 * 4)
    W_ffn = Region(sb("W_ffn", [128, 8320], F32), 8320 * 4)
    STK = 12500
    stacks = Region(sb("stacks", [128, STK], F32), STK * 4)
    WRK = 9500
    work = Region(sb("work", [128, WRK], F32), WRK * 4)
    PS = [ctx.enter_context(nc.psum_tensor(f"bank{i}", [128, 512], F32)) for i in range(8)]

    phase_done = sem("phase_done")
    meets = {}

    def meet(eng):
        n = meets[id(eng)] = meets.get(id(eng), 0) + 1
        eng.drain().then_inc(phase_done, 1)
        eng.wait_ge(phase_done, 5 * n)

    load_x = sem("load_x")
    load_c = sem("load_c")
    load_const = sem("load_const")

    setup_ready = sem("setup_ready")
    ctx_turned = sem("ctx_turned")
    ctx_stored = sem("ctx_stored")
    stats_sem = sem("stats_sem")
    work.restart()
    ctx_in = stacks.tile[:, 0:B * D]

    def setup_sync(sp):
        sp.dma_start(ctx_in.rearrange("p (b d) -> p b d", d=D), A["ctx"].rearrange("b t d -> t b d")).then_inc(load_c, 16)
        sp.dma_start(X[:], A["x"].rearrange("b t d -> t b d")).then_inc(load_x, 16)
        for dst, name in ((ident[:], "ident"), (rope[:].rearrange("p a t -> p (a t)"), "rope"),
                          (stack_sel[:].rearrange("p a b c t -> p (a b c t)"), "stack_sel"),
                          (const_f[:, 0:1536], "max_rows"), (const_f[:, 1536:1792], "causal")):
            sp.dma_start(dst, A[name]).then_inc(load_const, 16)
        for i, name in enumerate(("g_xattn", "g_ffn", "L2_gate")):
            n = A[name].shape[0]
            sp.dma_start(gates_in[:, 4 * i:4 * i + n], bcast_rows(A[name], 128)).then_inc(load_const, 16)

    const_f = work.take([1792], F32)
    gates_in = work.take([12], F32)
    N_CONST = 8 * 16

    def setup_vector(dve):
        dve.memset(minus_half[:], -0.5).then_inc(setup_ready, 1)
        dve.memset(gates_in[:, 9:12], 0.0).then_inc(setup_ready, 1)
        dve.memset(gateT[:], 0.0)
        dve.wait_ge(load_const, N_CONST)
        dve.tensor_copy(ident_b[:], ident[:]).then_inc(setup_ready, 1)
        dve.tensor_copy(max_rows[:].rearrange("p a t -> p (a t)"), const_f[:, 0:1536]).then_inc(setup_ready, 1)
        dve.tensor_copy(causal[:].rearrange("p a t -> p (a t)"), const_f[:, 1536:1792]).then_inc(setup_ready, 1)
        dve.wait_ge(load_x, 16)
        for b in range(B):
            dve.bn_stats(stats[:, b, :], X[:, b, :])

    def setup_scalar(act):
        act.wait_ge(load_const, N_CONST)
        act.wait_ge(setup_ready, 2)
        act.activation(gates[:], gates_in, ACT.Tanh)
        for i in range(B // 4):
            act.wait_ge(ctx_turned, i + 1)
            act.copy(ctxT[:, 512 * i:512 * i + 512], PS[i % 4][:]).then_inc(ctx_stored, 1)

    def setup_tensor(pe):
        pe.wait_ge(load_c, 16)
        pe.wait_ge(load_const, N_CONST)
        for i in range(B // 4):
            wait(pe, ctx_stored, i - 3)
            for k in range(4):
                b = 4 * i + k
                last = pe.transpose(PS[i % 4][:, 128 * k:128 * k + 128], ctx_in[:, b * D:(b + 1) * D], ident[:])
            last.then_inc(ctx_turned, 1)

    ln_dve = sem("ln_dve")
    ln_pool = sem("ln_pool")
    ln_turned = sem("ln_turned")
    ln_stored = sem("ln_stored")
    NG4 = B // 4
    ln_uses = {"n": 0}
    STEPS = 6

    def layer_norm(second=None):
        use = ln_uses["n"]
        ln_uses["n"] += 1
        work.restart()
        xn = work.take([2, 4, D], F32)
        xn1 = stacks.tile[:, 0:B * D].rearrange("p (b d) -> p b d", d=D)
        src = xn1 if second == "second" else X[:]
        st = stats2 if second == "second" else stats
        keep = second == "first"
        base_v = use * (STEPS + NG4) + (NG4 * 0)
        t = [ln_small[:, i, :] for i in range(10)]
        gamma, beta = cols[:, 2, 4:5], cols[:, 2, 5:6]

        def vector(dve):
            m0, v0, m1, v1 = st[:, :, 1], st[:, :, 2], st[:, :, 4], st[:, :, 5]
            dve.tensor_tensor(t[0], m0, m1, ALU.subtract)
            dve.tensor_tensor(t[1], m0, m1, ALU.add)
            dve.tensor_tensor(t[2], v0, v1, ALU.add).then_inc(ln_dve, 1)
            dve.wait_ge(ln_dve, base_v + 1)
            dve.tensor_tensor(t[3], t[0], t[0], ALU.mult).then_inc(ln_dve, 1)
            dve.wait_ge(ln_dve, base_v + 2)
            dve.scalar_tensor_tensor(t[4], t[3], 32.0, t[2], ALU.mult, ALU.add).then_inc(ln_dve, 1)
            dve.wait_ge(ln_dve, base_v + 3)
            dve.tensor_scalar(t[5], t[4], 1.0 / D, LN_EPS, ALU.mult, ALU.add).then_inc(ln_dve, 1)
            dve.tensor_scalar(t[7], t[1], 0.5, None, ALU.mult).then_inc(ln_dve, 1)
            dve.wait_ge(ln_dve, base_v + 5)
            dve.wait_ge(ln_pool, use + 1)
            dve.tensor_copy(t[8], t[6]).then_inc(ln_dve, 1)
            dve.wait_ge(ln_dve, base_v + 6)

            def group(g, par):
                if not keep:
                    wait(dve, ln_turned, ln_turn_base + g - 1)
                for k in range(4):
                    b = g * 4 + k
                    dst = xn1[:, bass.ds(b, 1), :] if keep else xn[:, par, k:k + 1, :]
                    last = dve.tensor_scalar(dst, src[:, bass.ds(b, 1), :], t[7][:, bass.ds(b, 1)],
                                             t[8][:, bass.ds(b, 1)], ALU.subtract, ALU.mult)
                last.then_inc(ln_dve, 1)
                if keep:
                    dve.wait_ge(ln_dve, base_v + STEPS + g + 1)
                    for k in range(4):
                        b = g * 4 + k
                        dve.bn_stats(stats2[:, bass.ds(b, 1), :], xn1[:, bass.ds(b, 1), :])
            pairs(dve, group)

        def pool(pl):
            pl.wait_ge(ln_dve, base_v + 4)
            pl.tensor_tensor(t[6], t[5], minus_half[:], ALU.pow).then_inc(ln_pool, 1)

        turned_before = ln_uses.get("turned", 0)
        ln_turn_base = turned_before * NG4
        if not keep:
            ln_uses["turned"] = turned_before + 1

        def tensor(pe):
            if keep:
                return

            def group(g, par):
                pe.wait_ge(ln_dve, base_v + STEPS + g + 1)
                wait(pe, ln_stored, ln_turn_base + g - 1)
                for k in range(4):
                    last = pe.transpose(PS[par][:, 128 * k:128 * k + 128], xn[:, par, k, :], ident[:])
                last.then_inc(ln_turned, 1)
            pairs(pe, group)

        def scalar(act):
            if keep:
                return

            def group(g, par):
                act.wait_ge(ln_turned, ln_turn_base + g + 1)
                dst = xnT[:, bass.ds(g * 512, 512)]
                if second == "second":
                    act.activation(dst, PS[par][:], ACT.Identity, scale=gamma, bias=beta).then_inc(ln_stored, 1)
                else:
                    act.copy(dst, PS[par][:]).then_inc(ln_stored, 1)
            pairs(act, group)

        return dict(vector=vector, gpsimd=pool, tensor=tensor, scalar=scalar)

    def pairs(eng, group):
        group(0, 0)
        group(1, 1)
        if NG4 > 2:
            with eng.Fori(1, NG4 // 2) as r:
                group(2 * r, 0)
                group(2 * r + 1, 1)

    def attention(l):
        dh = HEAD_DIMS[l]
        wide = dh == 64
        GB = 2 if wide else 4
        T = GB * S
        NG = B // GB
        scale = float(dh) ** -0.5
        rotary, masked = l == 0, l == 0
        R = 64 if wide else ROW_TILE
        inner = H * dh
        nchunk = inner // 128

        W_att.restart()
        wq = W_att.take([inner], F32)
        wk = W_att.take([inner], F32)
        wv = W_att.take([inner], F32)
        wo = W_att.take([nchunk, D], F32)
        if rotary:
            wq_turn = W_att.take([D], F32)
            wk_turn = W_att.take([D], F32)
        stacks.restart()
        if wide:
            Q = [stacks.take([2, 8, T], FP16) for _ in range(2)]
            K = [stacks.take([2, 8, T], FP16) for _ in range(2)]
        else:
            Q = [stacks.take([4, T], FP16) for _ in range(2)]
            K = [stacks.take([4, T], FP16) for _ in range(2)]
        V = [stacks.take([GB, 2, H, dh + 1], FP16) for _ in range(2)]
        work.restart()
        P32 = work.take([4, 512], F32)
        Phi = work.take([4, 512], FP16)
        Plo = work.take([4, 512], FP16)
        o32 = work.take([2, inner], F32)
        y32 = work.take([T], F32)
        cst = work.take([GB, S], F32)
        m16 = work.take([2, 16], F32)
        mcat = work.take([128], BF16)
        mT = work.take([2, 128], BF16)
        rec = work.take([2, 16], F32)
        if wide:
            oT = [stacks_tail_take(T)]
        else:
            oT = [work.take([1, T], F32) for _ in range(2)]
            k32 = work.take([T], F32)
            q32 = work.take([T], F32)
            v32 = work.take([T], F32)
            khl = work.take([2, T], FP16)
            qhl = work.take([2, T], FP16)
            if rotary:
                turn1 = W_att.take([T], F32)
                turn2 = W_att.take([T], F32)

        names = ["s_ready", "max_done", "m_split", "m_chain", "mt_ready", "mt_stored", "st_ready", "exp_done",
                 "plo_dve", "plo_pool", "pv_done", "rec_done", "o_done", "ot_ready", "ot_stored", "yt_ready",
                 "y_stored", "yb_ready", "x_done", "ctx_staged", "ones_set"]
        if wide:
            names += ["proj_ready", "hi_done", "lo_done"]
        else:
            names += ["kp_ready", "qp_ready", "k32_done", "q32_done", "v_ready", "v32_done", "hi_k", "hi_q", "hi_v",
                      "lo_kq", "lo_v", "selk_ready", "selk_stored_a", "selk_stored_v",
                      "selq_ready", "selq_stored_a", "selq_stored_v", "turn_done"]
        s = {n: phase_sem("att", n) for n in names}
        w_loaded = att_loaded[l]
        w_count = att_loads(l)[1]

        def heads(quad):
            if wide:
                u, j = divmod(quad, 2)
                return [(2 * (4 * u + k) + j, 64 * j, 4 * u + k, 4 + 4 * u + k) for k in range(4)]
            return [(4 * quad + k, 32 * quad, k, k) for k in range(4)]

        def products(which, par, r0, block, tok):
            def at(buf, part):
                return buf[par][r0:r0 + R, part, block, tok] if wide else buf[par][r0:r0 + R, block, tok]
            pairs_ = ((0, 0), (0, 1), (1, 0)) if wide else ((0, 0),)
            return [((at(Q, a), at(K, b)) if which == "qk" else (at(K, b), at(Q, a))) for a, b in pairs_]

        if wide:
            slots = {(0, "A"): ["yb"], (0, "B"): [], (0, "C"): ["k0", "k1", "k2"],
                     (1, "A"): ["k3", "v0", "v1"], (1, "B"): ["v2", "v3", "q0"], (1, "C"): ["q1", "q2", "q3", "yt"]}
            YB = 3
        else:
            slots = {(0, "A"): ["kp"] + ["kp2"] * rotary, (0, "B"): ["qp"] + ["qp2"] * rotary, (0, "C"): ["v"],
                     (1, "A"): ["selk0"], (1, "B"): ["selk1"], (1, "C"): ["selk2"],
                     (2, "A"): ["selk3", "yt"], (2, "B"): ["selq0"], (2, "C"): ["selq1"],
                     (3, "A"): ["selq2", "yb"], (3, "B"): ["selq3"], (3, "C"): []}
            YB = 2
        order = []
        for k in range(GB):
            order += [f"mt{k}"] + slots[k, "A"] + slots[k, "B"] + [f"ot{k}_{i}" for i in range(nchunk // 4 or 1)] + slots[k, "C"]
        banks = {job: 6 + i % 2 for i, job in enumerate(order)}
        NOT = nchunk // 4 or 1

        def ok(index, n):
            return not isinstance(index, int) or 0 <= index < n

        def rounds(eng, iteration, before=lambda: None):
            lead = 4 if wide else 2
            for g in range(lead):
                iteration(g, g % 2)
            if NG > lead:
                before()
                with eng.Fori(lead // 2, NG // 2) as r:
                    iteration(2 * r, 0)
                    iteration(2 * r + 1, 1)
            for g in range(NG, NG + (4 if wide else 3)):
                iteration(g, g % 2)

        def tensor(pe):
            pe.wait_ge(w_loaded, w_count)
            freed_by = {}
            for job in order:
                if job.startswith("mt"):
                    k = int(job[2])
                    freed_by[job] = ("mt_stored", lambda g, k=k: (g - 1) * GB + k)
                elif job.startswith("ot"):
                    k, i = int(job[2]), int(job[4])
                    freed_by[job] = ("ot_stored", lambda g, k=k, i=i: ((g - 1) * GB + k - 2) * NOT + i + 1)
                elif job == "yt":
                    freed_by[job] = ("y_stored", lambda g: g - 1)
                elif job == "yb":
                    freed_by[job] = ("x_done", lambda g: g - YB + 1)
                elif wide:
                    n = ["k0", "k1", "k2", "k3", "v0", "v1", "v2", "v3", "q0", "q1", "q2", "q3"].index(job)
                    freed_by[job] = ("lo_done", lambda g, n=n: 12 * g + n + 1)
                elif job in ("kp", "kp2"):
                    freed_by[job] = ("k32_done", lambda g: g + 1)
                elif job in ("qp", "qp2"):
                    freed_by[job] = ("q32_done", lambda g: g + 1)
                elif job == "v":
                    freed_by[job] = ("v32_done", lambda g: g + 1)
                else:
                    c = int(job[4])
                    kind = "selk" if job[3] == "k" else "selq"
                    freed_by[job] = (f"{kind}_stored_{'av'[c % 2]}", lambda g, c=c: 2 * g + c // 2 + 1)
            last_in = {6: None, 7: None}

            def take(job, g):
                bank = banks[job]
                if last_in[bank] is not None:
                    name, count = last_in[bank]
                    wait(pe, s[name], count(g))
                last_in[bank] = freed_by[job]
                return PS[bank]

            def age():
                for b, v in last_in.items():
                    if v is not None:
                        name, count = v
                        last_in[b] = (name, lambda g, count=count: count(g - 1))

            def job_run(job, g, par):
                if job == "yt":
                    a = g - 2
                    if ok(a, NG):
                        ps = take(job, g)
                        pe.wait_ge(s["ot_stored"], (a + 1) * GB * NOT)
                        src = oT[0] if wide else oT[par]
                        for c in range(nchunk):
                            last = pe.matmul(ps[:, 0:T], wo[:, c, :], src[:, c, :], start=(c == 0), stop=(c == nchunk - 1))
                        last.then_inc(s["yt_ready"], 1)
                elif job == "yb":
                    a = g - YB
                    if ok(a, NG):
                        ps = take(job, g)
                        pe.wait_ge(s["y_stored"], a + 1)
                        for k in range(GB):
                            last = pe.transpose(ps[:, 128 * k:128 * k + 128], y32[:, 128 * k:128 * k + 128], ident[:])
                        last.then_inc(s["yb_ready"], 1)
                elif not ok(g, NG):
                    return
                elif wide:
                    ps = take(job, g)
                    i = int(job[1])
                    if job[0] == "v":
                        pe.wait_ge(s["ctx_staged"], g + 1)
                        last = pe.matmul(ps[:], cst[:, i // 2, :], wv[:, 512 * (i % 2):512 * (i % 2) + 512], start=True, stop=True)
                    else:
                        w, src = (wk, ctxT) if job[0] == "k" else (wq, xnT)
                        for j in range(2):
                            t = 2 * i + j
                            last = pe.matmul(ps[:, T * j:T * j + T], w[:, 128 * t:128 * t + 128], src[:, bass.ds(g * T, T)],
                                             start=True, stop=True)
                    last.then_inc(s["proj_ready"], 1)
                elif job in ("kp", "kp2", "qp", "qp2"):
                    ps = take(job, g)
                    w = {"kp": wk, "qp": wq}.get(job)
                    if w is None:
                        w = wk_turn if job == "kp2" else wq_turn
                    src = ctxT if job[0] == "k" else xnT
                    pe.matmul(ps[:], w, src[:, bass.ds(g * T, T)], start=True, stop=True).then_inc(s[f"{job[0]}p_ready"], 1)
                elif job == "v":
                    ps = take(job, g)
                    pe.wait_ge(s["ctx_staged"], g + 1)
                    for k in range(GB):
                        last = pe.matmul(ps[:, 128 * k:128 * k + 128], cst[:, k, :], wv, start=True, stop=True)
                    last.then_inc(s["v_ready"], 1)
                else:
                    ps = take(job, g)
                    c, kind = int(job[4]), job[3]
                    if c == 0:
                        pe.wait_ge(s[f"hi_{kind}"], g + 1)
                        pe.wait_ge(s["lo_kq"], 2 * g + (1 if kind == "k" else 2))
                    src, t = (khl, 1) if kind == "k" else (qhl, 0)
                    pe.matmul(ps[:], stack_sel[:, t, 0, c, :], src[:, 0, :], start=True, stop=False)
                    pe.matmul(ps[:], stack_sel[:, t, 1, c, :], src[:, 1, :], start=False, stop=True).then_inc(s[f"sel{kind}_ready"], 1)

            def scores(b, quad, par, tok):
                ps = PS[quad % 2]
                wait(pe, s["max_done"], 4 * b + quad - 1)
                if masked:
                    pe.matmul(ps[:].rearrange("p (h k) -> p h k", h=4), ident_b[:],
                              causal[:, 0:1, :].to_broadcast([128, 4, 128]), start=True, stop=False, skip_group_check=True)
                for k, (h, r0, block, _) in enumerate(heads(quad)):
                    pr = products("qk", par, r0, block, tok)
                    for i, (a, c) in enumerate(pr):
                        last = pe.matmul(ps[:, 128 * k:128 * k + 128], a, c, start=(i == 0 and not masked),
                                         stop=(i == len(pr) - 1), skip_group_check=True)
                last.then_inc(s["s_ready"], 1)

            def scoresT(b, quad, par, tok, bp):
                ps = PS[2 + quad % 2]
                wait(pe, s["exp_done"], 4 * b + quad - 1)
                if quad == 0:
                    pe.wait_ge(s["mt_stored"], b + 1)
                if masked:
                    pe.matmul(ps[:].rearrange("p (h k) -> p h k", h=4), ident_b[:],
                              causal[:, 1:2, :].to_broadcast([128, 4, 128]), start=True, stop=False, skip_group_check=True)
                for k, (h, r0, block, ones) in enumerate(heads(quad)):
                    dst = ps[:, 128 * k:128 * k + 128]
                    for i, (a, c) in enumerate(products("kq", par, r0, block, tok)):
                        pe.matmul(dst, a, c, start=(i == 0 and not masked), stop=False, skip_group_check=True)
                    last = pe.matmul(dst, max_rows[r0:r0 + R, ones, :], mT[r0:r0 + R, bp, :],
                                     start=False, stop=True, skip_group_check=True)
                last.then_inc(s["st_ready"], 1)

            def values(b, quad, par, kk, bp):
                pe.wait_ge(s["exp_done"], 4 * b + quad + 1)
                pe.wait_ge(s["plo_pool" if quad % 2 else "plo_dve"], 2 * b + quad // 2 + 1)
                if wide:
                    ps = PS[4 + quad % 2]
                    wait(pe, s["o_done"], 4 * b + quad - 1)
                else:
                    ps = PS[4 + bp]
                    if quad == 0:
                        wait(pe, s["o_done"], b - 1)
                for k, (h, _, _, _) in enumerate(heads(quad)):
                    n = (k if wide else 4 * quad + k) * (dh + 1)
                    dst = ps[:, n:n + dh + 1]
                    hi, lo = Phi[:, quad, 128 * k:128 * k + 128], Plo[:, quad, 128 * k:128 * k + 128]
                    pe.matmul(dst, hi, V[par][:, kk, 0, h, :], start=True, stop=False)
                    pe.matmul(dst, hi, V[par][:, kk, 1, h, :], start=False, stop=False)
                    last = pe.matmul(dst, lo, V[par][:, kk, 0, h, :], start=False, stop=True)
                last.then_inc(s["pv_done"], 1)

            def iteration(g, gp):
                if not (isinstance(g, int) and g == 0):
                    age()
                for k in range(GB):
                    b0 = GB * (g - 1) + k
                    b1, b2 = b0 - 1, b0 - 2
                    par0 = 1 - gp
                    par1 = par0 if k >= 1 else gp
                    k1, bp1, bp2 = (k - 1) % GB, (k - 1) % 2, k % 2
                    tok0, tok1 = slice(128 * k, 128 * k + 128), slice(128 * k1, 128 * k1 + 128)
                    A0, A1, A2 = ok(b0, B), ok(b1, B), ok(b2, B)
                    if A0 and k == 0:
                        if wide:
                            pe.wait_ge(s["lo_done"], 12 * g)
                            pe.wait_ge(s["ones_set"], 1)
                        else:
                            for n in ("selk_stored_a", "selk_stored_v", "selq_stored_a", "selq_stored_v"):
                                pe.wait_ge(s[n], 2 * g)
                            pe.wait_ge(s["ones_set"], 1)
                            pe.wait_ge(s["hi_v"], g)
                            pe.wait_ge(s["lo_v"], g)
                    if A0: scores(b0, 0, par0, tok0)
                    if A1:
                        ps = take(f"mt{k}", g)
                        pe.wait_ge(s["m_split"], b1 + 1)
                        pe.transpose(ps[:, 0:64].bitcast(BF16), mcat, ident_b[:]).then_inc(s["mt_ready"], 1)
                    if A0: scores(b0, 1, par0, tok0)
                    if A1: scoresT(b1, 0, par1, tok1, bp1)
                    for job in slots[k, "A"]: job_run(job, g, gp)
                    if A0: scores(b0, 2, par0, tok0)
                    if A1:
                        scoresT(b1, 1, par1, tok1, bp1)
                        values(b1, 0, par1, k1, bp1)
                    for job in slots[k, "B"]: job_run(job, g, gp)
                    if A0: scores(b0, 3, par0, tok0)
                    if A1:
                        scoresT(b1, 2, par1, tok1, bp1)
                        values(b1, 1, par1, k1, bp1)
                    if A2:
                        for i in range(NOT):
                            ps = take(f"ot{k}_{i}", g)
                            if i == 0:
                                pe.wait_ge(s["o_done"], (b2 + 1) * (4 if wide else 1))
                            for c in range(min(4, nchunk)):
                                src = o32[:, bp2, 128 * (4 * i + c):128 * (4 * i + c) + 128]
                                last = pe.transpose(ps[:, 128 * c:128 * c + 128], src, ident[:])
                            last.then_inc(s["ot_ready"], 1)
                    if A1:
                        scoresT(b1, 3, par1, tok1, bp1)
                        values(b1, 2, par1, k1, bp1)
                    for job in slots[k, "C"]: job_run(job, g, gp)
                    if A1: values(b1, 3, par1, k1, bp1)
            rounds(pe, iteration)

        def scalar(act):
            def exps(b, quad):
                ps = PS[2 + quad % 2]
                act.wait_ge(s["st_ready"], 4 * b + quad + 1)
                wait(act, s["pv_done"], 4 * b + quad - 3)
                wait(act, s["plo_pool" if quad % 2 else "plo_dve"], 2 * b + quad // 2 - 1)
                act.activation(Phi[:, quad, :], ps[:], ACT.Exp, scale=scale)
                act.activation(P32[:, quad, :], ps[:], ACT.Exp, scale=scale).then_inc(s["exp_done"], 1)

            def job_run(job, g, gp):
                ps = PS[banks[job]]
                if job == "yt":
                    a = g - 2
                    if ok(a, NG):
                        act.wait_ge(s["yt_ready"], a + 1)
                        wait(act, s["yb_ready"], a)
                        act.activation(y32, ps[:, 0:T], ACT.Identity, scale=cols[:, l, 6:7], bias=cols[:, l, 3:4]).then_inc(s["y_stored"], 1)
                elif job == "yb" or not ok(g, NG):
                    return
                elif wide:
                    n = ["k0", "k1", "k2", "k3", "v0", "v1", "v2", "v3", "q0", "q1", "q2", "q3"].index(job)
                    act.wait_ge(s["proj_ready"], 12 * g + n + 1)
                    if n == 0:
                        wait(act, s["st_ready"], 4 * GB * (g - 1))
                    if n == 4:
                        wait(act, s["pv_done"], 4 * GB * (g - 1))
                    hi_dst, _, src = wide_place(job, gp)
                    act.copy(hi_dst, src).then_inc(s["hi_done"], 1)
                elif job in ("kp", "qp") and not rotary:
                    kind = job[0]
                    dst, col = (k32, 1) if kind == "k" else (q32, 0)
                    act.wait_ge(s[f"{kind}p_ready"], g + 1)
                    wait(act, s["lo_kq"], 2 * (g - 1) + (1 if kind == "k" else 2))
                    act.activation(dst, ps[:], ACT.Identity, bias=cols[:, l, col:col + 1]).then_inc(s[f"{kind}32_done"], 1)
                elif job[:3] == "sel" and int(job[4]) % 2 == 0:
                    kind, c = job[3], int(job[4])
                    act.wait_ge(s[f"sel{kind}_ready"], 4 * g + c + 1)
                    if c == 0:
                        wait(act, s["st_ready"], 16 * (g - 1))
                    act.copy((K if kind == "k" else Q)[gp][:, c, :], ps[:]).then_inc(s[f"sel{kind}_stored_a"], 1)

            def iteration(g, gp):
                for k in range(GB):
                    b1, b2 = GB * (g - 1) + k - 1, GB * (g - 1) + k - 2
                    A1, A2 = ok(b1, B), ok(b2, B)
                    bp1 = (k - 1) % 2
                    if k == 0 and ok(g, NG):
                        wait(act, s["proj_ready"] if wide else s["v_ready"], 12 * (g - 1) + 8 if wide else g)
                        act.copy(cst.rearrange("p a b -> p (a b)"), ctxT[:, bass.ds(g * T, T)]).then_inc(s["ctx_staged"], 1)
                    if A1:
                        act.wait_ge(s["mt_ready"], b1 + 1)
                        wait(act, s["st_ready"], 4 * (b1 - 1))
                        act.copy(mT[:, bp1, :], PS[banks[f"mt{k}"]][:, 0:64].bitcast(BF16)).then_inc(s["mt_stored"], 1)
                        exps(b1, 0)
                    for job in slots[k, "A"]: job_run(job, g, gp)
                    if A1: exps(b1, 1)
                    for job in slots[k, "B"]: job_run(job, g, gp)
                    if A1: exps(b1, 2)
                    if A2:
                        gpo = (1 - gp) if k >= 2 else gp
                        for i in range(NOT):
                            act.wait_ge(s["ot_ready"], b2 * NOT + i + 1)
                            n = min(4, nchunk)
                            src = PS[banks[f"ot{k}_{i}"]][:, 0:128 * n].rearrange("p (c t) -> p c t", c=n)
                            k2 = (k - 2) % GB
                            if k2 == 0 and i == 0:
                                wait(act, s["yt_ready"], g - 2 if wide else g - 2)
                            dst = (oT[0] if wide else oT[gpo])[:, n * i:n * i + n, 128 * k2:128 * k2 + 128]
                            act.copy(dst, src).then_inc(s["ot_stored"], 1)
                    if A1: exps(b1, 3)
                    for job in slots[k, "C"]: job_run(job, g, gp)
                    if not wide and ok(g, NG):
                        if k == 0:
                            for kind, x32, hl in (("k", k32, khl), ("q", q32, qhl)):
                                act.wait_ge(s[f"{kind}32_done"], g + 1)
                                wait(act, s[f"sel{kind}_ready"], 4 * g)
                                wait(act, s["lo_kq"], 2 * (g - 1) + (1 if kind == "k" else 2))
                                act.copy(hl[:, 0, :], x32).then_inc(s[f"hi_{kind}"], 1)
                        if k == 1:
                            act.wait_ge(s["v32_done"], g + 1)
                            wait(act, s["pv_done"], 16 * (g - 1))
                            act.copy(V[gp][:, :, 0, :, 0:dh], v32.rearrange("p (b h d) -> p b h d", b=GB, h=H)).then_inc(s["hi_v"], 1)
            rounds(act, iteration)

        def wide_place(job, gp):
            ps, i = PS[banks[job]], int(job[1])
            if job[0] == "v":
                src = ps[:].rearrange("p (h d) -> p h d", d=dh)
                h0 = 8 * (i % 2)
                return V[gp][:, i // 2, 0, h0:h0 + 8, 0:dh], V[gp][:, i // 2, 1, h0:h0 + 8, 0:dh], src
            buf = (K if job[0] == "k" else Q)[gp]
            src = ps[:].rearrange("p (j t) -> p j t", j=2)
            return buf[:, 0, 2 * i:2 * i + 2, :], buf[:, 1, 2 * i:2 * i + 2, :], src

        def vector(dve):
            dve.memset(mcat, 0.0).then_inc(s["ones_set"], 1)
            for p in range(2):
                for part in range(2):
                    last = dve.memset(V[p][:, :, part, :, dh:dh + 1], 1.0 - part)
            last.then_inc(s["ones_set"], 1)
            dve.wait_ge(s["ones_set"], 2)
            if wide:
                mview = mcat.rearrange("p (j k) -> p j k", j=2)
            else:
                mview = mcat.rearrange("p (j k) -> p j k", j=4)

            def row_max(b, quad, bp):
                dve.wait_ge(s["s_ready"], 4 * b + quad + 1)
                if quad == 0:
                    wait(dve, s["m_split"], b - 1)
                at = 8 * (quad % 2) + 4 * (quad // 2) if wide else 4 * quad
                dve.tensor_reduce(m16[:, bp, at:at + 4], PS[quad % 2][:].rearrange("p (h k) -> p h k", h=4),
                                  AX, ALU.max).then_inc(s["max_done"], 1)

            def split_max(b, bp):
                dve.wait_ge(s["max_done"], 4 * b + 4)
                wait(dve, s["mt_ready"], b)
                if wide:
                    src = m16[:, bp, :].rearrange("p (j k) -> p j k", j=2)
                    hi, lo = mview[:, :, 0:8], mview[:, :, 8:16]
                else:
                    src = m16[:, bp, :].rearrange("p (j k) -> p j k", j=4)
                    hi, lo = mview[:, :, 0:4], mview[:, :, 4:8]
                dve.tensor_scalar(hi, src, -1.0, None, ALU.mult).then_inc(s["m_chain"], 1)
                dve.wait_ge(s["m_chain"], b + 1)
                dve.scalar_tensor_tensor(lo, src, -1.0, hi, ALU.mult, ALU.subtract).then_inc(s["m_split"], 1)

            def normalise(b, units, bp, ob):
                for q in units:
                    n = 4 if wide else 16
                    cnt = (4 * b + q) if wide else b
                    ps = PS[4 + (q % 2 if wide else bp)][:, 0:n * (dh + 1)].rearrange("p (h d) -> p h d", h=n)
                    dve.wait_ge(s["pv_done"], 4 * b + q + 1)
                    rb = q % 2 if wide else bp
                    wait(dve, s["o_done"], cnt - 1)
                    dve.reciprocal(rec[:, rb, 0:n], ps[:, :, dh]).then_inc(s["rec_done"], 1)
                    dve.wait_ge(s["rec_done"], cnt + 1)
                    if wide:
                        if q == 0:
                            wait(dve, s["ot_ready"], 2 * (b - 1))
                        u, j = divmod(q, 2)
                        dst = o32[:, ob, :].rearrange("p (t j d) -> p t j d", j=2, d=dh)[:, 4 * u:4 * u + 4, j, :]
                    else:
                        wait(dve, s["ot_ready"], b - 1)
                        dst = o32[:, ob, :].rearrange("p (h d) -> p h d", h=16)
                    dve.tensor_tensor(dst, ps[:, :, 0:dh], rec[:, rb, 0:n].unsqueeze(2).to_broadcast([128, n, dh]),
                                      ALU.mult).then_inc(s["o_done"], 1)

            def low_half(b, quad):
                dve.wait_ge(s["exp_done"], 4 * b + quad + 1)
                wait(dve, s["pv_done"], 4 * b + quad - 3)
                dve.tensor_tensor(Plo[:, quad, :], P32[:, quad, :], Phi[:, quad, :], ALU.subtract).then_inc(s["plo_dve"], 1)

            def job_run(job, g, gp):
                ps = PS[banks[job]]
                if job == "yt":
                    return
                if job == "yb":
                    a = g - YB
                    if ok(a, NG):
                        dve.wait_ge(s["yb_ready"], a + 1)
                        xs = X[:, bass.ds(a * GB, GB), :]
                        dve.tensor_tensor(xs, xs, ps[:, 0:T].rearrange("p (b d) -> p b d", b=GB), ALU.add).then_inc(s["x_done"], 1)
                        dve.wait_ge(s["x_done"], a + 1)
                        for k in range(GB):
                            dve.bn_stats(stats[:, bass.ds(a * GB + k, 1), :], X[:, bass.ds(a * GB + k, 1), :])
                elif not ok(g, NG):
                    return
                elif wide:
                    n = ["k0", "k1", "k2", "k3", "v0", "v1", "v2", "v3", "q0", "q1", "q2", "q3"].index(job)
                    dve.wait_ge(s["hi_done"], 12 * g + n + 1)
                    hi, lo, src = wide_place(job, gp)
                    dve.tensor_tensor(lo, src, hi, ALU.subtract).then_inc(s["lo_done"], 1)
                elif job in ("kp2", "qp2"):
                    kind = job[0]
                    first = PS[banks[kind + "p"]][:].rearrange("p (b t) -> p b t", b=GB)
                    second = ps[:].rearrange("p (b t) -> p b t", b=GB)
                    dst = k32 if kind == "k" else q32
                    i = 0 if kind == "k" else 1
                    dve.wait_ge(s[f"{kind}p_ready"], 2 * g + 2)
                    wait(dve, s["turn_done"], 4 * g + 2 * i - 1 + 1)
                    dve.tensor_tensor(turn1.rearrange("p (b t) -> p b t", b=GB), first,
                                      rope[:, 0:1, :].to_broadcast([128, GB, 128]), ALU.mult).then_inc(s["turn_done"], 1)
                    dve.tensor_tensor(turn2.rearrange("p (b t) -> p b t", b=GB), second,
                                      rope[:, 1:2, :].to_broadcast([128, GB, 128]), ALU.mult).then_inc(s["turn_done"], 1)
                    dve.wait_ge(s["turn_done"], 4 * g + 2 * i + 2)
                    wait(dve, s["lo_kq"], 2 * (g - 1) + i + 1)
                    wait(dve, s[f"hi_{kind}"], g)
                    dve.tensor_tensor(dst, turn1, turn2, ALU.add).then_inc(s[f"{kind}32_done"], 1)
                    dve.wait_ge(s[f"{kind}32_done"], g + 1)
                elif job == "v":
                    dve.wait_ge(s["v_ready"], g + 1)
                    wait(dve, s["lo_v"], g)
                    dve.tensor_tensor(v32.rearrange("p (b d) -> p b d", b=GB), ps[:].rearrange("p (b d) -> p b d", b=GB),
                                      bv_row[:].unsqueeze(1).to_broadcast([128, GB, 128]), ALU.add).then_inc(s["v32_done"], 1)
                elif job[:3] == "sel" and int(job[4]) % 2 == 1:
                    kind, c = job[3], int(job[4])
                    dve.wait_ge(s[f"sel{kind}_ready"], 4 * g + c + 1)
                    if c == 1:
                        wait(dve, s["st_ready"], 16 * (g - 1))
                    dve.tensor_copy((K if kind == "k" else Q)[gp][:, c, :], ps[:]).then_inc(s[f"sel{kind}_stored_v"], 1)

            def iteration(g, gp):
                for k in range(GB):
                    b0 = GB * (g - 1) + k
                    b1, b2 = b0 - 1, b0 - 2
                    A0, A1, A2 = ok(b0, B), ok(b1, B), ok(b2, B)
                    bp0, bp1, bp2 = k % 2, (k - 1) % 2, k % 2
                    if A1: split_max(b1, bp1)
                    if A2: normalise(b2, (2, 3) if wide else (3,), bp2, bp2)
                    if A0:
                        row_max(b0, 0, bp0)
                        row_max(b0, 1, bp0)
                    for job in slots[k, "A"]: job_run(job, g, gp)
                    if A1: low_half(b1, 0)
                    if A0: row_max(b0, 2, bp0)
                    if A1 and wide: normalise(b1, (0,), bp1, bp1)
                    for job in slots[k, "B"]: job_run(job, g, gp)
                    if A0: row_max(b0, 3, bp0)
                    if A1: low_half(b1, 2)
                    if A1 and wide: normalise(b1, (1,), bp1, bp1)
                    for job in slots[k, "C"]: job_run(job, g, gp)
            rounds(dve, iteration)

        def gpsimd(pool):
            def low_half(b, quad):
                pool.wait_ge(s["exp_done"], 4 * b + quad + 1)
                wait(pool, s["pv_done"], 4 * b + quad - 3)
                pool.tensor_tensor(Plo[:, quad, :], P32[:, quad, :], Phi[:, quad, :], ALU.subtract).then_inc(s["plo_pool"], 1)

            def iteration(g, gp):
                for k in range(GB):
                    b1 = GB * (g - 1) + k - 1
                    if ok(b1, B):
                        low_half(b1, 1)
                        low_half(b1, 3)
                    if not wide and ok(g, NG):
                        if k == 0:
                            for i, (kind, x32, hl) in enumerate((("k", k32, khl), ("q", q32, qhl))):
                                pool.wait_ge(s[f"hi_{kind}"], g + 1)
                                wait(pool, s[f"sel{kind}_ready"], 4 * g)
                                pool.tensor_tensor(hl[:, 1, :], x32, hl[:, 0, :], ALU.subtract).then_inc(s["lo_kq"], 1)
                        if k == 1:
                            pool.wait_ge(s["hi_v"], g + 1)
                            vsrc = v32.rearrange("p (b h d) -> p b h d", b=GB, h=H)
                            for b in range(GB):
                                last = pool.tensor_tensor(V[gp][:, b, 1, :, 0:dh], vsrc[:, b], V[gp][:, b, 0, :, 0:dh], ALU.subtract)
                            last.then_inc(s["lo_v"], 1)
            rounds(pool, iteration)

        return dict(tensor=tensor, scalar=scalar, vector=vector, gpsimd=gpsimd)

    def stacks_tail_take(T):
        W_ffn.restart(W_ffn.size - 8 * T * 4)
        return W_ffn.take([8, T], F32)

    ffn_loaded = [sem(f"ffn_loaded{l}") for l in range(4)]
    EXPERTS = {0: 8, 1: 16, 3: 8}
    TOP = {0: 2, 1: 4, 3: 1}
    TILES = {0: 11, 1: 9, 3: 32}

    def ffn_weights(l):
        W_ffn.restart()
        if l == 2:
            w = {n: W_ffn.take([D], F32) for n in ("wr", "wk", "wv")}
            w["mu"] = W_ffn.take([4], F32)
            loads = [(w[n], A[f"F2_{n}"]) for n in ("wr", "wk", "wv")] + [(w["mu"][:, 0:2], A["F2_mu"])]
            return w, loads
        n, E = TILES[l], EXPERTS[l]
        w = {"up": W_ffn.take([n * 128], F32), "down": W_ffn.take([n * 128], F32), "router": W_ffn.take([E], F32)}
        if l == 0:
            w["up2"] = W_ffn.take([n * 128], F32)
        loads = [(w[k], A[f"F{l}_{k}"]) for k in w]
        ngate = A[f"gate_sel{l}"].shape[1]
        loads.append((gate_sel[:, 0:ngate], A[f"gate_sel{l}"]))
        if l == 3:
            w["b1"] = W_ffn.take([n], F32)
            loads.append((w["b1"], A["F3_b1"]))
            loads.append((b2_rows[:], A["F3_b2"]))
            loads.append((br_row[:], bcast_rows(A["F3_br"], 128)))
        return w, loads

    def ffn_load_phase(l):
        def sync(sp):
            for dst, src in ffn_weights(l)[1]:
                sp.dma_start(dst, src).then_inc(ffn_loaded[l], 16)
        return dict(sync=sync)

    def router(l):
        E, top = EXPERTS[l], TOP[l]
        w, loads = ffn_weights(l)
        work.restart()
        logits = work.take([B, E], F32)
        e = work.take([B, E], F32)
        rest = work.take([B, E], F32)
        gate = work.take([B, E], F32)
        part = work.take([B, 3, E], BF16)
        best = work.take([B, 8], F32)
        red = work.take([3, B], F32)
        logit_ready, exp_ready, step, part_ready, turned, turned_out = (
            phase_sem("router", n) for n in ("logit_ready", "exp_ready", "step", "part_ready", "turned", "turned_out"))

        def tensor(pe):
            pe.wait_ge(ffn_loaded[l], 16 * len(loads))
            for b in range(B):
                last = pe.matmul(PS[0][:, E * b:E * b + E], xnT[:, 128 * b:128 * b + 128], w["router"], start=True, stop=True)
            last.then_inc(logit_ready, 1)
            pe.wait_ge(part_ready, 1)
            for i in range(NG4):
                wait(pe, turned_out, i - 1)
                for k in range(4):
                    b = 4 * i + k
                    last = pe.transpose(PS[1 + i % 2][:].bitcast(BF16)[0:3 * E, 128 * k:128 * k + 128],
                                        part[:, b, :, :].rearrange("p a e -> p (a e)"), ident_b[:])
                last.then_inc(turned, 1)

        def scalar(act):
            act.wait_ge(step, 3)
            act.activation(e, logits, ACT.Exp).then_inc(exp_ready, 1)
            for i in range(NG4):
                act.wait_ge(turned, i + 1)
                act.copy(gateT[0:3 * E, 512 * i:512 * i + 512], PS[1 + i % 2][:].bitcast(BF16)[0:3 * E, 0:512]).then_inc(turned_out, 1)

        def vector(dve):
            n = [0]

            def chain(ins):
                n[0] += 1
                ins.then_inc(step, 1)
                dve.wait_ge(step, n[0])
            dve.wait_ge(logit_ready, 1)
            ps = PS[0][:, 0:B * E].rearrange("p (b e) -> p b e", e=E)
            if l == 3:
                chain(dve.tensor_tensor(logits, ps, br_row[:].unsqueeze(1).to_broadcast([128, B, E]), ALU.add))
            else:
                chain(dve.tensor_copy(logits, ps))
            chain(dve.tensor_reduce(red[:, 0, :], logits, AX, ALU.max))
            chain(dve.tensor_tensor(logits, logits, red[:, 0, :].unsqueeze(2).to_broadcast([128, B, E]), ALU.subtract))
            dve.wait_ge(exp_ready, 1)
            dve.tensor_reduce(red[:, 1, :], e, AX, ALU.add)
            for b in range(B):
                last = dve.max(best[:, b, :], e[:, b, :])
            chain(last)
            dve.reciprocal(red[:, 2, :], red[:, 1, :])
            chain(dve.memset(best[:, :, top:8], -1.0))
            for b in range(B):
                last = dve.match_replace(rest[:, b, :], best[:, b, :], e[:, b, :], -1.0)
            chain(last)
            chain(dve.scalar_tensor_tensor(gate, rest, 0.0, e, ALU.is_lt, ALU.mult))
            chain(dve.tensor_tensor(gate, gate, red[:, 2, :].unsqueeze(2).to_broadcast([128, B, E]), ALU.mult))
            chain(dve.tensor_copy(part[:, :, 0, :], gate))
            chain(dve.tensor_tensor(gate, gate, part[:, :, 0, :], ALU.subtract))
            chain(dve.tensor_copy(part[:, :, 1, :], gate))
            chain(dve.tensor_tensor(gate, gate, part[:, :, 1, :], ALU.subtract))
            dve.tensor_copy(part[:, :, 2, :], gate).then_inc(part_ready, 1)
            if l == 3:
                chain(dve.tensor_copy(b2_part[:, 0, :], b2_rows[:]))
                chain(dve.tensor_tensor(b2_rest[:], b2_rows[:], b2_part[:, 0, :], ALU.subtract))
                chain(dve.tensor_copy(b2_part[:, 1, :], b2_rest[:]))
                chain(dve.tensor_tensor(b2_rest[:], b2_rest[:], b2_part[:, 1, :], ALU.subtract))
                chain(dve.tensor_copy(b2_part[:, 2, :], b2_rest[:]))

        return dict(tensor=tensor, scalar=scalar, vector=vector)

    def experts(l):
        n, E = TILES[l], EXPERTS[l]
        w, loads = ffn_weights(l)
        func = ACT.Silu if l == 0 else ACT.Gelu
        work.restart()
        act_out = work.take([2, 512], F32)
        prod = work.take([2, 512], F32)
        hid = work.take([2, 512], F32)
        y32 = work.take([512], F32)
        up_ready, act_done, prod_done, hid_done, down_done, y_ready, y_stored, yb_ready, x_done = (
            phase_sem("experts", k) for k in ("up_ready", "act_done", "prod_done", "hid_done", "down_done", "y_ready",
                                       "y_stored", "yb_ready", "x_done"))

        def before(t):
            return 2 if t >= 2 or n % 2 == 0 else (1, 3)[t]

        def gate_of(t):
            return {0: t, 1: t - 1 if t else None, 3: t // 4}[l]

        def gate_bank(t):
            return PS[4 + ((t // 4) % 2 if l == 3 else t % 2)]

        def ok(g):
            return not isinstance(g, int) or 0 <= g < NG4

        def rounds(eng, group):
            group(0)
            if NG4 > 1:
                with eng.Fori(1, NG4) as g:
                    group(g)
            group(NG4)

        def tensor(pe):
            def down(g, t):
                N = g * n + t
                pe.wait_ge(hid_done, N + 1)
                if t == 0:
                    wait(pe, y_stored, g)
                    if l == 3:
                        for p in range(3):
                            pe.matmul(PS[6][:], b2_part[:, p, :], gateT[:, bass.ds(g * 512, 512)], start=(p == 0), stop=False)
                last = pe.matmul(PS[6][:], w["down"][:, 128 * t:128 * t + 128], hid[:, t % 2, :],
                                 start=(t == 0 and l != 3), stop=(t == n - 1))
                last.then_inc(down_done, 1)

            def group(g):
                if ok(g):
                    tok = bass.ds(g * 512, 512)
                for t in range(n):
                    if ok(g):
                        N = g * n + t
                        gt = gate_of(t)
                        if gt is not None and (l != 3 or t % 4 == 0):
                            wait(pe, hid_done, N - 4 if l == 3 else N - before(t) + 1)
                            pe.matmul(gate_bank(t)[:], gate_sel[:, 128 * gt:128 * gt + 128], gateT[:, tok], start=True, stop=True)
                        wait(pe, act_done, N - before(t) + 1)
                        if l == 0:
                            wait(pe, prod_done, N - before(t) + 1)
                            pe.matmul(PS[2 + t % 2][:], w["up2"][:, 128 * t:128 * t + 128], xnT[:, tok], start=True, stop=True)
                        pe.matmul(PS[t % 2][:], w["up"][:, 128 * t:128 * t + 128], xnT[:, tok], start=True, stop=True).then_inc(up_ready, 1)
                        if t:
                            down(g, t - 1)
                    if t == 0 and ok(g - 1):
                        down(g - 1, n - 1)
                    if t == 4 and ok(g - 1):
                        pe.wait_ge(y_stored, g)
                        wait(pe, x_done, g - 1)
                        for k in range(4):
                            last = pe.transpose(PS[7][:, 128 * k:128 * k + 128], y32[:, 128 * k:128 * k + 128], ident[:])
                        last.then_inc(yb_ready, 1)
            rounds(pe, group)

        def scalar(act):
            def group(g):
                for t in range(n):
                    if ok(g):
                        N = g * n + t
                        act.wait_ge(up_ready, N + 1)
                        wait(act, prod_done if l == 0 else hid_done, N - before(t) + 1)
                        act.activation(act_out[:, t % 2, :], PS[t % 2][:], func,
                                       **(dict(bias=w["b1"][:, t:t + 1]) if l == 3 else {})).then_inc(act_done, 1)
                    if t == 0 and ok(g - 1):
                        act.wait_ge(down_done, g * n)
                        wait(act, yb_ready, g - 1)
                        act.activation(y32, PS[6][:], ACT.Copy, scale=gates[:, 4 + l:5 + l]).then_inc(y_stored, 1)
            rounds(act, group)

        def vector(dve):
            def group(g):
                for t in range(n):
                    if ok(g):
                        N = g * n + t
                        dve.wait_ge(act_done, N + 1)
                        src = act_out[:, t % 2, :]
                        if l == 0:
                            wait(dve, hid_done, N - before(t) + 1)
                            dve.tensor_tensor(prod[:, t % 2, :], src, PS[2 + t % 2][:], ALU.mult).then_inc(prod_done, 1)
                            dve.wait_ge(prod_done, N + 1)
                            src = prod[:, t % 2, :]
                        wait(dve, down_done, N - before(t) + 1)
                        if gate_of(t) is None:
                            last = dve.tensor_copy(hid[:, t % 2, :], src)
                        else:
                            last = dve.tensor_tensor(hid[:, t % 2, :], src, gate_bank(t)[:], ALU.mult)
                        last.then_inc(hid_done, 1)
                    if t == 5 and ok(g - 1):
                        dve.wait_ge(yb_ready, g)
                        xs = X[:, bass.ds((g - 1) * 4, 4), :]
                        dve.tensor_tensor(xs, xs, PS[7][:].rearrange("p (b d) -> p b d", b=4), ALU.add).then_inc(x_done, 1)
                        dve.wait_ge(x_done, g)
                        for k in range(4):
                            dve.bn_stats(stats[:, bass.ds((g - 1) * 4 + k, 1), :], X[:, bass.ds((g - 1) * 4 + k, 1), :])
            rounds(dve, group)

        return dict(tensor=tensor, scalar=scalar, vector=vector)

    def token_mix():
        w, loads = ffn_weights(2)
        work.restart()
        faded = work.take([2, 512], F32)
        mixed = work.take([2, 2, 512], F32)
        r_gate = work.take([2, 512], F32)
        relu = work.take([512], F32)
        squared = work.take([2, 512], F32)
        y32 = work.take([2, 512], F32)
        mu, rest = w["mu"][:, 0:2], w["mu"][:, 2:4]
        mu_ready, faded_done, mixed_done, rk_ready, r_done, relu_done, sq_done, v_ready, y_done, yb_ready, x_done = (
            sem(f"T_{k}") for k in ("mu_ready", "faded_done", "mixed_done", "rk_ready", "r_done", "relu_done",
                                    "sq_done", "v_ready", "y_done", "yb_ready", "x_done"))

        def ok(g):
            return not isinstance(g, int) or 0 <= g < NG4

        def rounds(eng, step):
            for g in range(4):
                step(g, g % 2)
            if NG4 > 4:
                with eng.Fori(2, NG4 // 2) as r:
                    step(2 * r, 0)
                    step(2 * r + 1, 1)
            step(NG4, 0)
            step(NG4 + 1, 1)

        def tensor(pe):
            pe.wait_ge(ffn_loaded[2], 16 * len(loads))

            def step(g, p):
                if ok(g):
                    pe.wait_ge(mixed_done, g + 1)
                    wait(pe, r_done, g - 1)
                    wait(pe, relu_done, g - 1)
                    pe.matmul(PS[p][:], w["wr"], mixed[:, p, 0, :], start=True, stop=True)
                    pe.matmul(PS[2 + p][:], w["wk"], mixed[:, p, 1, :], start=True, stop=True).then_inc(rk_ready, 1)
                if ok(g - 1):
                    pe.wait_ge(sq_done, g)
                    wait(pe, y_done, g - 2)
                    pe.matmul(PS[5 - p][:], w["wv"], squared[:, 1 - p, :], start=True, stop=True).then_inc(v_ready, 1)
                if ok(g - 2):
                    pe.wait_ge(y_done, g - 1)
                    wait(pe, x_done, g - 3)
                    for k in range(4):
                        last = pe.transpose(PS[6 + p][:, 128 * k:128 * k + 128], y32[:, p, 128 * k:128 * k + 128], ident[:])
                    last.then_inc(yb_ready, 1)
            rounds(pe, step)

        def scalar(act):
            def step(g, p):
                if ok(g):
                    act.wait_ge(rk_ready, g + 1)
                    wait(act, y_done, g - 1)
                    act.activation(r_gate[:, p, :], PS[p][:], ACT.Sigmoid).then_inc(r_done, 1)
            rounds(act, step)

        def vector(dve):
            dve.wait_ge(ffn_loaded[2], 16 * len(loads))
            dve.tensor_scalar(rest, mu, -1.0, 1.0, ALU.mult, ALU.add).then_inc(mu_ready, 1)
            dve.wait_ge(mu_ready, 1)

            def step(g, p):
                if ok(g):
                    x = xnT[:, bass.ds(g * 512, 512)]
                    xs = x.rearrange("p (b t) -> p b t", b=4)
                    wait(dve, mixed_done, g)
                    for i in range(2):
                        last = dve.tensor_scalar(faded[:, i, :], x, rest[:, i:i + 1], None, ALU.mult)
                    last.then_inc(faded_done, 1)
                    dve.wait_ge(faded_done, g + 1)
                    wait(dve, rk_ready, g - 1)
                    for i in range(2):
                        m = mixed[:, p, i, :].rearrange("p (b t) -> p b t", b=4)
                        f = faded[:, i, :].rearrange("p (b t) -> p b t", b=4)
                        dve.tensor_scalar(m[:, :, 0:1], xs[:, :, 0:1], mu[:, i:i + 1], None, ALU.mult)
                        last = dve.scalar_tensor_tensor(m[:, :, 1:128], xs[:, :, 1:128], mu[:, i:i + 1], f[:, :, 0:127], ALU.mult, ALU.add)
                    last.then_inc(mixed_done, 1)
                if ok(g - 1):
                    q = 1 - p
                    dve.wait_ge(rk_ready, g)
                    wait(dve, sq_done, g - 1)
                    dve.tensor_scalar(relu, PS[2 + q][:], 0.0, None, ALU.max).then_inc(relu_done, 1)
                    dve.wait_ge(relu_done, g)
                    wait(dve, v_ready, g - 2)
                    dve.tensor_tensor(squared[:, q, :], relu, relu, ALU.mult).then_inc(sq_done, 1)
                    dve.wait_ge(v_ready, g)
                    dve.wait_ge(r_done, g)
                    wait(dve, yb_ready, g - 2)
                    dve.scalar_tensor_tensor(y32[:, q, :], PS[5 - p][:], gates[:, 6:7], r_gate[:, q, :], ALU.mult, ALU.mult).then_inc(y_done, 1)
                if ok(g - 2):
                    dve.wait_ge(yb_ready, g - 1)
                    xs = X[:, bass.ds((g - 2) * 4, 4), :]
                    dve.tensor_tensor(xs, xs, PS[6 + p][:].rearrange("p (b d) -> p b d", b=4), ALU.add).then_inc(x_done, 1)
                    dve.wait_ge(x_done, g - 1)
                    for k in range(4):
                        dve.bn_stats(stats[:, bass.ds((g - 2) * 4 + k, 1), :], X[:, bass.ds((g - 2) * 4 + k, 1), :])
            rounds(dve, step)

        return dict(tensor=tensor, scalar=scalar, vector=vector)

    def feed_forward(l):
        return [token_mix()] if l == 2 else [router(l), experts(l)]

    att_loaded = [sem(f"att_loaded{l}") for l in range(4)]

    def att_loads(l):
        W_att.restart()
        inner = H * HEAD_DIMS[l]
        nchunk = inner // 128
        dst = {n: W_att.take([inner], F32) for n in ("wq", "wk", "wv")}
        dst["wo"] = W_att.take([nchunk * D], F32)
        loads = [(dst[n], A[f"L{l}_{n}"]) for n in ("wq", "wk", "wv", "wo")]
        if l == 0:
            loads += [(W_att.take([D], F32), A["L0_wq_turn"]), (W_att.take([D], F32), A["L0_wk_turn"])]
        loads.append((cols[:, l, 0:3], A[f"L{l}_cols"][:, 0:3]))
        if l == 2:
            loads.append((cols[:, l, 4:6], A["L2_cols"][:, 3:5]))
        else:
            loads.append((bv_row[:], bcast_rows(A[f"L{l}_bv"], 128)))
        return loads, 16 * len(loads)

    def att_scales(l):
        def vector(dve):
            dve.wait_ge(att_loaded[l], att_loads(l)[1])
            if l == 2:
                dve.tensor_tensor(cols[:, l, 6:7], gates[:, l:l + 1], gates[:, 8:9], ALU.mult).then_inc(scale_ready[l], 1)
            else:
                dve.tensor_copy(cols[:, l, 6:7], gates[:, l:l + 1]).then_inc(scale_ready[l], 1)
            dve.wait_ge(scale_ready[l], 1)
            dve.tensor_tensor(cols[:, l, 3:4], cols[:, l, 2:3], cols[:, l, 6:7], ALU.mult).then_inc(scale_ready[l], 1)
        return dict(vector=vector)

    scale_ready = [sem(f"scale_ready{l}") for l in range(4)]

    phases = [dict(tensor=setup_tensor, scalar=setup_scalar, vector=setup_vector, sync=setup_sync)]

    def att_load_phase(l):
        def sync(sp):
            for dst, src in att_loads(l)[0]:
                sp.dma_start(dst, src).then_inc(att_loaded[l], 16)
        return dict(sync=sync)

    plan, ran = [], []
    for l in range(4):
        plan += [("att", l), ("ffn", l)]
    phases[0] = merge(phases[0], att_load_phase(0) if isinstance(upto, int) or upto[0][0] == "att" else ffn_load_phase(upto[0][1]))
    for kind, l in (plan[:upto] if isinstance(upto, int) else upto):
        if kind == "att":
            first = merge(att_scales(l), ffn_load_phase(l))
            while ran:
                first = merge(first, clear(ran.pop()))
            phases.append(first)
            if l == 2:
                phases.append(layer_norm("first"))
                phases.append(layer_norm("second"))
            else:
                phases.append(layer_norm())
            phases.append(attention(l))
            ran.append("att")
        else:
            phases.append(merge(layer_norm(), clear(ran.pop())) if ran else layer_norm())
            phases += feed_forward(l)
            if l != 2:
                ran += ["router", "experts"]
            if l < 3 and (isinstance(upto, int) or ("att", l + 1) in upto):
                phases[-1] = merge(phases[-1], att_load_phase(l + 1))

    stored = sem("stored")

    def store(sp):
        sp.dma_start(out.rearrange("b t d -> t b d"), X[:]).then_inc(stored, 16)
        sp.wait_ge(stored, 16)

    block = ctx.enter_context(nc.Block())

    def run(eng, name):
        for ph in phases:
            if name in ph:
                ph[name](eng)
            meet(eng)

    @block.sync
    def _(sp):
        run(sp, "sync")
        store(sp)

    @block.tensor
    def _(pe):
        run(pe, "tensor")

    @block.scalar
    def _(act):
        run(act, "scalar")

    @block.vector
    def _(dve):
        run(dve, "vector")

    @block.gpsimd
    def _(pool):
        run(pool, "gpsimd")


def merge(a, b):
    out = dict(a)
    for k, f in b.items():
        out[k] = (lambda e, p=a[k], q=f: (p(e), q(e))) if k in a else f
    return out


def bcast_rows(v, n):
    return v.rearrange("(a n) -> a n", a=1).to_broadcast([n, v.shape[0]])


def arrays_of(inputs):
    a = {k: np.asarray(v) for k, v in inputs.items()}
    B = a["x"].shape[0]
    f = {"x": a["x"], "ctx": a["ctx_1024"], "g_xattn": a["g_xattn"], "g_ffn": a["g_ffn"], "L2_gate": a["L2_xattn_gate"]}
    z = np.zeros((128,), np.float32)

    def turned(w):
        return w.reshape(64, 2, 128)[:, ::-1, :].reshape(128, 128)
    for l in (0, 1, 3):
        if l == 3:
            w = a["L3_xattn_in_proj_weight"]
            bb = a["L3_xattn_in_proj_bias"]
            wq, wk, wv, wo = w[0:128], w[128:256], w[256:384], a["L3_xattn_out_w"]
            bq, bk, bv, bo = bb[0:128], bb[128:256], bb[256:384], a["L3_xattn_out_b"]
        else:
            wq, wk, wv, wo = (a[f"L{l}_xattn_W{n}"] for n in "qkvo")
            bq, bk, bv, bo = (a[f"L1_xattn_b{n}"] for n in "qkvo") if l == 1 else (z, z, z, z)
        f[f"L{l}_wq"], f[f"L{l}_wk"], f[f"L{l}_wv"], f[f"L{l}_wo"] = wq.T, wk.T, wv.T, wo.T
        if l == 0:
            f["L0_wq_turn"], f["L0_wk_turn"] = turned(wq).T, turned(wk).T
        f[f"L{l}_cols"] = np.stack([bq, bk, bo], 1)
        f[f"L{l}_bv"] = bv
    f["L2_wq"] = a["L2_xattn_w_q"]
    f["L2_wk"] = a["L2_xattn_w_kv"][:, 0:1024]
    f["L2_wv"] = a["L2_xattn_w_kv"][:, 1024:2048]
    f["L2_wo"] = a["L2_xattn_w_out"].reshape(8, 128, 128).transpose(1, 0, 2).reshape(128, 1024)
    f["L2_cols"] = np.stack([z, z, a["L2_xattn_b_out"], a["L2_xattn_ln_gamma"], a["L2_xattn_ln_beta"]], 1)
    f["F0_up"], f["F0_up2"] = (a[f"L0_ffn_{n}"].transpose(1, 0, 2).reshape(128, 1408) for n in ("w1", "w3"))
    f["F0_down"] = rows_by_tile(a["L0_ffn_w2"].reshape(1408, 128))
    f["F0_router"] = a["L0_ffn_w_router"].T
    up = np.concatenate([a["L1_ffn_shared_up"], a["L1_ffn_routed_up"]], 0)
    down = np.concatenate([a["L1_ffn_shared_down"], a["L1_ffn_routed_down"]], 0)
    f["F1_up"] = up.reshape(1152, 128).T
    f["F1_down"] = rows_by_tile(down.transpose(0, 2, 1).reshape(1152, 128))
    f["F1_router"] = a["L1_ffn_router_w"].T
    f["F2_wr"], f["F2_wk"], f["F2_wv"] = (a[f"L2_ffn_W_{n}"].T for n in "rkv")
    f["F2_mu"] = np.stack([a["L2_ffn_mu_r"], a["L2_ffn_mu_k"]], 1)
    f["F3_up"] = a["L3_ffn_W1"].transpose(1, 0, 2).reshape(128, 4096)
    f["F3_down"] = rows_by_tile(a["L3_ffn_W2"].reshape(4096, 128))
    f["F3_router"], f["F3_br"] = a["L3_ffn_Wr"], a["L3_ffn_br"]
    f["F3_b1"] = a["L3_ffn_b1"].reshape(32, 128).T
    f["F3_b2"] = np.concatenate([np.tile(a["L3_ffn_b2"], (3, 1)), np.zeros((104, 128), np.float32)], 0)
    f.update(shape_constants(B))
    return {k: np.ascontiguousarray(v) for k, v in f.items()}


def rows_by_tile(w):
    return w.reshape(-1, 128, 128).transpose(1, 0, 2).reshape(128, -1)


def kernel(**inputs):
    import concourse.bacc as _bacc
    from concourse.bass_utils import run_bass_kernel_spmd as _run

    nc = _bacc.Bacc("TRN2", target_bir_lowering=False, num_devices=1)
    arrays = {f"in_{k}": v for k, v in arrays_of(inputs).items()}
    A = {k[3:]: nc.dram_tensor(k, v.shape, mybir.dt.from_np(v.dtype), kind="ExternalInput").ap() for k, v in arrays.items()}
    B = inputs["x"].shape[0]
    out = nc.dram_tensor("out_x", (B, S, D), F32, kind="ExternalOutput").ap()
    program(nc, A, out, B)
    r = _run(nc, [arrays], core_ids=[0])
    return r.results[0]["out_x"]
```

```python
from contextlib import ExitStack

import numpy as np

import concourse.bass as bass
from concourse import mybir

F32, BF16, FP16 = mybir.dt.float32, mybir.dt.bfloat16, mybir.dt.float16
ALU = mybir.AluOpType
ACT = mybir.ActivationFunctionType
AX = mybir.AxisListType.X

S = 128
D = 128
H = 16
LN_EPS = 1e-5
MASKED = -1e30
HEAD_DIMS = (8, 8, 64, 8)
ROW_TILE = 32


def wait(eng, sem, count):
    if isinstance(count, int) and count <= 0:
        return
    eng.wait_ge(sem, count)


def shape_constants(B):
    c = {}
    c["ident"] = np.eye(128, dtype=np.float32)
    sel = np.zeros((128, 2, 2, 4, 128), np.float32)
    for t, order in enumerate(((0, 0, 1, 1), (0, 1, 0, 1))):
        for j in range(4):
            for cc in range(4):
                for r, part in enumerate(order):
                    for d in range(8):
                        sel[8 * (4 * j + cc) + d, t, part, cc, 32 * j + 8 * r + d] = 1.0
    c["stack_sel"] = sel.reshape(128, -1).astype(np.float16)
    rows = np.zeros((128, 16, 128), np.float32)
    for i in range(16):
        for r in (i, 16 + i, 64 + i, 80 + i):
            rows[r, i, :] = 1.0
    c["max_rows"] = rows.reshape(128, -1)
    q, k = np.meshgrid(np.arange(S), np.arange(S), indexing="ij")
    hidden = np.where(k > q, MASKED, 0.0).astype(np.float32)
    c["causal"] = np.concatenate([hidden, hidden.T], 1)
    freq = (1.0 / np.float32(10000.0) ** (np.arange(0, 8, 2, dtype=np.float32) / np.float32(8))).astype(np.float32)
    ang = np.arange(S, dtype=np.float32)[:, None] * freq[None, :]
    cos, sin = np.cos(ang).astype(np.float32), np.sin(ang).astype(np.float32)
    i = (np.arange(D) % 8) // 2
    sign = np.where(np.arange(D) % 2 == 0, -1.0, 1.0).astype(np.float32)
    c["rope"] = np.concatenate([cos[:, i].T, sin[:, i].T * sign[:, None]], 1)
    c["zero_cols"] = np.zeros((128, 4), np.float32)
    c["zero_row"] = np.zeros((1, 128), np.float32)
    c["gate_sel0"] = gate_rows(8, [[(e, r) for r in range(128) for e in [(128 * t + r) // 176]] for t in range(11)], 11)
    c["gate_sel1"] = gate_rows(16, [[(2 * t + r // 64, r) for r in range(128)] for t in range(8)], 8)
    c["gate_sel3"] = gate_rows(8, [[(e, r) for r in range(128)] for e in range(8)], 8)
    return c


def gate_rows(E, tiles, n):
    g = np.zeros((128, n, 128), np.float32)
    for t, pairs in enumerate(tiles):
        for e, r in pairs:
            for part in range(3):
                g[part * E + e, t, r] = 1.0
    return g.reshape(128, n * 128).astype(mybir.dt.np(BF16))


class Region:

    def __init__(self, tile, size):
        self.tile, self.size, self.at = tile, size, 0

    def restart(self, at=0):
        self.at = at

    def take(self, dims, dtype, rows=128):
        width = 4 if dtype == F32 else 2
        n = int(np.prod(dims)) * width
        n = (n + 3) // 4 * 4
        assert self.at + n <= self.size, (self.at, n, self.size)
        ap = self.tile[0:rows, self.at // 4:(self.at + n) // 4]
        self.at += (n + 31) // 32 * 32
        if dtype != F32:
            ap = ap.bitcast(dtype)
        if len(dims) > 1:
            names = "abcdef"[:len(dims)]
            ap = ap.rearrange(f"p ({' '.join(names)}) -> p {' '.join(names)}",
                              **{x: d for x, d in zip(names[1:], dims[1:])})
        return ap


def program(nc, A, out, B, upto=8):
    ctx = ExitStack()
    with ctx:
        body(nc, A, out, B, upto, ctx)


def body(nc, A, out, B, upto, ctx):
    def sb(name, shape, dt):
        return ctx.enter_context(nc.sbuf_tensor(name, shape, dt))

    def sem(name):
        return ctx.enter_context(nc.semaphore(name))

    shared = {}

    def phase_sem(kind, name):
        if (kind, name) not in shared:
            shared[kind, name] = sem(f"{kind}_{name}")
        return shared[kind, name]

    def clear(kind):
        def sync(sp):
            for (k, _), handle in shared.items():
                if k == kind:
                    sp.sem_clear(handle)
        return dict(sync=sync)

    NT = B * S

    X = sb("X", [128, B, D], F32)
    ctxT = sb("ctxT", [128, NT], F32)
    xnT = sb("xnT", [128, NT], F32)
    ident = sb("ident_f", [128, 128], F32)
    ident_b = sb("ident_b", [128, 128], BF16)
    stack_sel = sb("stack_sel", [128, 2, 2, 4, 128], FP16)
    max_rows = sb("max_rows", [128, 16, 128], BF16)
    causal = sb("causal", [128, 2, 128], BF16)
    rope = sb("rope", [128, 2, 128], F32)
    gates = sb("gates", [128, 12], F32)
    stats = sb("stats", [128, B, 6], F32)
    stats2 = sb("stats2", [128, B, 6], F32)
    ln_small = sb("ln_small", [128, 10, B], F32)
    minus_half = sb("minus_half", [128, B], F32)
    cols = sb("cols", [128, 4, 8], F32)
    bv_row = sb("bv_row", [128, 128], F32)
    gate_sel = sb("gate_sel", [128, 11 * 128], BF16)
    gateT = sb("gateT", [128, NT], BF16)
    b2_rows = sb("b2_rows", [128, 128], F32)
    b2_rest = sb("b2_rest", [128, 128], F32)
    b2_part = sb("b2_part", [128, 3, 128], BF16)
    br_row = sb("br_row", [128, 8], F32)
    W_att = Region(sb("W_att", [128, 4096], F32), 4096 * 4)
    W_ffn = Region(sb("W_ffn", [128, 8320], F32), 8320 * 4)
    STK = 12480
    stacks = Region(sb("stacks", [128, STK], F32), STK * 4)
    WRK = 9240
    work = Region(sb("work", [128, WRK], F32), WRK * 4)
    PS = [ctx.enter_context(nc.psum_tensor(f"bank{i}", [128, 512], F32)) for i in range(8)]

    phase_done = sem("phase_done")
    meets = {}

    def meet(eng):
        n = meets[id(eng)] = meets.get(id(eng), 0) + 1
        eng.drain().then_inc(phase_done, 1)
        eng.wait_ge(phase_done, 5 * n)

    load_x = sem("load_x")
    load_c = sem("load_c")
    load_const = sem("load_const")

    setup_ready = sem("setup_ready")
    ctx_turned = sem("ctx_turned")
    ctx_stored = sem("ctx_stored")
    stats_sem = sem("stats_sem")
    work.restart()
    ctx_in = stacks.tile[:, 0:B * D]

    def setup_sync(sp):
        sp.dma_start(ctx_in.rearrange("p (b d) -> p b d", d=D), A["ctx"].rearrange("b t d -> t b d")).then_inc(load_c, 16)
        sp.dma_start(X[:], A["x"].rearrange("b t d -> t b d")).then_inc(load_x, 16)
        for dst, name in ((ident[:], "ident"), (rope[:].rearrange("p a t -> p (a t)"), "rope"),
                          (stack_sel[:].rearrange("p a b c t -> p (a b c t)"), "stack_sel"),
                          (const_f[:, 0:2048], "max_rows"), (const_f[:, 2048:2304], "causal")):
            sp.dma_start(dst, A[name]).then_inc(load_const, 16)
        for i, name in enumerate(("g_xattn", "g_ffn", "L2_gate")):
            n = A[name].shape[0]
            sp.dma_start(gates_in[:, 4 * i:4 * i + n], bcast_rows(A[name], 128)).then_inc(load_const, 16)

    const_f = work.take([2304], F32)
    gates_in = work.take([12], F32)
    N_CONST = 8 * 16

    def setup_vector(dve):
        dve.memset(minus_half[:], -0.5).then_inc(setup_ready, 1)
        dve.memset(gates_in[:, 9:12], 0.0).then_inc(setup_ready, 1)
        dve.memset(gateT[:], 0.0)
        dve.wait_ge(load_const, N_CONST)
        dve.tensor_copy(ident_b[:], ident[:]).then_inc(setup_ready, 1)
        dve.tensor_copy(max_rows[:].rearrange("p a t -> p (a t)"), const_f[:, 0:2048]).then_inc(setup_ready, 1)
        dve.tensor_copy(causal[:].rearrange("p a t -> p (a t)"), const_f[:, 2048:2304]).then_inc(setup_ready, 1)
        dve.wait_ge(load_x, 16)
        for b in range(B):
            dve.bn_stats(stats[:, b, :], X[:, b, :])

    def setup_scalar(act):
        act.wait_ge(load_const, N_CONST)
        act.wait_ge(setup_ready, 2)
        act.activation(gates[:], gates_in, ACT.Tanh)
        for i in range(B // 4):
            act.wait_ge(ctx_turned, i + 1)
            act.copy(ctxT[:, 512 * i:512 * i + 512], PS[i % 4][:]).then_inc(ctx_stored, 1)

    def setup_tensor(pe):
        pe.wait_ge(load_c, 16)
        pe.wait_ge(load_const, N_CONST)
        for i in range(B // 4):
            wait(pe, ctx_stored, i - 3)
            for k in range(4):
                b = 4 * i + k
                last = pe.transpose(PS[i % 4][:, 128 * k:128 * k + 128], ctx_in[:, b * D:(b + 1) * D], ident[:])
            last.then_inc(ctx_turned, 1)

    ln_dve = sem("ln_dve")
    ln_pool = sem("ln_pool")
    ln_turned = sem("ln_turned")
    ln_stored = sem("ln_stored")
    NG4 = B // 4
    ln_uses = {"n": 0}
    STEPS = 6

    def layer_norm(second=None):
        use = ln_uses["n"]
        ln_uses["n"] += 1
        work.restart()
        xn = work.take([2, 4, D], F32)
        xn1 = stacks.tile[:, 0:B * D].rearrange("p (b d) -> p b d", d=D)
        src = xn1 if second == "second" else X[:]
        st = stats2 if second == "second" else stats
        keep = second == "first"
        base_v = use * (STEPS + NG4) + (NG4 * 0)
        t = [ln_small[:, i, :] for i in range(10)]
        gamma, beta = cols[:, 2, 4:5], cols[:, 2, 5:6]

        def vector(dve):
            m0, v0, m1, v1 = st[:, :, 1], st[:, :, 2], st[:, :, 4], st[:, :, 5]
            dve.tensor_tensor(t[0], m0, m1, ALU.subtract)
            dve.tensor_tensor(t[1], m0, m1, ALU.add)
            dve.tensor_tensor(t[2], v0, v1, ALU.add).then_inc(ln_dve, 1)
            dve.wait_ge(ln_dve, base_v + 1)
            dve.tensor_tensor(t[3], t[0], t[0], ALU.mult).then_inc(ln_dve, 1)
            dve.wait_ge(ln_dve, base_v + 2)
            dve.scalar_tensor_tensor(t[4], t[3], 32.0, t[2], ALU.mult, ALU.add).then_inc(ln_dve, 1)
            dve.wait_ge(ln_dve, base_v + 3)
            dve.tensor_scalar(t[5], t[4], 1.0 / D, LN_EPS, ALU.mult, ALU.add).then_inc(ln_dve, 1)
            dve.tensor_scalar(t[7], t[1], 0.5, None, ALU.mult).then_inc(ln_dve, 1)
            dve.wait_ge(ln_dve, base_v + 5)
            dve.wait_ge(ln_pool, use + 1)
            dve.tensor_copy(t[8], t[6]).then_inc(ln_dve, 1)
            dve.wait_ge(ln_dve, base_v + 6)

            def group(g, par):
                if not keep:
                    wait(dve, ln_turned, ln_turn_base + g - 1)
                for k in range(4):
                    b = g * 4 + k
                    dst = xn1[:, bass.ds(b, 1), :] if keep else xn[:, par, k:k + 1, :]
                    last = dve.tensor_scalar(dst, src[:, bass.ds(b, 1), :], t[7][:, bass.ds(b, 1)],
                                             t[8][:, bass.ds(b, 1)], ALU.subtract, ALU.mult)
                last.then_inc(ln_dve, 1)
                if keep:
                    dve.wait_ge(ln_dve, base_v + STEPS + g + 1)
                    for k in range(4):
                        b = g * 4 + k
                        dve.bn_stats(stats2[:, bass.ds(b, 1), :], xn1[:, bass.ds(b, 1), :])
            pairs(dve, group)

        def pool(pl):
            pl.wait_ge(ln_dve, base_v + 4)
            pl.tensor_tensor(t[6], t[5], minus_half[:], ALU.pow).then_inc(ln_pool, 1)

        turned_before = ln_uses.get("turned", 0)
        ln_turn_base = turned_before * NG4
        if not keep:
            ln_uses["turned"] = turned_before + 1

        def tensor(pe):
            if keep:
                return

            def group(g, par):
                pe.wait_ge(ln_dve, base_v + STEPS + g + 1)
                wait(pe, ln_stored, ln_turn_base + g - 1)
                for k in range(4):
                    last = pe.transpose(PS[par][:, 128 * k:128 * k + 128], xn[:, par, k, :], ident[:])
                last.then_inc(ln_turned, 1)
            pairs(pe, group)

        def scalar(act):
            if keep:
                return

            def group(g, par):
                act.wait_ge(ln_turned, ln_turn_base + g + 1)
                dst = xnT[:, bass.ds(g * 512, 512)]
                if second == "second":
                    act.activation(dst, PS[par][:], ACT.Identity, scale=gamma, bias=beta).then_inc(ln_stored, 1)
                else:
                    act.copy(dst, PS[par][:]).then_inc(ln_stored, 1)
            pairs(act, group)

        return dict(vector=vector, gpsimd=pool, tensor=tensor, scalar=scalar)

    def pairs(eng, group):
        group(0, 0)
        group(1, 1)
        if NG4 > 2:
            with eng.Fori(1, NG4 // 2) as r:
                group(2 * r, 0)
                group(2 * r + 1, 1)

    def attention(l):
        dh = HEAD_DIMS[l]
        wide = dh == 64
        GB = 2 if wide else 4
        T = GB * S
        NG = B // GB
        scale = float(dh) ** -0.5
        rotary, masked = l == 0, l == 0
        R = 64 if wide else ROW_TILE
        inner = H * dh
        nchunk = inner // 128

        W_att.restart()
        wq = W_att.take([inner], F32)
        wk = W_att.take([inner], F32)
        wv = W_att.take([inner], F32)
        wo = W_att.take([nchunk, D], F32)
        if rotary:
            wq_turn = W_att.take([D], F32)
            wk_turn = W_att.take([D], F32)
        stacks.restart()
        if wide:
            Q = [stacks.take([2, 8, T], FP16) for _ in range(2)]
            K = [stacks.take([2, 8, T], FP16) for _ in range(2)]
        else:
            Q = [stacks.take([4, T], FP16) for _ in range(2)]
            K = [stacks.take([4, 4, T], FP16) for _ in range(2)]
            K_stack = stacks.take([4, T], FP16)
        V = [stacks.take([GB, 2, H, dh + 1], FP16) for _ in range(2)]
        work.restart()
        P32 = work.take([4, 512], F32)
        Phi = work.take([4, 512], FP16)
        Plo = work.take([4, 512], FP16)
        o32 = work.take([2, inner], F32)
        y32 = work.take([T], F32)
        cst = work.take([GB, S], F32)
        m16 = work.take([2, 16], F32)
        mcat = work.take([128], BF16)
        mT = work.take([2, 128], BF16)
        rec = work.take([2, 16], F32)
        if wide:
            oT = [stacks_tail_take(T)]
        else:
            oT = [work.take([1, T], F32) for _ in range(2)]
            k32 = work.take([T], F32)
            q32 = work.take([T], F32)
            v32 = work.take([T], F32)
            khl = work.take([2, T], FP16)
            qhl = work.take([2, T], FP16)
            if rotary:
                turn1 = W_att.take([T], F32)
                turn2 = W_att.take([T], F32)

        names = ["s_ready", "max_done", "m_split", "m_chain", "mt_ready", "mt_stored", "st_ready", "exp_done",
                 "plo_dve", "plo_pool", "pv_done", "rec_done", "o_done", "ot_ready", "ot_stored", "yt_ready",
                 "y_stored", "yb_ready", "x_done", "ctx_staged", "ones_set"]
        if wide:
            names += ["kq_ready", "kq_hi", "kq_lo", "v_ready", "hi_v", "lo_v"]
        else:
            names += ["kp_ready", "qp_ready", "k32_done", "q32_done", "v_ready", "v32_done", "hi_k", "hi_q", "hi_v",
                      "lo_kq", "lo_v", "selk_ready", "selk_stored_a", "selk_stored_v", "zeros_dve", "zeros_pool",
                      "k_spread", "selq_ready", "selq_stored_a", "selq_stored_v", "turn_done"]
        s = {n: phase_sem("att", n) for n in names}
        w_loaded = att_loaded[l]
        w_count = att_loads(l)[1]

        def heads(quad):
            if wide:
                u, j = divmod(quad, 2)
                return [(2 * (4 * u + k) + j, slice(64 * j, 64 * j + 64), 4 * u + k, 4 * u + k) for k in range(4)]
            return [(4 * j + quad, slice(0, 128), j, 4 * quad + j) for j in range(4)]

        if wide:
            slots = {(0, 0): ["v0"], (0, 1): ["v1"], (0, 2): ["v2"], (0, 3): ["yt", "v3"],
                     (1, 0): ["k0", "q0"], (1, 1): ["k1", "q1"], (1, 2): ["k2", "q2", "yb"], (1, 3): ["k3", "q3"]}
            YT = 3
        else:
            slots = {(0, 0): ["kp"] + ["kp2"] * rotary, (0, 1): ["qp"] + ["qp2"] * rotary, (0, 2): ["v"], (0, 3): [],
                     (1, 0): ["selk0"], (1, 1): ["selk1"], (1, 2): ["selk2"], (1, 3): ["selk3"],
                     (2, 0): ["selq0"], (2, 1): ["selq1"], (2, 2): ["selq2"], (2, 3): ["selq3"],
                     (3, 0): ["yt"], (3, 1): [], (3, 2): ["yb"], (3, 3): []}
            YT = 2
        KQ_JOBS = ["k0", "q0", "k1", "q1", "k2", "q2", "k3", "q3"]
        order = []
        for k in range(GB):
            for q in range(4):
                order += [f"mt{k}"] * (q == 1) + [f"ot{k}_{i}" for i in range(nchunk // 4 or 1)] * (q == 2) + slots[k, q]
        banks = {job: 6 + i % 2 for i, job in enumerate(order)}
        NOT = nchunk // 4 or 1

        def ok(index, n):
            return not isinstance(index, int) or 0 <= index < n

        def rounds(eng, iteration):
            lead = 4
            for g in range(lead):
                iteration(g, g % 2)
            if NG > lead:
                with eng.Fori(lead // 2, NG // 2) as r:
                    iteration(2 * r, 0)
                    iteration(2 * r + 1, 1)
            for g in range(NG, NG + (3 if wide else 2)):
                iteration(g, g % 2)

        def stage(g, gp, k, q):
            b0 = GB * (g - 1) + k
            return b0, b0 - 1, b0 - 2, b0 - 3, (b0 - 2, q + 2, 2) if q < 2 else (b0 - 1, q - 2, 1)

        def place(g, gp, k, back):
            return ((1 - gp) if (k - back) // GB % 2 == 0 else gp), (k - back) % GB, (k - back) % 2

        def tensor(pe):
            pe.wait_ge(w_loaded, w_count)
            freed_by = {}
            for job in order:
                if job.startswith("mt"):
                    k = int(job[2])
                    freed_by[job] = ("mt_stored", lambda g, k=k: (g - 1) * GB + k)
                elif job.startswith("ot"):
                    k, i = int(job[2]), int(job[4])
                    freed_by[job] = ("ot_stored", lambda g, k=k, i=i: ((g - 1) * GB + k - 3) * NOT + i + 1)
                elif job == "yt":
                    freed_by[job] = ("y_stored", lambda g: g - YT + 1)
                elif job == "yb":
                    freed_by[job] = ("x_done", lambda g: g - YT + 1)
                elif wide and job[0] == "v":
                    freed_by[job] = ("lo_v", lambda g, n=int(job[1]): 4 * (g - 1) + n + 1)
                elif wide:
                    freed_by[job] = ("kq_lo", lambda g, n=KQ_JOBS.index(job): 8 * g + n + 1)
                elif job in ("kp", "kp2"):
                    freed_by[job] = ("k32_done", lambda g: g + 1)
                elif job in ("qp", "qp2"):
                    freed_by[job] = ("q32_done", lambda g: g + 1)
                elif job == "v":
                    freed_by[job] = ("v32_done", lambda g: g + 1)
                else:
                    c = int(job[4])
                    kind = "selk" if job[3] == "k" else "selq"
                    freed_by[job] = (f"{kind}_stored_{'av'[c % 2]}", lambda g, c=c: 2 * g + c // 2 + 1)
            last_in = {6: None, 7: None}

            def take(job, g):
                bank = banks[job]
                if last_in[bank] is not None:
                    name, count = last_in[bank]
                    wait(pe, s[name], count(g))
                last_in[bank] = freed_by[job]
                return PS[bank]

            def age():
                for b, v in last_in.items():
                    if v is not None:
                        name, count = v
                        last_in[b] = (name, lambda g, count=count: count(g - 1))

            def job_run(job, g, par):
                if job == "yt":
                    a = g - YT
                    if ok(a, NG):
                        ps = take(job, g)
                        pe.wait_ge(s["ot_stored"], (a + 1) * GB * NOT)
                        src = oT[0] if wide else oT[par]
                        for c in range(nchunk):
                            last = pe.matmul(ps[:, 0:T], wo[:, c, :], src[:, c, :], start=(c == 0), stop=(c == nchunk - 1))
                        last.then_inc(s["yt_ready"], 1)
                elif job == "yb":
                    a = g - YT
                    if ok(a, NG):
                        ps = take(job, g)
                        pe.wait_ge(s["y_stored"], a + 1)
                        for k in range(GB):
                            last = pe.transpose(ps[:, 128 * k:128 * k + 128], y32[:, 128 * k:128 * k + 128], ident[:])
                        last.then_inc(s["yb_ready"], 1)
                elif wide and job[0] == "v":
                    if ok(g - 1, NG):
                        ps = take(job, g)
                        i = int(job[1])
                        pe.wait_ge(s["ctx_staged"], g)
                        pe.matmul(ps[:], cst[:, i // 2, :], wv[:, 512 * (i % 2):512 * (i % 2) + 512],
                                  start=True, stop=True).then_inc(s["v_ready"], 1)
                elif not ok(g, NG):
                    return
                elif wide:
                    ps = take(job, g)
                    i = int(job[1])
                    w, src = (wk, ctxT) if job[0] == "k" else (wq, xnT)
                    for j in range(2):
                        t = 2 * i + j
                        last = pe.matmul(ps[:, T * j:T * j + T], w[:, 128 * t:128 * t + 128], src[:, bass.ds(g * T, T)],
                                         start=True, stop=True)
                    last.then_inc(s["kq_ready"], 1)
                elif job in ("kp", "kp2", "qp", "qp2"):
                    ps = take(job, g)
                    w = {"kp": wk, "qp": wq}.get(job)
                    if w is None:
                        w = wk_turn if job == "kp2" else wq_turn
                    src = ctxT if job[0] == "k" else xnT
                    pe.matmul(ps[:], w, src[:, bass.ds(g * T, T)], start=True, stop=True).then_inc(s[f"{job[0]}p_ready"], 1)
                elif job == "v":
                    ps = take(job, g)
                    pe.wait_ge(s["ctx_staged"], g + 1)
                    for k in range(GB):
                        last = pe.matmul(ps[:, 128 * k:128 * k + 128], cst[:, k, :], wv, start=True, stop=True)
                    last.then_inc(s["v_ready"], 1)
                else:
                    ps = take(job, g)
                    c, kind = int(job[4]), job[3]
                    if c == 0:
                        pe.wait_ge(s[f"hi_{kind}"], g + 1)
                        pe.wait_ge(s["lo_kq"], 2 * g + (1 if kind == "k" else 2))
                    src, t = (khl, 1) if kind == "k" else (qhl, 0)
                    pe.matmul(ps[:], stack_sel[:, t, 0, c, :], src[:, 0, :], start=True, stop=False)
                    pe.matmul(ps[:], stack_sel[:, t, 1, c, :], src[:, 1, :], start=False, stop=True).then_inc(s[f"sel{kind}_ready"], 1)

            def scores(b, quad, par, tok):
                ps = PS[quad % 2]
                wait(pe, s["max_done"], 4 * b + quad - 1)
                if masked:
                    pe.matmul(ps[:].rearrange("p (h k) -> p h k", h=4), ident_b[:],
                              causal[:, 0:1, :].to_broadcast([128, 4, 128]), start=True, stop=False, skip_group_check=True)
                if wide:
                    for k, (_, rows, block, _) in enumerate(heads(quad)):
                        for i, (a, c) in enumerate(((0, 0), (0, 1), (1, 0))):
                            last = pe.matmul(ps[:, 128 * k:128 * k + 128], Q[par][rows, a, block, tok], K[par][rows, c, block, tok],
                                             start=(i == 0), stop=(i == 2), skip_group_check=True)
                else:
                    last = pe.matmul(ps[:].rearrange("p (h k) -> p h k", h=4), Q[par][:, quad, tok], K[par][:, quad, :, tok],
                                     start=not masked, stop=True, skip_group_check=True)
                last.then_inc(s["s_ready"], 1)

            def scoresT(b, quad, par, tok, bp):
                ps = PS[2 + quad % 2]
                wait(pe, s["exp_done"], 4 * b + quad - 1)
                if quad == 0:
                    pe.wait_ge(s["mt_stored"], b + 1)
                if masked:
                    pe.matmul(ps[:].rearrange("p (h k) -> p h k", h=4), ident_b[:],
                              causal[:, 1:2, :].to_broadcast([128, 4, 128]), start=True, stop=False, skip_group_check=True)
                for k, (h, rows, block, pattern) in enumerate(heads(quad)):
                    dst = ps[:, 128 * k:128 * k + 128]
                    if wide:
                        for i, (a, c) in enumerate(((0, 0), (0, 1), (1, 0))):
                            pe.matmul(dst, K[par][rows, a, block, tok], Q[par][rows, c, block, tok], start=(i == 0), stop=False, skip_group_check=True)
                    else:
                        pe.matmul(dst, K[par][:, quad, block, tok], Q[par][:, quad, tok], start=not masked, stop=False, skip_group_check=True)
                    last = pe.matmul(dst, max_rows[rows, pattern, :], mT[rows, bp, :], start=False, stop=True, skip_group_check=True)
                last.then_inc(s["st_ready"], 1)

            def values(b, quad, par, kk, bp):
                pe.wait_ge(s["exp_done"], 4 * b + quad + 1)
                pe.wait_ge(s["plo_pool" if quad % 2 else "plo_dve"], 2 * b + quad // 2 + 1)
                if wide:
                    ps = PS[4 + quad % 2]
                    wait(pe, s["o_done"], 4 * b + quad - 1)
                else:
                    ps = PS[4 + bp]
                    if quad == 0:
                        wait(pe, s["o_done"], b - 1)
                for k, (h, _, _, _) in enumerate(heads(quad)):
                    n = (k if wide else h) * (dh + 1)
                    dst = ps[:, n:n + dh + 1]
                    hi, lo = Phi[:, quad, 128 * k:128 * k + 128], Plo[:, quad, 128 * k:128 * k + 128]
                    pe.matmul(dst, hi, V[par][:, kk, 0, h, :], start=True, stop=False)
                    pe.matmul(dst, hi, V[par][:, kk, 1, h, :], start=False, stop=False)
                    last = pe.matmul(dst, lo, V[par][:, kk, 0, h, :], start=False, stop=True)
                last.then_inc(s["pv_done"], 1)

            def iteration(g, gp):
                if not (isinstance(g, int) and g == 0):
                    age()
                for k in range(GB):
                    for q in range(4):
                        b0, b1, b2, b3, (bt, quad, back) = stage(g, gp, k, q)
                        if ok(b0, B):
                            par, kk, _ = place(g, gp, k, 0)
                            if k == 0 and q == 0:
                                pe.wait_ge(s["ones_set"], 1)
                                if wide:
                                    pe.wait_ge(s["kq_lo"], 8 * (g - 1) + 4)
                                else:
                                    pe.wait_ge(s["k_spread"], 64 * g)
                                    pe.wait_ge(s["selq_stored_a"], 2 * g)
                                    pe.wait_ge(s["selq_stored_v"], 2 * g)
                            if wide and k == 0 and q == 2:
                                pe.wait_ge(s["kq_lo"], 8 * g)
                            scores(b0, q, par, slice(128 * kk, 128 * kk + 128))
                        if q == 1 and ok(b1, B):
                            ps = take(f"mt{k}", g)
                            pe.wait_ge(s["m_split"], b1 + 1)
                            pe.transpose(ps[:, 0:64].bitcast(BF16), mcat, ident_b[:]).then_inc(s["mt_ready"], 1)
                        if q == 2 and ok(b3, B):
                            pe.wait_ge(s["o_done"], (b3 + 1) * (4 if wide else 1))
                            for i in range(NOT):
                                ps = take(f"ot{k}_{i}", g)
                                for c in range(min(4, nchunk)):
                                    src = o32[:, (k - 3) % 2, 128 * (4 * i + c):128 * (4 * i + c) + 128]
                                    last = pe.transpose(ps[:, 128 * c:128 * c + 128], src, ident[:])
                                last.then_inc(s["ot_ready"], 1)
                        if ok(bt, B):
                            par, kk, bp = place(g, gp, k, back)
                            scoresT(bt, quad, par, slice(128 * kk, 128 * kk + 128), bp)
                        for job in slots[k, q]: job_run(job, g, gp)
                        if ok(b2, B):
                            par, kk, bp = place(g, gp, k, 2)
                            if kk == 0 and q == 0:
                                n = g if k >= 2 else g - 1
                                pe.wait_ge(s["hi_v"], 4 * n if wide else n)
                                pe.wait_ge(s["lo_v"], 4 * n if wide else n)
                            values(b2, q, par, kk, bp)
            rounds(pe, iteration)

        def scalar(act):
            def exps(b, quad):
                ps = PS[2 + quad % 2]
                act.wait_ge(s["st_ready"], 4 * b + quad + 1)
                wait(act, s["pv_done"], 4 * b + quad - 3)
                wait(act, s["plo_pool" if quad % 2 else "plo_dve"], 2 * b + quad // 2 - 1)
                act.activation(Phi[:, quad, :], ps[:], ACT.Exp, scale=scale)
                act.activation(P32[:, quad, :], ps[:], ACT.Exp, scale=scale).then_inc(s["exp_done"], 1)

            def job_run(job, g, gp):
                ps = PS[banks[job]]
                if job == "yt":
                    a = g - YT
                    if ok(a, NG):
                        act.wait_ge(s["yt_ready"], a + 1)
                        wait(act, s["yb_ready"], a)
                        act.activation(y32, ps[:, 0:T], ACT.Identity, scale=cols[:, l, 6:7], bias=cols[:, l, 3:4]).then_inc(s["y_stored"], 1)
                elif wide and job[0] == "v":
                    if ok(g - 1, NG):
                        n = int(job[1])
                        act.wait_ge(s["v_ready"], 4 * (g - 1) + n + 1)
                        wait(act, s["pv_done"], 4 * GB * (g - 2))
                        act.copy(wide_place(job, 1 - gp)[0], wide_place(job, 1 - gp)[2]).then_inc(s["hi_v"], 1)
                elif job == "yb" or not ok(g, NG):
                    return
                elif wide:
                    n = KQ_JOBS.index(job)
                    act.wait_ge(s["kq_ready"], 8 * g + n + 1)
                    wait(act, s["st_ready"], 4 * GB * (g - 1) - (2 if n < 4 else 0))
                    hi_dst, _, src = wide_place(job, gp)
                    act.copy(hi_dst, src).then_inc(s["kq_hi"], 1)
                elif job in ("kp", "qp") and not rotary:
                    kind = job[0]
                    dst, col = (k32, 1) if kind == "k" else (q32, 0)
                    act.wait_ge(s[f"{kind}p_ready"], g + 1)
                    wait(act, s["lo_kq"], 2 * (g - 1) + (1 if kind == "k" else 2))
                    act.activation(dst, ps[:], ACT.Identity, bias=cols[:, l, col:col + 1]).then_inc(s[f"{kind}32_done"], 1)
                elif job[:3] == "sel" and int(job[4]) % 2 == 0:
                    kind, c = job[3], int(job[4])
                    act.wait_ge(s[f"sel{kind}_ready"], 4 * g + c + 1)
                    if c == 0 and kind == "k":
                        wait(act, s["k_spread"], 64 * g)
                    if c == 0 and kind == "q":
                        wait(act, s["st_ready"], 16 * (g - 1))
                    act.copy((K_stack if kind == "k" else Q[gp])[:, c, :], ps[:]).then_inc(s[f"sel{kind}_stored_a"], 1)

            def iteration(g, gp):
                for k in range(GB):
                    for q in range(4):
                        b0, b1, b2, b3, (bt, quad, back) = stage(g, gp, k, q)
                        gc = g - 1 if wide else g
                        if k == 0 and q == 0 and ok(gc, NG):
                            wait(act, s["v_ready"], 4 * gc if wide else gc)
                            act.copy(cst.rearrange("p a b -> p (a b)"), ctxT[:, bass.ds(gc * T, T)]).then_inc(s["ctx_staged"], 1)
                        if q == 1 and ok(b1, B):
                            act.wait_ge(s["mt_ready"], b1 + 1)
                            wait(act, s["st_ready"], 4 * (b1 - 1))
                            act.copy(mT[:, (k - 1) % 2, :], PS[banks[f"mt{k}"]][:, 0:64].bitcast(BF16)).then_inc(s["mt_stored"], 1)
                        if ok(bt, B): exps(bt, quad)
                        if q == 2 and ok(b3, B):
                            par, k3, _ = place(g, gp, k, 3)
                            for i in range(NOT):
                                act.wait_ge(s["ot_ready"], b3 * NOT + i + 1)
                                n = min(4, nchunk)
                                src = PS[banks[f"ot{k}_{i}"]][:, 0:128 * n].rearrange("p (c t) -> p c t", c=n)
                                if k3 == 0 and i == 0:
                                    wait(act, s["yt_ready"], g - 2)
                                dst = (oT[0] if wide else oT[par])[:, n * i:n * i + n, 128 * k3:128 * k3 + 128]
                                act.copy(dst, src).then_inc(s["ot_stored"], 1)
                        for job in slots[k, q]: job_run(job, g, gp)
                        if not wide and ok(g, NG):
                            if k == 0 and q in (1, 2):
                                kind, x32, hl, n = (("k", k32, khl, 1), ("q", q32, qhl, 2))[q - 1]
                                act.wait_ge(s[f"{kind}32_done"], g + 1)
                                wait(act, s[f"sel{kind}_ready"], 4 * g)
                                wait(act, s["lo_kq"], 2 * (g - 1) + n)
                                act.copy(hl[:, 0, :], x32).then_inc(s[f"hi_{kind}"], 1)
                            if k == 2 and q == 1:
                                act.wait_ge(s["v32_done"], g + 1)
                                wait(act, s["pv_done"], 16 * (g - 1))
                                act.copy(V[gp][:, :, 0, :, 0:dh], v32.rearrange("p (b h d) -> p b h d", b=GB, h=H)).then_inc(s["hi_v"], 1)
            rounds(act, iteration)

        def wide_place(job, gp):
            ps, i = PS[banks[job]], int(job[1])
            if job[0] == "v":
                src = ps[:].rearrange("p (h d) -> p h d", d=dh)
                h0 = 8 * (i % 2)
                return V[gp][:, i // 2, 0, h0:h0 + 8, 0:dh], V[gp][:, i // 2, 1, h0:h0 + 8, 0:dh], src
            buf = (K if job[0] == "k" else Q)[gp]
            src = ps[:].rearrange("p (j t) -> p j t", j=2)
            return buf[:, 0, 2 * i:2 * i + 2, :], buf[:, 1, 2 * i:2 * i + 2, :], src

        def vector(dve):
            dve.memset(mcat, 0.0).then_inc(s["ones_set"], 1)
            for p in range(2):
                for part in range(2):
                    last = dve.memset(V[p][:, :, part, :, dh:dh + 1], 1.0 - part)
            last.then_inc(s["ones_set"], 1)
            dve.wait_ge(s["ones_set"], 2)
            if not wide:
                dve.memset(K[0].rearrange("p c j t -> p (c j t)"), 0.0).then_inc(s["zeros_dve"], 1)

            def row_max(b, quad, bp):
                dve.wait_ge(s["s_ready"], 4 * b + quad + 1)
                if quad == 0:
                    wait(dve, s["m_split"], b - 1)
                at = 8 * (quad % 2) + 4 * (quad // 2) if wide else 4 * quad
                dve.tensor_reduce(m16[:, bp, at:at + 4], PS[quad % 2][:].rearrange("p (h k) -> p h k", h=4),
                                  AX, ALU.max).then_inc(s["max_done"], 1)

            def split_max(b, bp):
                dve.wait_ge(s["max_done"], 4 * b + 4)
                wait(dve, s["mt_ready"], b)
                if wide:
                    src = m16[:, bp, :].rearrange("p (j k) -> p j k", j=2)
                    mview = mcat.rearrange("p (j k) -> p j k", j=2)
                    hi, lo = mview[:, :, 0:8], mview[:, :, 16:24]
                else:
                    src, hi, lo = m16[:, bp, :], mcat[:, 0:16], mcat[:, 16:32]
                dve.tensor_scalar(hi, src, -1.0, None, ALU.mult).then_inc(s["m_chain"], 1)
                dve.wait_ge(s["m_chain"], b + 1)
                dve.scalar_tensor_tensor(lo, src, -1.0, hi, ALU.mult, ALU.subtract).then_inc(s["m_split"], 1)

            def normalise(b, units, bp, ob):
                for q in units:
                    n = 4 if wide else 16
                    cnt = (4 * b + q) if wide else b
                    ps = PS[4 + (q % 2 if wide else bp)][:, 0:n * (dh + 1)].rearrange("p (h d) -> p h d", h=n)
                    dve.wait_ge(s["pv_done"], 4 * b + q + 1)
                    rb = q % 2 if wide else bp
                    wait(dve, s["o_done"], cnt - 1)
                    dve.reciprocal(rec[:, rb, 0:n], ps[:, :, dh]).then_inc(s["rec_done"], 1)
                    dve.wait_ge(s["rec_done"], cnt + 1)
                    if wide:
                        if q == 0:
                            wait(dve, s["ot_ready"], 2 * (b - 1))
                        u, j = divmod(q, 2)
                        dst = o32[:, ob, :].rearrange("p (t j d) -> p t j d", j=2, d=dh)[:, 4 * u:4 * u + 4, j, :]
                    else:
                        wait(dve, s["ot_ready"], b - 1)
                        dst = o32[:, ob, :].rearrange("p (h d) -> p h d", h=16)
                    dve.tensor_tensor(dst, ps[:, :, 0:dh], rec[:, rb, 0:n].unsqueeze(2).to_broadcast([128, n, dh]),
                                      ALU.mult).then_inc(s["o_done"], 1)

            def low_half(b, quad):
                dve.wait_ge(s["exp_done"], 4 * b + quad + 1)
                wait(dve, s["pv_done"], 4 * b + quad - 3)
                dve.tensor_tensor(Plo[:, quad, :], P32[:, quad, :], Phi[:, quad, :], ALU.subtract).then_inc(s["plo_dve"], 1)

            def job_run(job, g, gp):
                ps = PS[banks[job]]
                if job == "yt":
                    return
                if job == "yb":
                    a = g - YT
                    if ok(a, NG):
                        dve.wait_ge(s["yb_ready"], a + 1)
                        xs = X[:, bass.ds(a * GB, GB), :]
                        dve.tensor_tensor(xs, xs, ps[:, 0:T].rearrange("p (b d) -> p b d", b=GB), ALU.add).then_inc(s["x_done"], 1)
                        dve.wait_ge(s["x_done"], a + 1)
                        for k in range(GB):
                            dve.bn_stats(stats[:, bass.ds(a * GB + k, 1), :], X[:, bass.ds(a * GB + k, 1), :])
                elif wide and job[0] == "v":
                    if ok(g - 1, NG):
                        dve.wait_ge(s["hi_v"], 4 * (g - 1) + int(job[1]) + 1)
                        hi, lo, src = wide_place(job, 1 - gp)
                        dve.tensor_tensor(lo, src, hi, ALU.subtract).then_inc(s["lo_v"], 1)
                elif not ok(g, NG):
                    return
                elif wide:
                    dve.wait_ge(s["kq_hi"], 8 * g + KQ_JOBS.index(job) + 1)
                    hi, lo, src = wide_place(job, gp)
                    dve.tensor_tensor(lo, src, hi, ALU.subtract).then_inc(s["kq_lo"], 1)
                elif job in ("kp2", "qp2"):
                    kind = job[0]
                    first = PS[banks[kind + "p"]][:].rearrange("p (b t) -> p b t", b=GB)
                    second = ps[:].rearrange("p (b t) -> p b t", b=GB)
                    dst = k32 if kind == "k" else q32
                    i = 0 if kind == "k" else 1
                    dve.wait_ge(s[f"{kind}p_ready"], 2 * g + 2)
                    wait(dve, s["turn_done"], 4 * g + 2 * i - 1 + 1)
                    dve.tensor_tensor(turn1.rearrange("p (b t) -> p b t", b=GB), first,
                                      rope[:, 0:1, :].to_broadcast([128, GB, 128]), ALU.mult).then_inc(s["turn_done"], 1)
                    dve.tensor_tensor(turn2.rearrange("p (b t) -> p b t", b=GB), second,
                                      rope[:, 1:2, :].to_broadcast([128, GB, 128]), ALU.mult).then_inc(s["turn_done"], 1)
                    dve.wait_ge(s["turn_done"], 4 * g + 2 * i + 2)
                    wait(dve, s["lo_kq"], 2 * (g - 1) + i + 1)
                    wait(dve, s[f"hi_{kind}"], g)
                    dve.tensor_tensor(dst, turn1, turn2, ALU.add).then_inc(s[f"{kind}32_done"], 1)
                    dve.wait_ge(s[f"{kind}32_done"], g + 1)
                elif job == "v":
                    dve.wait_ge(s["v_ready"], g + 1)
                    wait(dve, s["lo_v"], g)
                    dve.tensor_tensor(v32.rearrange("p (b d) -> p b d", b=GB), ps[:].rearrange("p (b d) -> p b d", b=GB),
                                      bv_row[:].unsqueeze(1).to_broadcast([128, GB, 128]), ALU.add).then_inc(s["v32_done"], 1)
                elif job[:3] == "sel" and int(job[4]) % 2 == 1:
                    kind, c = job[3], int(job[4])
                    dve.wait_ge(s[f"sel{kind}_ready"], 4 * g + c + 1)
                    if c == 1 and kind == "k":
                        wait(dve, s["k_spread"], 64 * g)
                    if c == 1 and kind == "q":
                        wait(dve, s["st_ready"], 16 * (g - 1))
                    dve.tensor_copy((K_stack if kind == "k" else Q[gp])[:, c, :], ps[:]).then_inc(s[f"sel{kind}_stored_v"], 1)

            def iteration(g, gp):
                for k in range(GB):
                    for q in range(4):
                        b0, b1, b2, b3, _ = stage(g, gp, k, q)
                        p0, p1, p2 = k % 2, (k - 1) % 2, k % 2
                        if q == 0:
                            if ok(b1, B): split_max(b1, p1)
                            if ok(b3, B): normalise(b3, (3,), p1, p1)
                        if q == 1 and ok(b2, B): low_half(b2, 2)
                        if q == 3 and ok(b1, B): low_half(b1, 0)
                        if ok(b0, B): row_max(b0, q, p0)
                        if wide and q >= 1 and ok(b2, B): normalise(b2, (q - 1,), p2, p2)
                        for job in slots[k, q]: job_run(job, g, gp)
            rounds(dve, iteration)

        def gpsimd(pool):
            def low_half(b, quad):
                pool.wait_ge(s["exp_done"], 4 * b + quad + 1)
                wait(pool, s["pv_done"], 4 * b + quad - 3)
                pool.tensor_tensor(Plo[:, quad, :], P32[:, quad, :], Phi[:, quad, :], ALU.subtract).then_inc(s["plo_pool"], 1)

            def iteration(g, gp):
                for k in range(GB):
                    for q in range(4):
                        b0, b1, b2, b3, _ = stage(g, gp, k, q)
                        if q == 1 and ok(b2, B): low_half(b2, 3)
                        if q == 3 and ok(b1, B): low_half(b1, 1)
                        if wide or not ok(g, NG):
                            continue
                        if k == 0 and q in (1, 2):
                            kind, x32, hl = (("k", k32, khl), ("q", q32, qhl))[q - 1]
                            pool.wait_ge(s[f"hi_{kind}"], g + 1)
                            wait(pool, s[f"sel{kind}_ready"], 4 * g)
                            pool.tensor_tensor(hl[:, 1, :], x32, hl[:, 0, :], ALU.subtract).then_inc(s["lo_kq"], 1)
                        if k == 2 and q == 2:
                            pool.wait_ge(s["hi_v"], g + 1)
                            vsrc = v32.rearrange("p (b h d) -> p b h d", b=GB, h=H)
                            for b in range(GB):
                                last = pool.tensor_tensor(V[gp][:, b, 1, :, 0:dh], vsrc[:, b], V[gp][:, b, 0, :, 0:dh], ALU.subtract)
                            last.then_inc(s["lo_v"], 1)
            if not wide:
                pool.memset(K[1].rearrange("p c j t -> p (c j t)"), 0.0).then_inc(s["zeros_pool"], 1)
            rounds(pool, iteration)

        def sync(sp):
            if wide:
                return

            sp.wait_ge(s["zeros_dve"], 1)
            sp.wait_ge(s["zeros_pool"], 1)
            for g in range(NG):
                sp.wait_ge(s["selk_stored_a"], 2 * g + 2)
                sp.wait_ge(s["selk_stored_v"], 2 * g + 2)
                wait(sp, s["st_ready"], 16 * (g - 1))
                for j in range(4):
                    rows = slice(32 * j, 32 * j + 32)
                    sp.dma_start(K[g % 2][rows, :, j, :], K_stack[rows, :, :]).then_inc(s["k_spread"], 16)

        return dict(tensor=tensor, scalar=scalar, vector=vector, gpsimd=gpsimd, sync=sync)

    def stacks_tail_take(T):
        W_ffn.restart(W_ffn.size - 8 * T * 4)
        return W_ffn.take([8, T], F32)

    ffn_loaded = [sem(f"ffn_loaded{l}") for l in range(4)]
    EXPERTS = {0: 8, 1: 16, 3: 8}
    TOP = {0: 2, 1: 4, 3: 1}
    TILES = {0: 11, 1: 9, 3: 32}

    def ffn_weights(l):
        W_ffn.restart()
        if l == 2:
            w = {n: W_ffn.take([D], F32) for n in ("wr", "wk", "wv")}
            w["mu"] = W_ffn.take([4], F32)
            loads = [(w[n], A[f"F2_{n}"]) for n in ("wr", "wk", "wv")] + [(w["mu"][:, 0:2], A["F2_mu"])]
            return w, loads
        n, E = TILES[l], EXPERTS[l]
        w = {"up": W_ffn.take([n * 128], F32), "down": W_ffn.take([n * 128], F32), "router": W_ffn.take([E], F32)}
        if l == 0:
            w["up2"] = W_ffn.take([n * 128], F32)
        loads = [(w[k], A[f"F{l}_{k}"]) for k in w]
        ngate = A[f"gate_sel{l}"].shape[1]
        loads.append((gate_sel[:, 0:ngate], A[f"gate_sel{l}"]))
        if l == 3:
            w["b1"] = W_ffn.take([n], F32)
            loads.append((w["b1"], A["F3_b1"]))
            loads.append((b2_rows[:], A["F3_b2"]))
            loads.append((br_row[:], bcast_rows(A["F3_br"], 128)))
        return w, loads

    def ffn_load_phase(l):
        def sync(sp):
            for dst, src in ffn_weights(l)[1]:
                sp.dma_start(dst, src).then_inc(ffn_loaded[l], 16)
        return dict(sync=sync)

    def router(l):
        E, top = EXPERTS[l], TOP[l]
        w, loads = ffn_weights(l)
        work.restart()
        logits = work.take([B, E], F32)
        e = work.take([B, E], F32)
        rest = work.take([B, E], F32)
        gate = work.take([B, E], F32)
        part = work.take([B, 3, E], BF16)
        best = work.take([B, 8], F32)
        red = work.take([3, B], F32)
        logit_ready, exp_ready, step, part_ready, turned, turned_out = (
            phase_sem("router", n) for n in ("logit_ready", "exp_ready", "step", "part_ready", "turned", "turned_out"))

        def tensor(pe):
            pe.wait_ge(ffn_loaded[l], 16 * len(loads))
            for b in range(B):
                last = pe.matmul(PS[0][:, E * b:E * b + E], xnT[:, 128 * b:128 * b + 128], w["router"], start=True, stop=True)
            last.then_inc(logit_ready, 1)
            pe.wait_ge(part_ready, 1)
            for i in range(NG4):
                wait(pe, turned_out, i - 1)
                for k in range(4):
                    b = 4 * i + k
                    last = pe.transpose(PS[1 + i % 2][:].bitcast(BF16)[0:3 * E, 128 * k:128 * k + 128],
                                        part[:, b, :, :].rearrange("p a e -> p (a e)"), ident_b[:])
                last.then_inc(turned, 1)

        def scalar(act):
            act.wait_ge(step, 3)
            act.activation(e, logits, ACT.Exp).then_inc(exp_ready, 1)
            for i in range(NG4):
                act.wait_ge(turned, i + 1)
                act.copy(gateT[0:3 * E, 512 * i:512 * i + 512], PS[1 + i % 2][:].bitcast(BF16)[0:3 * E, 0:512]).then_inc(turned_out, 1)

        def vector(dve):
            n = [0]

            def chain(ins):
                n[0] += 1
                ins.then_inc(step, 1)
                dve.wait_ge(step, n[0])
            dve.wait_ge(logit_ready, 1)
            ps = PS[0][:, 0:B * E].rearrange("p (b e) -> p b e", e=E)
            if l == 3:
                chain(dve.tensor_tensor(logits, ps, br_row[:].unsqueeze(1).to_broadcast([128, B, E]), ALU.add))
            else:
                chain(dve.tensor_copy(logits, ps))
            chain(dve.tensor_reduce(red[:, 0, :], logits, AX, ALU.max))
            chain(dve.tensor_tensor(logits, logits, red[:, 0, :].unsqueeze(2).to_broadcast([128, B, E]), ALU.subtract))
            dve.wait_ge(exp_ready, 1)
            dve.tensor_reduce(red[:, 1, :], e, AX, ALU.add)
            for b in range(B):
                last = dve.max(best[:, b, :], e[:, b, :])
            chain(last)
            dve.reciprocal(red[:, 2, :], red[:, 1, :])
            chain(dve.memset(best[:, :, top:8], -1.0))
            for b in range(B):
                last = dve.match_replace(rest[:, b, :], best[:, b, :], e[:, b, :], -1.0)
            chain(last)
            chain(dve.scalar_tensor_tensor(gate, rest, 0.0, e, ALU.is_lt, ALU.mult))
            chain(dve.tensor_tensor(gate, gate, red[:, 2, :].unsqueeze(2).to_broadcast([128, B, E]), ALU.mult))
            chain(dve.tensor_copy(part[:, :, 0, :], gate))
            chain(dve.tensor_tensor(gate, gate, part[:, :, 0, :], ALU.subtract))
            chain(dve.tensor_copy(part[:, :, 1, :], gate))
            chain(dve.tensor_tensor(gate, gate, part[:, :, 1, :], ALU.subtract))
            dve.tensor_copy(part[:, :, 2, :], gate).then_inc(part_ready, 1)
            if l == 3:
                chain(dve.tensor_copy(b2_part[:, 0, :], b2_rows[:]))
                chain(dve.tensor_tensor(b2_rest[:], b2_rows[:], b2_part[:, 0, :], ALU.subtract))
                chain(dve.tensor_copy(b2_part[:, 1, :], b2_rest[:]))
                chain(dve.tensor_tensor(b2_rest[:], b2_rest[:], b2_part[:, 1, :], ALU.subtract))
                chain(dve.tensor_copy(b2_part[:, 2, :], b2_rest[:]))

        return dict(tensor=tensor, scalar=scalar, vector=vector)

    def experts(l):
        n, E = TILES[l], EXPERTS[l]
        w, loads = ffn_weights(l)
        func = ACT.Silu if l == 0 else ACT.Gelu
        work.restart()
        act_out = work.take([2, 512], F32)
        prod = work.take([2, 512], F32)
        hid = work.take([2, 512], F32)
        y32 = work.take([512], F32)
        up_ready, act_done, prod_done, hid_done, down_done, y_ready, y_stored, yb_ready, x_done = (
            phase_sem("experts", k) for k in ("up_ready", "act_done", "prod_done", "hid_done", "down_done", "y_ready",
                                       "y_stored", "yb_ready", "x_done"))

        def before(t):
            return 2 if t >= 2 or n % 2 == 0 else (1, 3)[t]

        def gate_of(t):
            return {0: t, 1: t - 1 if t else None, 3: t // 4}[l]

        def gate_bank(t):
            return PS[4 + ((t // 4) % 2 if l == 3 else t % 2)]

        def ok(g):
            return not isinstance(g, int) or 0 <= g < NG4

        def rounds(eng, group):
            group(0)
            if NG4 > 1:
                with eng.Fori(1, NG4) as g:
                    group(g)
            group(NG4)

        def tensor(pe):
            def down(g, t):
                N = g * n + t
                pe.wait_ge(hid_done, N + 1)
                if t == 0:
                    wait(pe, y_stored, g)
                    if l == 3:
                        for p in range(3):
                            pe.matmul(PS[6][:], b2_part[:, p, :], gateT[:, bass.ds(g * 512, 512)], start=(p == 0), stop=False)
                last = pe.matmul(PS[6][:], w["down"][:, 128 * t:128 * t + 128], hid[:, t % 2, :],
                                 start=(t == 0 and l != 3), stop=(t == n - 1))
                last.then_inc(down_done, 1)

            def group(g):
                if ok(g):
                    tok = bass.ds(g * 512, 512)
                for t in range(n):
                    if ok(g):
                        N = g * n + t
                        gt = gate_of(t)
                        if gt is not None and (l != 3 or t % 4 == 0):
                            wait(pe, hid_done, N - 4 if l == 3 else N - before(t) + 1)
                            pe.matmul(gate_bank(t)[:], gate_sel[:, 128 * gt:128 * gt + 128], gateT[:, tok], start=True, stop=True)
                        wait(pe, act_done, N - before(t) + 1)
                        if l == 0:
                            wait(pe, prod_done, N - before(t) + 1)
                            pe.matmul(PS[2 + t % 2][:], w["up2"][:, 128 * t:128 * t + 128], xnT[:, tok], start=True, stop=True)
                        pe.matmul(PS[t % 2][:], w["up"][:, 128 * t:128 * t + 128], xnT[:, tok], start=True, stop=True).then_inc(up_ready, 1)
                        if t:
                            down(g, t - 1)
                    if t == 0 and ok(g - 1):
                        down(g - 1, n - 1)
                    if t == 4 and ok(g - 1):
                        pe.wait_ge(y_stored, g)
                        wait(pe, x_done, g - 1)
                        for k in range(4):
                            last = pe.transpose(PS[7][:, 128 * k:128 * k + 128], y32[:, 128 * k:128 * k + 128], ident[:])
                        last.then_inc(yb_ready, 1)
            rounds(pe, group)

        def scalar(act):
            def group(g):
                for t in range(n):
                    if ok(g):
                        N = g * n + t
                        act.wait_ge(up_ready, N + 1)
                        wait(act, prod_done if l == 0 else hid_done, N - before(t) + 1)
                        act.activation(act_out[:, t % 2, :], PS[t % 2][:], func,
                                       **(dict(bias=w["b1"][:, t:t + 1]) if l == 3 else {})).then_inc(act_done, 1)
                    if t == 0 and ok(g - 1):
                        act.wait_ge(down_done, g * n)
                        wait(act, yb_ready, g - 1)
                        act.activation(y32, PS[6][:], ACT.Copy, scale=gates[:, 4 + l:5 + l]).then_inc(y_stored, 1)
            rounds(act, group)

        def vector(dve):
            def group(g):
                for t in range(n):
                    if ok(g):
                        N = g * n + t
                        dve.wait_ge(act_done, N + 1)
                        src = act_out[:, t % 2, :]
                        if l == 0:
                            wait(dve, hid_done, N - before(t) + 1)
                            dve.tensor_tensor(prod[:, t % 2, :], src, PS[2 + t % 2][:], ALU.mult).then_inc(prod_done, 1)
                            dve.wait_ge(prod_done, N + 1)
                            src = prod[:, t % 2, :]
                        wait(dve, down_done, N - before(t) + 1)
                        if gate_of(t) is None:
                            last = dve.tensor_copy(hid[:, t % 2, :], src)
                        else:
                            last = dve.tensor_tensor(hid[:, t % 2, :], src, gate_bank(t)[:], ALU.mult)
                        last.then_inc(hid_done, 1)
                    if t == 5 and ok(g - 1):
                        dve.wait_ge(yb_ready, g)
                        xs = X[:, bass.ds((g - 1) * 4, 4), :]
                        dve.tensor_tensor(xs, xs, PS[7][:].rearrange("p (b d) -> p b d", b=4), ALU.add).then_inc(x_done, 1)
                        dve.wait_ge(x_done, g)
                        for k in range(4):
                            dve.bn_stats(stats[:, bass.ds((g - 1) * 4 + k, 1), :], X[:, bass.ds((g - 1) * 4 + k, 1), :])
            rounds(dve, group)

        return dict(tensor=tensor, scalar=scalar, vector=vector)

    def token_mix():
        w, loads = ffn_weights(2)
        work.restart()
        faded = work.take([2, 512], F32)
        mixed = work.take([2, 2, 512], F32)
        r_gate = work.take([2, 512], F32)
        relu = work.take([512], F32)
        squared = work.take([2, 512], F32)
        y32 = work.take([2, 512], F32)
        mu, rest = w["mu"][:, 0:2], w["mu"][:, 2:4]
        mu_ready, faded_done, mixed_done, rk_ready, r_done, relu_done, sq_done, v_ready, y_done, yb_ready, x_done = (
            sem(f"T_{k}") for k in ("mu_ready", "faded_done", "mixed_done", "rk_ready", "r_done", "relu_done",
                                    "sq_done", "v_ready", "y_done", "yb_ready", "x_done"))

        def ok(g):
            return not isinstance(g, int) or 0 <= g < NG4

        def rounds(eng, step):
            for g in range(4):
                step(g, g % 2)
            if NG4 > 4:
                with eng.Fori(2, NG4 // 2) as r:
                    step(2 * r, 0)
                    step(2 * r + 1, 1)
            step(NG4, 0)
            step(NG4 + 1, 1)

        def tensor(pe):
            pe.wait_ge(ffn_loaded[2], 16 * len(loads))

            def step(g, p):
                if ok(g):
                    pe.wait_ge(mixed_done, g + 1)
                    wait(pe, r_done, g - 1)
                    wait(pe, relu_done, g - 1)
                    pe.matmul(PS[p][:], w["wr"], mixed[:, p, 0, :], start=True, stop=True)
                    pe.matmul(PS[2 + p][:], w["wk"], mixed[:, p, 1, :], start=True, stop=True).then_inc(rk_ready, 1)
                if ok(g - 1):
                    pe.wait_ge(sq_done, g)
                    wait(pe, y_done, g - 2)
                    pe.matmul(PS[5 - p][:], w["wv"], squared[:, 1 - p, :], start=True, stop=True).then_inc(v_ready, 1)
                if ok(g - 2):
                    pe.wait_ge(y_done, g - 1)
                    wait(pe, x_done, g - 3)
                    for k in range(4):
                        last = pe.transpose(PS[6 + p][:, 128 * k:128 * k + 128], y32[:, p, 128 * k:128 * k + 128], ident[:])
                    last.then_inc(yb_ready, 1)
            rounds(pe, step)

        def scalar(act):
            def step(g, p):
                if ok(g):
                    act.wait_ge(rk_ready, g + 1)
                    wait(act, y_done, g - 1)
                    act.activation(r_gate[:, p, :], PS[p][:], ACT.Sigmoid).then_inc(r_done, 1)
            rounds(act, step)

        def vector(dve):
            dve.wait_ge(ffn_loaded[2], 16 * len(loads))
            dve.tensor_scalar(rest, mu, -1.0, 1.0, ALU.mult, ALU.add).then_inc(mu_ready, 1)
            dve.wait_ge(mu_ready, 1)

            def step(g, p):
                if ok(g):
                    x = xnT[:, bass.ds(g * 512, 512)]
                    xs = x.rearrange("p (b t) -> p b t", b=4)
                    wait(dve, mixed_done, g)
                    for i in range(2):
                        last = dve.tensor_scalar(faded[:, i, :], x, rest[:, i:i + 1], None, ALU.mult)
                    last.then_inc(faded_done, 1)
                    dve.wait_ge(faded_done, g + 1)
                    wait(dve, rk_ready, g - 1)
                    for i in range(2):
                        m = mixed[:, p, i, :].rearrange("p (b t) -> p b t", b=4)
                        f = faded[:, i, :].rearrange("p (b t) -> p b t", b=4)
                        dve.tensor_scalar(m[:, :, 0:1], xs[:, :, 0:1], mu[:, i:i + 1], None, ALU.mult)
                        last = dve.scalar_tensor_tensor(m[:, :, 1:128], xs[:, :, 1:128], mu[:, i:i + 1], f[:, :, 0:127], ALU.mult, ALU.add)
                    last.then_inc(mixed_done, 1)
                if ok(g - 1):
                    q = 1 - p
                    dve.wait_ge(rk_ready, g)
                    wait(dve, sq_done, g - 1)
                    dve.tensor_scalar(relu, PS[2 + q][:], 0.0, None, ALU.max).then_inc(relu_done, 1)
                    dve.wait_ge(relu_done, g)
                    wait(dve, v_ready, g - 2)
                    dve.tensor_tensor(squared[:, q, :], relu, relu, ALU.mult).then_inc(sq_done, 1)
                    dve.wait_ge(v_ready, g)
                    dve.wait_ge(r_done, g)
                    wait(dve, yb_ready, g - 2)
                    dve.scalar_tensor_tensor(y32[:, q, :], PS[5 - p][:], gates[:, 6:7], r_gate[:, q, :], ALU.mult, ALU.mult).then_inc(y_done, 1)
                if ok(g - 2):
                    dve.wait_ge(yb_ready, g - 1)
                    xs = X[:, bass.ds((g - 2) * 4, 4), :]
                    dve.tensor_tensor(xs, xs, PS[6 + p][:].rearrange("p (b d) -> p b d", b=4), ALU.add).then_inc(x_done, 1)
                    dve.wait_ge(x_done, g - 1)
                    for k in range(4):
                        dve.bn_stats(stats[:, bass.ds((g - 2) * 4 + k, 1), :], X[:, bass.ds((g - 2) * 4 + k, 1), :])
            rounds(dve, step)

        return dict(tensor=tensor, scalar=scalar, vector=vector)

    def feed_forward(l):
        return [token_mix()] if l == 2 else [router(l), experts(l)]

    att_loaded = [sem(f"att_loaded{l}") for l in range(4)]

    def att_loads(l):
        W_att.restart()
        inner = H * HEAD_DIMS[l]
        nchunk = inner // 128
        dst = {n: W_att.take([inner], F32) for n in ("wq", "wk", "wv")}
        dst["wo"] = W_att.take([nchunk * D], F32)
        loads = [(dst[n], A[f"L{l}_{n}"]) for n in ("wq", "wk", "wv", "wo")]
        if l == 0:
            loads += [(W_att.take([D], F32), A["L0_wq_turn"]), (W_att.take([D], F32), A["L0_wk_turn"])]
        loads.append((cols[:, l, 0:3], A[f"L{l}_cols"][:, 0:3]))
        if l == 2:
            loads.append((cols[:, l, 4:6], A["L2_cols"][:, 3:5]))
        else:
            loads.append((bv_row[:], bcast_rows(A[f"L{l}_bv"], 128)))
        return loads, 16 * len(loads)

    def att_scales(l):
        def vector(dve):
            dve.wait_ge(att_loaded[l], att_loads(l)[1])
            if l == 2:
                dve.tensor_tensor(cols[:, l, 6:7], gates[:, l:l + 1], gates[:, 8:9], ALU.mult).then_inc(scale_ready[l], 1)
            else:
                dve.tensor_copy(cols[:, l, 6:7], gates[:, l:l + 1]).then_inc(scale_ready[l], 1)
            dve.wait_ge(scale_ready[l], 1)
            dve.tensor_tensor(cols[:, l, 3:4], cols[:, l, 2:3], cols[:, l, 6:7], ALU.mult).then_inc(scale_ready[l], 1)
        return dict(vector=vector)

    scale_ready = [sem(f"scale_ready{l}") for l in range(4)]

    phases = [dict(tensor=setup_tensor, scalar=setup_scalar, vector=setup_vector, sync=setup_sync)]

    def att_load_phase(l):
        def sync(sp):
            for dst, src in att_loads(l)[0]:
                sp.dma_start(dst, src).then_inc(att_loaded[l], 16)
        return dict(sync=sync)

    plan, ran = [], []
    for l in range(4):
        plan += [("att", l), ("ffn", l)]
    phases[0] = merge(phases[0], att_load_phase(0 if isinstance(upto, int) else upto[0][1]) if isinstance(upto, int) or upto[0][0] == "att" else ffn_load_phase(upto[0][1]))
    for kind, l in (plan[:upto] if isinstance(upto, int) else upto):
        if kind == "att":
            first = merge(att_scales(l), ffn_load_phase(l))
            while ran:
                first = merge(first, clear(ran.pop()))
            phases.append(first)
            if l == 2:
                phases.append(layer_norm("first"))
                phases.append(layer_norm("second"))
            else:
                phases.append(layer_norm())
            phases.append(attention(l))
            ran.append("att")
        else:
            phases.append(merge(layer_norm(), clear(ran.pop())) if ran else layer_norm())
            phases += feed_forward(l)
            if l != 2:
                ran += ["router", "experts"]
            if l < 3 and (isinstance(upto, int) or ("att", l + 1) in upto):
                phases[-1] = merge(phases[-1], att_load_phase(l + 1))

    stored = sem("stored")

    def store(sp):
        sp.dma_start(out.rearrange("b t d -> t b d"), X[:]).then_inc(stored, 16)
        sp.wait_ge(stored, 16)

    block = ctx.enter_context(nc.Block())

    def run(eng, name):
        for ph in phases:
            if name in ph:
                ph[name](eng)
            meet(eng)

    @block.sync
    def _(sp):
        run(sp, "sync")
        store(sp)

    @block.tensor
    def _(pe):
        run(pe, "tensor")

    @block.scalar
    def _(act):
        run(act, "scalar")

    @block.vector
    def _(dve):
        run(dve, "vector")

    @block.gpsimd
    def _(pool):
        run(pool, "gpsimd")


def merge(a, b):
    out = dict(a)
    for k, f in b.items():
        out[k] = (lambda e, p=a[k], q=f: (p(e), q(e))) if k in a else f
    return out


def bcast_rows(v, n):
    return v.rearrange("(a n) -> a n", a=1).to_broadcast([n, v.shape[0]])


def arrays_of(inputs):
    a = {k: np.asarray(v) for k, v in inputs.items()}
    B = a["x"].shape[0]
    f = {"x": a["x"], "ctx": a["ctx_1024"], "g_xattn": a["g_xattn"], "g_ffn": a["g_ffn"], "L2_gate": a["L2_xattn_gate"]}
    z = np.zeros((128,), np.float32)

    def turned(w):
        return w.reshape(64, 2, 128)[:, ::-1, :].reshape(128, 128)
    for l in (0, 1, 3):
        if l == 3:
            w = a["L3_xattn_in_proj_weight"]
            bb = a["L3_xattn_in_proj_bias"]
            wq, wk, wv, wo = w[0:128], w[128:256], w[256:384], a["L3_xattn_out_w"]
            bq, bk, bv, bo = bb[0:128], bb[128:256], bb[256:384], a["L3_xattn_out_b"]
        else:
            wq, wk, wv, wo = (a[f"L{l}_xattn_W{n}"] for n in "qkvo")
            bq, bk, bv, bo = (a[f"L1_xattn_b{n}"] for n in "qkvo") if l == 1 else (z, z, z, z)
        f[f"L{l}_wq"], f[f"L{l}_wk"], f[f"L{l}_wv"], f[f"L{l}_wo"] = wq.T, wk.T, wv.T, wo.T
        if l == 0:
            f["L0_wq_turn"], f["L0_wk_turn"] = turned(wq).T, turned(wk).T
        f[f"L{l}_cols"] = np.stack([bq, bk, bo], 1)
        f[f"L{l}_bv"] = bv
    f["L2_wq"] = a["L2_xattn_w_q"]
    f["L2_wk"] = a["L2_xattn_w_kv"][:, 0:1024]
    f["L2_wv"] = a["L2_xattn_w_kv"][:, 1024:2048]
    f["L2_wo"] = a["L2_xattn_w_out"].reshape(8, 128, 128).transpose(1, 0, 2).reshape(128, 1024)
    f["L2_cols"] = np.stack([z, z, a["L2_xattn_b_out"], a["L2_xattn_ln_gamma"], a["L2_xattn_ln_beta"]], 1)
    f["F0_up"], f["F0_up2"] = (a[f"L0_ffn_{n}"].transpose(1, 0, 2).reshape(128, 1408) for n in ("w1", "w3"))
    f["F0_down"] = rows_by_tile(a["L0_ffn_w2"].reshape(1408, 128))
    f["F0_router"] = a["L0_ffn_w_router"].T
    up = np.concatenate([a["L1_ffn_shared_up"], a["L1_ffn_routed_up"]], 0)
    down = np.concatenate([a["L1_ffn_shared_down"], a["L1_ffn_routed_down"]], 0)
    f["F1_up"] = up.reshape(1152, 128).T
    f["F1_down"] = rows_by_tile(down.transpose(0, 2, 1).reshape(1152, 128))
    f["F1_router"] = a["L1_ffn_router_w"].T
    f["F2_wr"], f["F2_wk"], f["F2_wv"] = (a[f"L2_ffn_W_{n}"].T for n in "rkv")
    f["F2_mu"] = np.stack([a["L2_ffn_mu_r"], a["L2_ffn_mu_k"]], 1)
    f["F3_up"] = a["L3_ffn_W1"].transpose(1, 0, 2).reshape(128, 4096)
    f["F3_down"] = rows_by_tile(a["L3_ffn_W2"].reshape(4096, 128))
    f["F3_router"], f["F3_br"] = a["L3_ffn_Wr"], a["L3_ffn_br"]
    f["F3_b1"] = a["L3_ffn_b1"].reshape(32, 128).T
    f["F3_b2"] = np.concatenate([np.tile(a["L3_ffn_b2"], (3, 1)), np.zeros((104, 128), np.float32)], 0)
    f.update(shape_constants(B))
    return {k: np.ascontiguousarray(v) for k, v in f.items()}


def rows_by_tile(w):
    return w.reshape(-1, 128, 128).transpose(1, 0, 2).reshape(128, -1)


def kernel(**inputs):
    import concourse.bacc as _bacc
    from concourse.bass_utils import run_bass_kernel_spmd as _run

    nc = _bacc.Bacc("TRN2", target_bir_lowering=False, num_devices=1)
    arrays = {f"in_{k}": v for k, v in arrays_of(inputs).items()}
    A = {k[3:]: nc.dram_tensor(k, v.shape, mybir.dt.from_np(v.dtype), kind="ExternalInput").ap() for k, v in arrays.items()}
    B = inputs["x"].shape[0]
    out = nc.dram_tensor("out_x", (B, S, D), F32, kind="ExternalOutput").ap()
    program(nc, A, out, B)
    r = _run(nc, [arrays], core_ids=[0])
    return r.results[0]["out_x"]
```

```python
from contextlib import ExitStack

import numpy as np

import concourse.bass as bass
from concourse import mybir

F32, BF16, FP16 = mybir.dt.float32, mybir.dt.bfloat16, mybir.dt.float16
ALU = mybir.AluOpType
ACT = mybir.ActivationFunctionType
AX = mybir.AxisListType.X

S = 128
D = 128
H = 16
LN_EPS = 1e-5
MASKED = -1e30
HEAD_DIMS = (8, 8, 64, 8)
W_SCALE, X_SCALE, HID_SCALE = 2.0 ** 8, 2.0 ** 6, 2.0 ** 6


def wait(eng, sem, count):
    if isinstance(count, int) and count <= 0:
        return
    eng.wait_ge(sem, count)


def shape_constants(B):
    c = {}
    c["ident"] = np.eye(128, dtype=np.float32)
    sel = np.zeros((128, 2, 2, 4, 128), np.float32)
    for t, order in enumerate(((0, 0, 1, 1), (0, 1, 0, 1))):
        for j in range(4):
            for cc in range(4):
                for r, part in enumerate(order):
                    for d in range(8):
                        sel[8 * (4 * j + cc) + d, t, part, cc, 32 * j + 8 * r + d] = 1.0
    c["stack_sel"] = sel.reshape(128, -1).astype(np.float16)
    rows = np.zeros((128, 16, 128), np.float32)
    for i in range(16):
        for r in (i, 16 + i, 64 + i, 80 + i):
            rows[r, i, :] = 1.0
    c["max_rows"] = rows.reshape(128, -1)
    q, k = np.meshgrid(np.arange(S), np.arange(S), indexing="ij")
    hidden = np.where(k > q, MASKED, 0.0).astype(np.float32)
    c["causal"] = np.concatenate([hidden, hidden.T], 1)
    freq = (1.0 / np.float32(10000.0) ** (np.arange(0, 8, 2, dtype=np.float32) / np.float32(8))).astype(np.float32)
    ang = np.arange(S, dtype=np.float32)[:, None] * freq[None, :]
    cos, sin = np.cos(ang).astype(np.float32), np.sin(ang).astype(np.float32)
    i = (np.arange(D) % 8) // 2
    sign = np.where(np.arange(D) % 2 == 0, -1.0, 1.0).astype(np.float32)
    c["rope"] = np.concatenate([cos[:, i].T, sin[:, i].T * sign[:, None]], 1)
    c["zero_cols"] = np.zeros((128, 4), np.float32)
    c["zero_row"] = np.zeros((1, 128), np.float32)
    c["gate_sel0"] = gate_rows(8, [[((128 * t + r) // 176, r) for r in range(128)] for t in range(11)], 11,
                               HID_SCALE / (W_SCALE * X_SCALE))
    c["gate_sel1"] = gate_rows(16, [[(2 * t + r // 64, r) for r in range(128)] for t in range(8)], 8, HID_SCALE)
    c["gate_sel3"] = gate_rows(8, [[(e, r) for r in range(128)] for e in range(8)], 8, HID_SCALE)
    return c


def gate_rows(E, tiles, n, value):
    g = np.zeros((128, n, 128), np.float32)
    for t, pairs in enumerate(tiles):
        for e, r in pairs:
            for part in range(3):
                g[part * E + e, t, r] = value
    return g.reshape(128, n * 128).astype(mybir.dt.np(BF16))


class Region:

    def __init__(self, tile, size):
        self.tile, self.size, self.at = tile, size, 0

    def restart(self, at=0):
        self.at = at

    def take(self, dims, dtype, rows=128):
        width = 4 if dtype == F32 else 2
        n = int(np.prod(dims)) * width
        n = (n + 3) // 4 * 4
        assert self.at + n <= self.size, (self.at, n, self.size)
        ap = self.tile[0:rows, self.at // 4:(self.at + n) // 4]
        self.at += (n + 31) // 32 * 32
        if dtype != F32:
            ap = ap.bitcast(dtype)
        if len(dims) > 1:
            names = "abcdef"[:len(dims)]
            ap = ap.rearrange(f"p ({' '.join(names)}) -> p {' '.join(names)}",
                              **{x: d for x, d in zip(names[1:], dims[1:])})
        return ap


def program(nc, A, out, B, upto=8):
    ctx = ExitStack()
    with ctx:
        body(nc, A, out, B, upto, ctx)


def body(nc, A, out, B, upto, ctx):
    def sb(name, shape, dt):
        return ctx.enter_context(nc.sbuf_tensor(name, shape, dt))

    def sem(name):
        return ctx.enter_context(nc.semaphore(name))

    shared = {}

    def phase_sem(kind, name):
        if (kind, name) not in shared:
            shared[kind, name] = sem(f"{kind}_{name}")
        return shared[kind, name]

    def clear(kind):
        def sync(sp):
            for (k, _), handle in shared.items():
                if k == kind:
                    sp.sem_clear(handle)
        return dict(sync=sync)

    NT = B * S

    X = sb("X", [128, B, D], F32)
    ctxT = sb("ctxT", [128, NT], F32)
    xnT = sb("xnT", [128, NT], F32)
    x16 = xnT[:].bitcast(FP16).rearrange("p (a t) -> p a t", a=2)
    ident = sb("ident_f", [128, 128], F32)
    ident_b = sb("ident_b", [128, 128], BF16)
    stack_sel = sb("stack_sel", [128, 2, 2, 4, 128], FP16)
    max_rows = sb("max_rows", [128, 16, 128], BF16)
    causal = sb("causal", [128, 2, 128], BF16)
    rope = sb("rope", [128, 2, 128], F32)
    gates = sb("gates", [128, 12], F32)
    stats = sb("stats", [128, B, 6], F32)
    stats2 = sb("stats2", [128, B, 6], F32)
    ln_small = sb("ln_small", [128, 10, B], F32)
    minus_half = sb("minus_half", [128, B], F32)
    cols = sb("cols", [128, 4, 8], F32)
    bv_row = sb("bv_row", [128, 128], F32)
    gate_sel = sb("gate_sel", [128, 11 * 128], BF16)
    gateT = sb("gateT", [128, NT], BF16)
    b2_rows = sb("b2_rows", [128, 128], F32)
    b2_rest = sb("b2_rest", [128, 128], F32)
    b2_part = sb("b2_part", [128, 3, 128], BF16)
    br_row = sb("br_row", [128, 8], F32)
    y_scale = sb("y_scale", [128, 1], F32)
    W_att = Region(sb("W_att", [128, 4096], F32), 4096 * 4)
    W_ffn = Region(sb("W_ffn", [128, 8320], F32), 8320 * 4)
    STK = 12480
    stacks = Region(sb("stacks", [128, STK], F32), STK * 4)
    WRK = 9240
    work = Region(sb("work", [128, WRK], F32), WRK * 4)
    PS = [ctx.enter_context(nc.psum_tensor(f"bank{i}", [128, 512], F32)) for i in range(8)]

    phase_done = sem("phase_done")
    meets = {}

    def meet(eng):
        n = meets[id(eng)] = meets.get(id(eng), 0) + 1
        eng.drain().then_inc(phase_done, 1)
        eng.wait_ge(phase_done, 5 * n)

    load_x = sem("load_x")
    load_c = sem("load_c")
    load_const = sem("load_const")

    setup_ready = sem("setup_ready")
    ctx_turned = sem("ctx_turned")
    ctx_stored = sem("ctx_stored")
    stats_sem = sem("stats_sem")
    work.restart()
    ctx_in = stacks.tile[:, 0:B * D]

    def setup_sync(sp):
        sp.dma_start(ctx_in.rearrange("p (b d) -> p b d", d=D), A["ctx"].rearrange("b t d -> t b d")).then_inc(load_c, 16)
        sp.dma_start(X[:], A["x"].rearrange("b t d -> t b d")).then_inc(load_x, 16)
        for dst, name in ((ident[:], "ident"), (rope[:].rearrange("p a t -> p (a t)"), "rope"),
                          (stack_sel[:].rearrange("p a b c t -> p (a b c t)"), "stack_sel"),
                          (const_f[:, 0:2048], "max_rows"), (const_f[:, 2048:2304], "causal")):
            sp.dma_start(dst, A[name]).then_inc(load_const, 16)
        for i, name in enumerate(("g_xattn", "g_ffn", "L2_gate")):
            n = A[name].shape[0]
            sp.dma_start(gates_in[:, 4 * i:4 * i + n], bcast_rows(A[name], 128)).then_inc(load_const, 16)

    const_f = work.take([2304], F32)
    gates_in = work.take([12], F32)
    N_CONST = 8 * 16

    def setup_vector(dve):
        dve.memset(minus_half[:], -0.5).then_inc(setup_ready, 1)
        dve.memset(gates_in[:, 9:12], 0.0).then_inc(setup_ready, 1)
        dve.memset(gateT[:], 0.0)
        dve.wait_ge(load_const, N_CONST)
        dve.tensor_copy(ident_b[:], ident[:]).then_inc(setup_ready, 1)
        dve.tensor_copy(max_rows[:].rearrange("p a t -> p (a t)"), const_f[:, 0:2048]).then_inc(setup_ready, 1)
        dve.tensor_copy(causal[:].rearrange("p a t -> p (a t)"), const_f[:, 2048:2304]).then_inc(setup_ready, 1)
        dve.wait_ge(load_x, 16)
        for b in range(B):
            dve.bn_stats(stats[:, b, :], X[:, b, :])

    def setup_scalar(act):
        act.wait_ge(load_const, N_CONST)
        act.wait_ge(setup_ready, 2)
        act.activation(gates[:], gates_in, ACT.Tanh)
        for i in range(B // 4):
            act.wait_ge(ctx_turned, i + 1)
            act.copy(ctxT[:, 512 * i:512 * i + 512], PS[i % 4][:]).then_inc(ctx_stored, 1)

    def setup_tensor(pe):
        pe.wait_ge(load_c, 16)
        pe.wait_ge(load_const, N_CONST)
        for i in range(B // 4):
            wait(pe, ctx_stored, i - 3)
            for k in range(4):
                b = 4 * i + k
                last = pe.transpose(PS[i % 4][:, 128 * k:128 * k + 128], ctx_in[:, b * D:(b + 1) * D], ident[:])
            last.then_inc(ctx_turned, 1)

    ln_dve = sem("ln_dve")
    ln_pool = sem("ln_pool")
    ln_turned = sem("ln_turned")
    ln_stored = sem("ln_stored")
    ln_low = sem("ln_low")
    ln_act = sem("ln_act")
    ln_pow = sem("ln_pow")
    NG4 = B // 4
    ln_uses = {"n": 0}
    STEPS = 5

    def layer_norm(second=None, halves=False):
        use = ln_uses["n"]
        ln_uses["n"] += 1
        work.restart()
        xn = work.take([2, 4, D], F32)
        xn1 = stacks.tile[:, 0:B * D].rearrange("p (b d) -> p b d", d=D)
        src = xn1 if second == "second" else X[:]
        st = stats2 if second == "second" else stats
        keep = second == "first"
        base_v = use * (STEPS + NG4)
        t = [ln_small[:, i, :] for i in range(10)]
        mean, minus_mean, rstd, shift = t[7], t[8], t[6], t[9]
        gamma, beta = cols[:, 2, 4:5], cols[:, 2, 5:6]
        group0 = use * NG4
        turn0 = ln_uses.get("turned", 0)
        low0 = ln_uses.get("low", 0)
        if not keep:
            ln_uses["turned"] = turn0 + NG4
        if halves:
            ln_uses["low"] = low0 + NG4
        BY_DVE = 2

        def place(g, par, k):
            b = g * 4 + k
            return b, (xn1[:, bass.ds(b, 1), :] if keep else xn[:, par, k:k + 1, :])

        def vector(dve):
            m0, v0, m1, v1 = st[:, :, 1], st[:, :, 2], st[:, :, 4], st[:, :, 5]
            dve.tensor_tensor(t[0], m0, m1, ALU.subtract)
            dve.tensor_tensor(t[1], m0, m1, ALU.add)
            dve.tensor_tensor(t[2], v0, v1, ALU.add).then_inc(ln_dve, 1)
            dve.wait_ge(ln_dve, base_v + 1)
            dve.tensor_tensor(t[3], t[0], t[0], ALU.mult).then_inc(ln_dve, 1)
            dve.wait_ge(ln_dve, base_v + 2)
            dve.scalar_tensor_tensor(t[4], t[3], 32.0, t[2], ALU.mult, ALU.add).then_inc(ln_dve, 1)
            dve.wait_ge(ln_dve, base_v + 3)
            dve.tensor_scalar(t[5], t[4], 1.0 / D, LN_EPS, ALU.mult, ALU.add)
            dve.tensor_scalar(minus_mean, t[1], -0.5, None, ALU.mult).then_inc(ln_dve, 1)
            dve.tensor_scalar(mean, t[1], 0.5, None, ALU.mult).then_inc(ln_dve, 1)
            dve.wait_ge(ln_dve, base_v + STEPS)

            def group(g, par):
                dve.wait_ge(ln_pool, group0 + g + 1)
                if not keep:
                    wait(dve, ln_turned, turn0 + g - 1)
                for k in range(BY_DVE):
                    b, dst = place(g, par, k)
                    last = dve.tensor_scalar(dst, src[:, bass.ds(b, 1), :], mean[:, bass.ds(b, 1)],
                                             rstd[:, bass.ds(b, 1)], ALU.subtract, ALU.mult)
                last.then_inc(ln_dve, 1)
                if keep:
                    dve.wait_ge(ln_dve, base_v + STEPS + g + 1)
                    dve.wait_ge(ln_act, group0 + g + 1)
                    for k in range(4):
                        b = g * 4 + k
                        dve.bn_stats(stats2[:, bass.ds(b, 1), :], xn1[:, bass.ds(b, 1), :])

            def low(g, par):
                if halves:
                    dve.wait_ge(ln_stored, turn0 + g + 1)
                    dve.scalar_tensor_tensor(x16[:, 1, bass.ds(g * 512, 512)], PS[par][:], X_SCALE, x16[:, 0, bass.ds(g * 512, 512)],
                                             ALU.mult, ALU.subtract).then_inc(ln_low, 1)
            trailing(dve, group, low)

        def pool(pl):
            pl.wait_ge(ln_dve, base_v + 4)
            for g in range(NG4):
                some = slice(4 * g, 4 * g + 4)
                pl.tensor_tensor(rstd[:, some], t[5][:, some], minus_half[:, some], ALU.pow).then_inc(ln_pow, 1)
                pl.wait_ge(ln_pow, group0 + g + 1)
                pl.tensor_tensor(shift[:, some], minus_mean[:, some], rstd[:, some], ALU.mult).then_inc(ln_pool, 1)

        def tensor(pe):
            if keep:
                return

            def group(g, par):
                pe.wait_ge(ln_dve, base_v + STEPS + g + 1)
                pe.wait_ge(ln_act, group0 + g + 1)
                wait(pe, ln_stored, turn0 + g - 1)
                if halves:
                    wait(pe, ln_low, low0 + g - 1)
                for k in range(4):
                    last = pe.transpose(PS[par][:, 128 * k:128 * k + 128], xn[:, par, k, :], ident[:])
                last.then_inc(ln_turned, 1)
            trailing(pe, group, lambda g, par: None)

        def scalar(act):
            def group(g, par):
                act.wait_ge(ln_pool, group0 + g + 1)
                if not keep:
                    wait(act, ln_turned, turn0 + g - 1)
                for k in range(BY_DVE, 4):
                    b, dst = place(g, par, k)
                    last = act.activation(dst, src[:, bass.ds(b, 1), :], ACT.Identity, scale=rstd[:, bass.ds(b, 1)],
                                          bias=shift[:, bass.ds(b, 1)])
                last.then_inc(ln_act, 1)

            def store(g, par):
                if keep:
                    return
                act.wait_ge(ln_turned, turn0 + g + 1)
                dst = xnT[:, bass.ds(g * 512, 512)]
                if halves:
                    act.activation(x16[:, 0, bass.ds(g * 512, 512)], PS[par][:], ACT.Copy, scale=X_SCALE).then_inc(ln_stored, 1)
                elif second == "second":
                    act.activation(dst, PS[par][:], ACT.Identity, scale=gamma, bias=beta).then_inc(ln_stored, 1)
                else:
                    act.copy(dst, PS[par][:]).then_inc(ln_stored, 1)
            trailing(act, group, store)

        return dict(vector=vector, gpsimd=pool, tensor=tensor, scalar=scalar)

    def trailing(eng, group, after):
        group(0, 0)
        group(1, 1)
        after(0, 0)
        if NG4 > 2:
            with eng.Fori(1, NG4 // 2) as r:
                group(2 * r, 0)
                after(2 * r - 1, 1)
                group(2 * r + 1, 1)
                after(2 * r, 0)
        after(NG4 - 1, 1)

    def attention(l):
        dh = HEAD_DIMS[l]
        wide = dh == 64
        GB = 2 if wide else 4
        T = GB * S
        NG = B // GB
        scale = float(dh) ** -0.5
        rotary, masked = l == 0, l == 0
        inner = H * dh
        nchunk = inner // 128

        W_att.restart()
        wq = W_att.take([inner], F32)
        wk = W_att.take([inner], F32)
        wv = W_att.take([inner], F32)
        wo = W_att.take([nchunk, D], F32)
        if wide:
            w16 = att_halves()
        if rotary:
            wq_turn = W_att.take([D], F32)
            wk_turn = W_att.take([D], F32)
        stacks.restart()
        if wide:
            Q = [stacks.take([2, 8, T], FP16) for _ in range(2)]
            K = [stacks.take([2, 8, T], FP16) for _ in range(2)]
        else:
            Q = [stacks.take([4, T], FP16) for _ in range(2)]
            K = [stacks.take([4, 4, T], FP16) for _ in range(2)]
            K_stack = stacks.take([4, T], FP16)
        V = [stacks.take([GB, 2, H, dh + 1], FP16) for _ in range(2)]
        work.restart()
        P32 = work.take([4, 512], F32)
        Phi = work.take([4, 512], FP16)
        Plo = work.take([4, 512], FP16)
        o32 = work.take([2, inner], F32)
        y32 = work.take([T], F32)
        if wide:
            c16 = work.take([2, T], FP16)
            x16g = work.take([2, T], FP16)
        else:
            cst = work.take([GB, S], F32)
        m16 = work.take([2, 16], F32)
        mcat = work.take([128], BF16)
        mT = work.take([2, 128], BF16)
        rec = work.take([2, 16], F32)
        if wide:
            oT = stacks_tail_take(T)
        else:
            oT = [work.take([1, T], F32) for _ in range(2)]
            k32 = work.take([T], F32)
            q32 = work.take([T], F32)
            v32 = work.take([T], F32)
            khl = work.take([2, T], FP16)
            qhl = work.take([2, T], FP16)
            if rotary:
                turn1 = W_att.take([T], F32)
                turn2 = W_att.take([T], F32)

        names = ["s_ready", "max_done", "m_split", "m_chain", "mt_ready", "mt_stored", "st_ready", "exp_done",
                 "plo_dve", "plo_pool", "pv_done", "rec_done", "o_done", "ot_ready", "ot_stored", "yt_ready",
                 "y_stored", "yb_ready", "x_done", "ctx_staged", "ones_set"]
        if wide:
            names += ["kq_ready", "kq_hi", "kq_lo", "v_ready", "hi_v", "lo_v", "in_hi", "in_lo", "ot_lo"]
        else:
            names += ["kp_ready", "qp_ready", "k32_done", "q32_done", "v_ready", "v32_done", "hi_k", "hi_q", "hi_v",
                      "lo_kq", "lo_v", "selk_ready", "selk_stored_a", "selk_stored_v", "zeros_dve", "zeros_pool",
                      "k_spread", "selq_ready", "selq_stored_a", "selq_stored_v", "turn_done"]
        s = {n: phase_sem("att", n) for n in names}
        w_loaded = att_loaded[l]
        w_count = att_loads(l)[1]

        def heads(quad):
            if wide:
                u, j = divmod(quad, 2)
                return [(2 * (4 * u + k) + j, slice(64 * j, 64 * j + 64), 4 * u + k, 4 * u + k) for k in range(4)]
            return [(4 * j + quad, slice(0, 128), j, 4 * quad + j) for j in range(4)]

        if wide:
            slots = {(0, 0): ["v0"], (0, 1): ["v1"], (0, 2): ["v2"], (0, 3): ["yt", "v3"],
                     (1, 0): ["k0", "q0"], (1, 1): ["k1", "q1"], (1, 2): ["k2", "q2", "yb"], (1, 3): ["k3", "q3"]}
            YT = 3
        else:
            slots = {(0, 0): ["kp"] + ["kp2"] * rotary, (0, 1): ["qp"] + ["qp2"] * rotary, (0, 2): ["v"], (0, 3): [],
                     (1, 0): ["selk0"], (1, 1): ["selk1"], (1, 2): ["selk2"], (1, 3): ["selk3"],
                     (2, 0): ["selq0"], (2, 1): ["selq1"], (2, 2): ["selq2"], (2, 3): ["selq3"],
                     (3, 0): ["yt"], (3, 1): [], (3, 2): ["yb"], (3, 3): []}
            YT = 2
        turns = {0: [0], 2: [1]} if wide else {2: [0]}
        KQ_JOBS = ["k0", "q0", "k1", "q1", "k2", "q2", "k3", "q3"]
        order = []
        for k in range(GB):
            for q in range(4):
                order += [f"mt{k}"] * (q == 1) + [f"ot{k}_{i}" for i in turns.get(q, [])] + slots[k, q]
        banks = {job: 6 + i % 2 for i, job in enumerate(order)}
        NOT = nchunk // 4 or 1

        def ok(index, n):
            return not isinstance(index, int) or 0 <= index < n

        def rounds(eng, iteration):
            lead = 4
            for g in range(lead):
                iteration(g, g % 2)
            if NG > lead:
                with eng.Fori(lead // 2, NG // 2) as r:
                    iteration(2 * r, 0)
                    iteration(2 * r + 1, 1)
            for g in range(NG, NG + (3 if wide else 2)):
                iteration(g, g % 2)

        def stage(g, gp, k, q):
            b0 = GB * (g - 1) + k
            return b0, b0 - 1, b0 - 2, b0 - 3, (b0 - 2, q + 2, 2) if q < 2 else (b0 - 1, q - 2, 1)

        def place(g, gp, k, back):
            return ((1 - gp) if (k - back) // GB % 2 == 0 else gp), (k - back) % GB, (k - back) % 2

        def tensor(pe):
            def halves_product(dst, a, b, start=True, stop=True):
                for i, (x, y) in enumerate(((0, 0), (0, 1), (1, 0))):
                    last = pe.matmul(dst, a(x), b(y), start=(start and i == 0), stop=(stop and i == 2))
                return last

            pe.wait_ge(w_loaded, w_count)
            freed_by = {}
            for job in order:
                if job.startswith("mt"):
                    k = int(job[2])
                    freed_by[job] = ("mt_stored", lambda g, k=k: (g - 1) * GB + k)
                elif job.startswith("ot"):
                    k, i = int(job[2]), int(job[4])
                    freed_by[job] = ("ot_lo" if wide else "ot_stored", lambda g, k=k, i=i: ((g - 1) * GB + k - 3) * NOT + i + 1)
                elif job == "yt":
                    freed_by[job] = ("y_stored", lambda g: g - YT + 1)
                elif job == "yb":
                    freed_by[job] = ("x_done", lambda g: g - YT + 1)
                elif wide and job[0] == "v":
                    freed_by[job] = ("lo_v", lambda g, n=int(job[1]): 4 * (g - 1) + n + 1)
                elif wide:
                    freed_by[job] = ("kq_lo", lambda g, n=KQ_JOBS.index(job): 8 * g + n + 1)
                elif job in ("kp", "kp2"):
                    freed_by[job] = ("k32_done", lambda g: g + 1)
                elif job in ("qp", "qp2"):
                    freed_by[job] = ("q32_done", lambda g: g + 1)
                elif job == "v":
                    freed_by[job] = ("v32_done", lambda g: g + 1)
                else:
                    c = int(job[4])
                    kind = "selk" if job[3] == "k" else "selq"
                    freed_by[job] = (f"{kind}_stored_{'av'[c % 2]}", lambda g, c=c: 2 * g + c // 2 + 1)
            last_in = {6: None, 7: None}

            def take(job, g):
                bank = banks[job]
                if last_in[bank] is not None:
                    name, count = last_in[bank]
                    wait(pe, s[name], count(g))
                last_in[bank] = freed_by[job]
                return PS[bank]

            def age():
                for b, v in last_in.items():
                    if v is not None:
                        name, count = v
                        last_in[b] = (name, lambda g, count=count: count(g - 1))

            def job_run(job, g, par):
                if job == "yt":
                    a = g - YT
                    if ok(a, NG):
                        ps = take(job, g)
                        if wide:
                            pe.wait_ge(s["ot_lo"], (a + 1) * GB * NOT)
                            for c in range(nchunk):
                                last = halves_product(ps[:, 0:T], lambda x: w16["wo"][:, x, 128 * c:128 * c + 128],
                                                      lambda y: oT[:, y, c, :], start=(c == 0), stop=(c == nchunk - 1))
                        else:
                            pe.wait_ge(s["ot_stored"], (a + 1) * GB * NOT)
                            last = pe.matmul(ps[:], wo[:, 0, :], oT[par][:, 0, :], start=True, stop=True)
                        last.then_inc(s["yt_ready"], 1)
                elif job == "yb":
                    a = g - YT
                    if ok(a, NG):
                        ps = take(job, g)
                        pe.wait_ge(s["y_stored"], a + 1)
                        for k in range(GB):
                            last = pe.transpose(ps[:, 128 * k:128 * k + 128], y32[:, 128 * k:128 * k + 128], ident[:])
                        last.then_inc(s["yb_ready"], 1)
                elif wide and job[0] == "v":
                    if ok(g - 1, NG):
                        ps = take(job, g)
                        i = int(job[1])
                        k, cols_ = i // 2, slice(512 * (i % 2), 512 * (i % 2) + 512)
                        halves_product(ps[:], lambda x: c16[:, x, 128 * k:128 * k + 128],
                                       lambda y: w16["wv"][:, y, cols_]).then_inc(s["v_ready"], 1)
                elif not ok(g, NG):
                    return
                elif wide:
                    ps = take(job, g)
                    i = int(job[1])
                    w, src = (w16["wk"], c16) if job[0] == "k" else (w16["wq"], x16g)
                    pe.wait_ge(s["in_lo"], 2 * g + 2)
                    for j in range(2):
                        t = 2 * i + j
                        last = halves_product(ps[:, T * j:T * j + T], lambda x: w[:, x, 128 * t:128 * t + 128], lambda y: src[:, y, :])
                    last.then_inc(s["kq_ready"], 1)
                elif job in ("kp", "kp2", "qp", "qp2"):
                    ps = take(job, g)
                    w = {"kp": wk, "qp": wq}.get(job)
                    if w is None:
                        w = wk_turn if job == "kp2" else wq_turn
                    src = ctxT if job[0] == "k" else xnT
                    pe.matmul(ps[:], w, src[:, bass.ds(g * T, T)], start=True, stop=True).then_inc(s[f"{job[0]}p_ready"], 1)
                elif job == "v":
                    ps = take(job, g)
                    pe.wait_ge(s["ctx_staged"], g + 1)
                    for k in range(GB):
                        last = pe.matmul(ps[:, 128 * k:128 * k + 128], cst[:, k, :], wv, start=True, stop=True)
                    last.then_inc(s["v_ready"], 1)
                else:
                    ps = take(job, g)
                    c, kind = int(job[4]), job[3]
                    if c == 0:
                        pe.wait_ge(s[f"hi_{kind}"], g + 1)
                        pe.wait_ge(s["lo_kq"], 2 * g + (1 if kind == "k" else 2))
                    src, t = (khl, 1) if kind == "k" else (qhl, 0)
                    pe.matmul(ps[:], stack_sel[:, t, 0, c, :], src[:, 0, :], start=True, stop=False)
                    pe.matmul(ps[:], stack_sel[:, t, 1, c, :], src[:, 1, :], start=False, stop=True).then_inc(s[f"sel{kind}_ready"], 1)

            def scores(b, quad, par, tok):
                ps = PS[quad % 2]
                wait(pe, s["max_done"], 4 * b + quad - 1)
                if masked:
                    pe.matmul(ps[:].rearrange("p (h k) -> p h k", h=4), ident_b[:],
                              causal[:, 0:1, :].to_broadcast([128, 4, 128]), start=True, stop=False, skip_group_check=True)
                if wide:
                    for k, (_, rows, block, _) in enumerate(heads(quad)):
                        for i, (a, c) in enumerate(((0, 0), (0, 1), (1, 0))):
                            last = pe.matmul(ps[:, 128 * k:128 * k + 128], Q[par][rows, a, block, tok], K[par][rows, c, block, tok],
                                             start=(i == 0), stop=(i == 2), skip_group_check=True)
                else:
                    last = pe.matmul(ps[:].rearrange("p (h k) -> p h k", h=4), Q[par][:, quad, tok], K[par][:, quad, :, tok],
                                     start=not masked, stop=True, skip_group_check=True)
                last.then_inc(s["s_ready"], 1)

            def scoresT(b, quad, par, tok, bp):
                ps = PS[2 + quad % 2]
                wait(pe, s["exp_done"], 4 * b + quad - 1)
                if quad == 0:
                    pe.wait_ge(s["mt_stored"], b + 1)
                if masked:
                    pe.matmul(ps[:].rearrange("p (h k) -> p h k", h=4), ident_b[:],
                              causal[:, 1:2, :].to_broadcast([128, 4, 128]), start=True, stop=False, skip_group_check=True)
                for k, (h, rows, block, pattern) in enumerate(heads(quad)):
                    dst = ps[:, 128 * k:128 * k + 128]
                    if wide:
                        for i, (a, c) in enumerate(((0, 0), (0, 1), (1, 0))):
                            pe.matmul(dst, K[par][rows, a, block, tok], Q[par][rows, c, block, tok], start=(i == 0), stop=False, skip_group_check=True)
                    else:
                        pe.matmul(dst, K[par][:, quad, block, tok], Q[par][:, quad, tok], start=not masked, stop=False, skip_group_check=True)
                    last = pe.matmul(dst, max_rows[rows, pattern, :], mT[rows, bp, :], start=False, stop=True, skip_group_check=True)
                last.then_inc(s["st_ready"], 1)

            def values(b, quad, par, kk, bp):
                pe.wait_ge(s["exp_done"], 4 * b + quad + 1)
                pe.wait_ge(s["plo_pool" if quad % 2 else "plo_dve"], 2 * b + quad // 2 + 1)
                if wide:
                    ps = PS[4 + quad % 2]
                    wait(pe, s["o_done"], 4 * b + quad - 1)
                else:
                    ps = PS[4 + bp]
                    if quad == 0:
                        wait(pe, s["o_done"], b - 1)
                for k, (h, _, _, _) in enumerate(heads(quad)):
                    n = (k if wide else h) * (dh + 1)
                    dst = ps[:, n:n + dh + 1]
                    hi, lo = Phi[:, quad, 128 * k:128 * k + 128], Plo[:, quad, 128 * k:128 * k + 128]
                    pe.matmul(dst, hi, V[par][:, kk, 0, h, :], start=True, stop=False)
                    pe.matmul(dst, hi, V[par][:, kk, 1, h, :], start=False, stop=False)
                    last = pe.matmul(dst, lo, V[par][:, kk, 0, h, :], start=False, stop=True)
                last.then_inc(s["pv_done"], 1)

            def iteration(g, gp):
                if not (isinstance(g, int) and g == 0):
                    age()
                for k in range(GB):
                    for q in range(4):
                        b0, b1, b2, b3, (bt, quad, back) = stage(g, gp, k, q)
                        if ok(b0, B):
                            par, kk, _ = place(g, gp, k, 0)
                            if k == 0 and q == 0:
                                pe.wait_ge(s["ones_set"], 1)
                                if wide:
                                    pe.wait_ge(s["kq_lo"], 8 * (g - 1) + 4)
                                else:
                                    pe.wait_ge(s["k_spread"], 64 * g)
                                    pe.wait_ge(s["selq_stored_a"], 2 * g)
                                    pe.wait_ge(s["selq_stored_v"], 2 * g)
                            if wide and k == 0 and q == 2:
                                pe.wait_ge(s["kq_lo"], 8 * g)
                            scores(b0, q, par, slice(128 * kk, 128 * kk + 128))
                        if q == 1 and ok(b1, B):
                            ps = take(f"mt{k}", g)
                            pe.wait_ge(s["m_split"], b1 + 1)
                            pe.transpose(ps[:, 0:64].bitcast(BF16), mcat, ident_b[:]).then_inc(s["mt_ready"], 1)
                        if ok(b3, B):
                            for i in turns.get(q, []):
                                pe.wait_ge(s["o_done"], 4 * b3 + 2 * i + 2 if wide else b3 + 1)
                                ps = take(f"ot{k}_{i}", g)
                                for c in range(min(4, nchunk)):
                                    src = o32[:, (k - 3) % 2, 128 * (4 * i + c):128 * (4 * i + c) + 128]
                                    last = pe.transpose(ps[:, 128 * c:128 * c + 128], src, ident[:])
                                last.then_inc(s["ot_ready"], 1)
                        if ok(bt, B):
                            par, kk, bp = place(g, gp, k, back)
                            scoresT(bt, quad, par, slice(128 * kk, 128 * kk + 128), bp)
                        for job in slots[k, q]: job_run(job, g, gp)
                        if ok(b2, B):
                            par, kk, bp = place(g, gp, k, 2)
                            if kk == 0 and q == 0:
                                n = g if k >= 2 else g - 1
                                pe.wait_ge(s["hi_v"], 4 * n if wide else n)
                                pe.wait_ge(s["lo_v"], 4 * n if wide else n)
                            values(b2, q, par, kk, bp)
            rounds(pe, iteration)

        def scalar(act):
            def exps(b, quad):
                ps = PS[2 + quad % 2]
                act.wait_ge(s["st_ready"], 4 * b + quad + 1)
                wait(act, s["pv_done"], 4 * b + quad - 3)
                wait(act, s["plo_pool" if quad % 2 else "plo_dve"], 2 * b + quad // 2 - 1)
                act.activation(Phi[:, quad, :], ps[:], ACT.Exp, scale=scale)
                act.activation(P32[:, quad, :], ps[:], ACT.Exp, scale=scale).then_inc(s["exp_done"], 1)

            def job_run(job, g, gp):
                ps = PS[banks[job]]
                if job == "yt":
                    a = g - YT
                    if ok(a, NG):
                        act.wait_ge(s["yt_ready"], a + 1)
                        wait(act, s["yb_ready"], a)
                        act.activation(y32, ps[:, 0:T], ACT.Identity, scale=cols[:, l, 6:7], bias=cols[:, l, 3:4]).then_inc(s["y_stored"], 1)
                elif wide and job[0] == "v":
                    if ok(g - 1, NG):
                        n = int(job[1])
                        act.wait_ge(s["v_ready"], 4 * (g - 1) + n + 1)
                        wait(act, s["pv_done"], 4 * GB * (g - 2))
                        hi_dst, _, src = wide_place(job, 1 - gp)
                        act.activation(hi_dst, src, ACT.Copy, scale=1.0 / W_SCALE).then_inc(s["hi_v"], 1)
                elif job == "yb" or not ok(g, NG):
                    return
                elif wide:
                    n = KQ_JOBS.index(job)
                    act.wait_ge(s["kq_ready"], 8 * g + n + 1)
                    wait(act, s["st_ready"], 4 * GB * (g - 1) - (2 if n < 4 else 0))
                    hi_dst, _, src = wide_place(job, gp)
                    act.activation(hi_dst, src, ACT.Copy, scale=1.0 / W_SCALE).then_inc(s["kq_hi"], 1)
                elif job in ("kp", "qp") and not rotary:
                    kind = job[0]
                    dst, col = (k32, 1) if kind == "k" else (q32, 0)
                    act.wait_ge(s[f"{kind}p_ready"], g + 1)
                    wait(act, s["lo_kq"], 2 * (g - 1) + (1 if kind == "k" else 2))
                    act.activation(dst, ps[:], ACT.Identity, bias=cols[:, l, col:col + 1]).then_inc(s[f"{kind}32_done"], 1)
                elif job[:3] == "sel" and int(job[4]) % 2 == 0:
                    kind, c = job[3], int(job[4])
                    act.wait_ge(s[f"sel{kind}_ready"], 4 * g + c + 1)
                    if c == 0 and kind == "k":
                        wait(act, s["k_spread"], 64 * g)
                    if c == 0 and kind == "q":
                        wait(act, s["st_ready"], 16 * (g - 1))
                    act.copy((K_stack if kind == "k" else Q[gp])[:, c, :], ps[:]).then_inc(s[f"sel{kind}_stored_a"], 1)

            def iteration(g, gp):
                for k in range(GB):
                    for q in range(4):
                        b0, b1, b2, b3, (bt, quad, back) = stage(g, gp, k, q)
                        if not wide and k == 0 and q == 0 and ok(g, NG):
                            wait(act, s["v_ready"], g)
                            act.copy(cst.rearrange("p a b -> p (a b)"), ctxT[:, bass.ds(g * T, T)]).then_inc(s["ctx_staged"], 1)
                        if q == 1 and ok(b1, B):
                            act.wait_ge(s["mt_ready"], b1 + 1)
                            wait(act, s["st_ready"], 4 * (b1 - 1))
                            act.copy(mT[:, (k - 1) % 2, :], PS[banks[f"mt{k}"]][:, 0:64].bitcast(BF16)).then_inc(s["mt_stored"], 1)
                        if ok(b3, B):
                            par, k3, _ = place(g, gp, k, 3)
                            for i in turns.get(q, []):
                                act.wait_ge(s["ot_ready"], b3 * NOT + i + 1)
                                n = min(4, nchunk)
                                src = PS[banks[f"ot{k}_{i}"]][:, 0:128 * n].rearrange("p (c t) -> p c t", c=n)
                                if k3 == 0 and i == 0:
                                    wait(act, s["yt_ready"], g - 2)
                                dst = oT[:, 0] if wide else oT[par]
                                dst = dst[:, n * i:n * i + n, 128 * k3:128 * k3 + 128]
                                act.copy(dst, src).then_inc(s["ot_stored"], 1)
                        if ok(bt, B): exps(bt, quad)
                        for job in slots[k, q]: job_run(job, g, gp)
                        if wide and k == 0 and q == 3 and ok(g, NG):
                            wait(act, s["v_ready"], 4 * g)
                            wait(act, s["kq_ready"], 8 * g)
                            for dst, src in ((c16, ctxT), (x16g, xnT)):
                                act.copy(dst[:, 0, :], src[:, bass.ds(g * T, T)]).then_inc(s["in_hi"], 1)
                        if not wide and ok(g, NG):
                            if k == 0 and q in (1, 2):
                                kind, x32, hl, n = (("k", k32, khl, 1), ("q", q32, qhl, 2))[q - 1]
                                act.wait_ge(s[f"{kind}32_done"], g + 1)
                                wait(act, s[f"sel{kind}_ready"], 4 * g)
                                wait(act, s["lo_kq"], 2 * (g - 1) + n)
                                act.copy(hl[:, 0, :], x32).then_inc(s[f"hi_{kind}"], 1)
                            if k == 2 and q == 1:
                                act.wait_ge(s["v32_done"], g + 1)
                                wait(act, s["pv_done"], 16 * (g - 1))
                                act.copy(V[gp][:, :, 0, :, 0:dh], v32.rearrange("p (b h d) -> p b h d", b=GB, h=H)).then_inc(s["hi_v"], 1)
            rounds(act, iteration)

        def wide_place(job, gp):
            ps, i = PS[banks[job]], int(job[1])
            if job[0] == "v":
                src = ps[:].rearrange("p (h d) -> p h d", d=dh)
                h0 = 8 * (i % 2)
                return V[gp][:, i // 2, 0, h0:h0 + 8, 0:dh], V[gp][:, i // 2, 1, h0:h0 + 8, 0:dh], src
            buf = (K if job[0] == "k" else Q)[gp]
            src = ps[:].rearrange("p (j t) -> p j t", j=2)
            return buf[:, 0, 2 * i:2 * i + 2, :], buf[:, 1, 2 * i:2 * i + 2, :], src

        def vector(dve):
            dve.memset(mcat, 0.0).then_inc(s["ones_set"], 1)
            for p in range(2):
                for part in range(2):
                    last = dve.memset(V[p][:, :, part, :, dh:dh + 1], 1.0 - part)
            last.then_inc(s["ones_set"], 1)
            dve.wait_ge(s["ones_set"], 2)
            if not wide:
                dve.memset(K[0].rearrange("p c j t -> p (c j t)"), 0.0).then_inc(s["zeros_dve"], 1)

            def row_max(b, quad, bp):
                dve.wait_ge(s["s_ready"], 4 * b + quad + 1)
                if quad == 0:
                    wait(dve, s["m_split"], b - 1)
                at = 8 * (quad % 2) + 4 * (quad // 2) if wide else 4 * quad
                dve.tensor_reduce(m16[:, bp, at:at + 4], PS[quad % 2][:].rearrange("p (h k) -> p h k", h=4),
                                  AX, ALU.max).then_inc(s["max_done"], 1)

            def split_max(b, bp):
                dve.wait_ge(s["max_done"], 4 * b + 4)
                wait(dve, s["mt_ready"], b)
                if wide:
                    src = m16[:, bp, :].rearrange("p (j k) -> p j k", j=2)
                    mview = mcat.rearrange("p (j k) -> p j k", j=2)
                    hi, lo = mview[:, :, 0:8], mview[:, :, 16:24]
                else:
                    src, hi, lo = m16[:, bp, :], mcat[:, 0:16], mcat[:, 16:32]
                dve.tensor_scalar(hi, src, -1.0, None, ALU.mult).then_inc(s["m_chain"], 1)
                dve.wait_ge(s["m_chain"], b + 1)
                dve.scalar_tensor_tensor(lo, src, -1.0, hi, ALU.mult, ALU.subtract).then_inc(s["m_split"], 1)

            def normalise(b, units, bp, ob):
                for q in units:
                    n = 4 if wide else 16
                    cnt = (4 * b + q) if wide else b
                    ps = PS[4 + (q % 2 if wide else bp)][:, 0:n * (dh + 1)].rearrange("p (h d) -> p h d", h=n)
                    dve.wait_ge(s["pv_done"], 4 * b + q + 1)
                    rb = q % 2 if wide else bp
                    wait(dve, s["o_done"], cnt - 1)
                    dve.reciprocal(rec[:, rb, 0:n], ps[:, :, dh]).then_inc(s["rec_done"], 1)
                    dve.wait_ge(s["rec_done"], cnt + 1)
                    if wide:
                        if q == 0:
                            wait(dve, s["ot_ready"], 2 * (b - 1))
                        u, j = divmod(q, 2)
                        dst = o32[:, ob, :].rearrange("p (t j d) -> p t j d", j=2, d=dh)[:, 4 * u:4 * u + 4, j, :]
                    else:
                        wait(dve, s["ot_ready"], b - 1)
                        dst = o32[:, ob, :].rearrange("p (h d) -> p h d", h=16)
                    dve.tensor_tensor(dst, ps[:, :, 0:dh], rec[:, rb, 0:n].unsqueeze(2).to_broadcast([128, n, dh]),
                                      ALU.mult).then_inc(s["o_done"], 1)

            def low_half(b, quad):
                dve.wait_ge(s["exp_done"], 4 * b + quad + 1)
                wait(dve, s["pv_done"], 4 * b + quad - 3)
                dve.tensor_tensor(Plo[:, quad, :], P32[:, quad, :], Phi[:, quad, :], ALU.subtract).then_inc(s["plo_dve"], 1)

            def job_run(job, g, gp):
                ps = PS[banks[job]]
                if job == "yt":
                    return
                if job == "yb":
                    a = g - YT
                    if ok(a, NG):
                        dve.wait_ge(s["yb_ready"], a + 1)
                        xs = X[:, bass.ds(a * GB, GB), :]
                        dve.tensor_tensor(xs, xs, ps[:, 0:T].rearrange("p (b d) -> p b d", b=GB), ALU.add).then_inc(s["x_done"], 1)
                        dve.wait_ge(s["x_done"], a + 1)
                        for k in range(GB):
                            dve.bn_stats(stats[:, bass.ds(a * GB + k, 1), :], X[:, bass.ds(a * GB + k, 1), :])
                elif wide and job[0] == "v":
                    if ok(g - 1, NG):
                        dve.wait_ge(s["hi_v"], 4 * (g - 1) + int(job[1]) + 1)
                        hi, lo, src = wide_place(job, 1 - gp)
                        dve.scalar_tensor_tensor(lo, src, 1.0 / W_SCALE, hi, ALU.mult, ALU.subtract).then_inc(s["lo_v"], 1)
                elif not ok(g, NG):
                    return
                elif wide:
                    dve.wait_ge(s["kq_hi"], 8 * g + KQ_JOBS.index(job) + 1)
                    hi, lo, src = wide_place(job, gp)
                    dve.scalar_tensor_tensor(lo, src, 1.0 / W_SCALE, hi, ALU.mult, ALU.subtract).then_inc(s["kq_lo"], 1)
                elif job in ("kp2", "qp2"):
                    kind = job[0]
                    first = PS[banks[kind + "p"]][:].rearrange("p (b t) -> p b t", b=GB)
                    second = ps[:].rearrange("p (b t) -> p b t", b=GB)
                    dst = k32 if kind == "k" else q32
                    i = 0 if kind == "k" else 1
                    dve.wait_ge(s[f"{kind}p_ready"], 2 * g + 2)
                    wait(dve, s["turn_done"], 4 * g + 2 * i - 1 + 1)
                    dve.tensor_tensor(turn1.rearrange("p (b t) -> p b t", b=GB), first,
                                      rope[:, 0:1, :].to_broadcast([128, GB, 128]), ALU.mult).then_inc(s["turn_done"], 1)
                    dve.tensor_tensor(turn2.rearrange("p (b t) -> p b t", b=GB), second,
                                      rope[:, 1:2, :].to_broadcast([128, GB, 128]), ALU.mult).then_inc(s["turn_done"], 1)
                    dve.wait_ge(s["turn_done"], 4 * g + 2 * i + 2)
                    wait(dve, s["lo_kq"], 2 * (g - 1) + i + 1)
                    wait(dve, s[f"hi_{kind}"], g)
                    dve.tensor_tensor(dst, turn1, turn2, ALU.add).then_inc(s[f"{kind}32_done"], 1)
                    dve.wait_ge(s[f"{kind}32_done"], g + 1)
                elif job == "v":
                    dve.wait_ge(s["v_ready"], g + 1)
                    wait(dve, s["lo_v"], g)
                    dve.tensor_tensor(v32.rearrange("p (b d) -> p b d", b=GB), ps[:].rearrange("p (b d) -> p b d", b=GB),
                                      bv_row[:].unsqueeze(1).to_broadcast([128, GB, 128]), ALU.add).then_inc(s["v32_done"], 1)
                elif job[:3] == "sel" and int(job[4]) % 2 == 1:
                    kind, c = job[3], int(job[4])
                    dve.wait_ge(s[f"sel{kind}_ready"], 4 * g + c + 1)
                    if c == 1 and kind == "k":
                        wait(dve, s["k_spread"], 64 * g)
                    if c == 1 and kind == "q":
                        wait(dve, s["st_ready"], 16 * (g - 1))
                    dve.tensor_copy((K_stack if kind == "k" else Q[gp])[:, c, :], ps[:]).then_inc(s[f"sel{kind}_stored_v"], 1)

            def iteration(g, gp):
                for k in range(GB):
                    for q in range(4):
                        b0, b1, b2, b3, _ = stage(g, gp, k, q)
                        p0, p1, p2 = k % 2, (k - 1) % 2, k % 2
                        if q == 0:
                            if ok(b1, B): split_max(b1, p1)
                            if ok(b3, B): normalise(b3, (3,), p1, p1)
                        if wide and ok(b3, B):
                            for i in turns.get(q, []):
                                dve.wait_ge(s["ot_stored"], b3 * NOT + i + 1)
                                src = PS[banks[f"ot{k}_{i}"]][:].rearrange("p (c t) -> p c t", c=4)
                                hi, lo = (oT[:, x, 4 * i:4 * i + 4, 128 * (1 - k):128 * (1 - k) + 128] for x in range(2))
                                dve.tensor_tensor(lo, src, hi, ALU.subtract).then_inc(s["ot_lo"], 1)
                        if q == 1 and ok(b2, B): low_half(b2, 2)
                        if q == 3 and ok(b1, B): low_half(b1, 0)
                        if ok(b0, B): row_max(b0, q, p0)
                        if wide and q >= 1 and ok(b2, B): normalise(b2, (q - 1,), p2, p2)
                        for job in slots[k, q]: job_run(job, g, gp)
                        if wide and k == 0 and q == 3 and ok(g, NG):
                            for i, (dst, src) in enumerate(((c16, ctxT), (x16g, xnT))):
                                dve.wait_ge(s["in_hi"], 2 * g + i + 1)
                                dve.tensor_tensor(dst[:, 1, :], src[:, bass.ds(g * T, T)], dst[:, 0, :], ALU.subtract).then_inc(s["in_lo"], 1)
            rounds(dve, iteration)

        def gpsimd(pool):
            def low_half(b, quad):
                pool.wait_ge(s["exp_done"], 4 * b + quad + 1)
                wait(pool, s["pv_done"], 4 * b + quad - 3)
                pool.tensor_tensor(Plo[:, quad, :], P32[:, quad, :], Phi[:, quad, :], ALU.subtract).then_inc(s["plo_pool"], 1)

            def iteration(g, gp):
                for k in range(GB):
                    for q in range(4):
                        b0, b1, b2, b3, _ = stage(g, gp, k, q)
                        if q == 1 and ok(b2, B): low_half(b2, 3)
                        if q == 3 and ok(b1, B): low_half(b1, 1)
                        if wide or not ok(g, NG):
                            continue
                        if k == 0 and q in (1, 2):
                            kind, x32, hl = (("k", k32, khl), ("q", q32, qhl))[q - 1]
                            pool.wait_ge(s[f"hi_{kind}"], g + 1)
                            wait(pool, s[f"sel{kind}_ready"], 4 * g)
                            pool.tensor_tensor(hl[:, 1, :], x32, hl[:, 0, :], ALU.subtract).then_inc(s["lo_kq"], 1)
                        if k == 2 and q == 2:
                            pool.wait_ge(s["hi_v"], g + 1)
                            vsrc = v32.rearrange("p (b h d) -> p b h d", b=GB, h=H)
                            for b in range(GB):
                                last = pool.tensor_tensor(V[gp][:, b, 1, :, 0:dh], vsrc[:, b], V[gp][:, b, 0, :, 0:dh], ALU.subtract)
                            last.then_inc(s["lo_v"], 1)
            if not wide:
                pool.memset(K[1].rearrange("p c j t -> p (c j t)"), 0.0).then_inc(s["zeros_pool"], 1)
            rounds(pool, iteration)

        def sync(sp):
            if wide:
                return

            sp.wait_ge(s["zeros_dve"], 1)
            sp.wait_ge(s["zeros_pool"], 1)
            for g in range(NG):
                sp.wait_ge(s["selk_stored_a"], 2 * g + 2)
                sp.wait_ge(s["selk_stored_v"], 2 * g + 2)
                wait(sp, s["st_ready"], 16 * (g - 1))
                for j in range(4):
                    rows = slice(32 * j, 32 * j + 32)
                    sp.dma_start(K[g % 2][rows, :, j, :], K_stack[rows, :, :]).then_inc(s["k_spread"], 16)

        return dict(tensor=tensor, scalar=scalar, vector=vector, gpsimd=gpsimd, sync=sync)

    def stacks_tail_take(T):
        W_ffn.restart(W_ffn.size - 8 * T * 4)
        return W_ffn.take([2, 8, T], FP16)

    def att_halves():
        W_ffn.restart(8 * 1024)
        return {n: W_ffn.take([2, 1024], FP16) for n in ("wq", "wk", "wv", "wo")}

    def split_att_weights():
        h = att_halves()
        att_loads(2)
        W_att.restart()
        w = {n: W_att.take([1024], F32) for n in ("wq", "wk", "wv", "wo")}

        def scalar(act):
            act.wait_ge(att_loaded[2], att_loads(2)[1])
            for n in h:
                act.activation(h[n][:, 0, :], w[n], ACT.Copy, scale=W_SCALE).then_inc(att_w_hi, 1)

        def vector(dve):
            for i, n in enumerate(h):
                dve.wait_ge(att_w_hi, i + 1)
                dve.scalar_tensor_tensor(h[n][:, 1, :], w[n], W_SCALE, h[n][:, 0, :], ALU.mult, ALU.subtract).then_inc(att_w_lo, 1)
            dve.wait_ge(scale_ready[2], 2)
            dve.tensor_scalar(cols[:, 2, 6:7], cols[:, 2, 6:7], 1.0 / W_SCALE, None, ALU.mult).then_inc(att_w_lo, 1)
        return dict(scalar=scalar, vector=vector)

    ffn_loaded = [sem(f"ffn_loaded{l}") for l in range(4)]
    EXPERTS = {0: 8, 1: 16, 3: 8}
    TOP = {0: 2, 1: 4, 3: 1}
    TILES = {0: 11, 1: 9, 3: 32}

    def ffn_weights(l):
        W_ffn.restart()
        if l == 2:
            w = {n: W_ffn.take([D], F32) for n in ("wr", "wk", "wv")}
            w["mu"] = W_ffn.take([4], F32)
            loads = [(w[n], A[f"F2_{n}"]) for n in ("wr", "wk", "wv")] + [(w["mu"][:, 0:2], A["F2_mu"])]
            return w, loads
        n, E = TILES[l], EXPERTS[l]
        w = {"up": W_ffn.take([n * 128], F32), "down": W_ffn.take([n * 128], F32), "router": W_ffn.take([E], F32)}
        if l == 0:
            w["up2"] = W_ffn.take([n * 128], F32)
        loads = [(w[k], A[f"F{l}_{k}"]) for k in w]
        ngate = A[f"gate_sel{l}"].shape[1]
        loads.append((gate_sel[:, 0:ngate], A[f"gate_sel{l}"]))
        if l == 3:
            w["b1"] = W_ffn.take([n], F32)
            loads.append((w["b1"], A["F3_b1"]))
            loads.append((b2_rows[:], A["F3_b2"]))
            loads.append((br_row[:], bcast_rows(A["F3_br"], 128)))
        return w, loads

    def halves_of(l):
        stacks.restart()
        n, E = TILES[l], EXPERTS[l]
        sizes = {"up": n * 128, "up2": n * 128 if l == 0 else 0, "down": n * 128, "router": E}
        return {k: stacks.take([2, m], FP16) for k, m in sizes.items() if m}

    def split_weights(l):
        w, loads = ffn_weights(l)
        h = halves_of(l)
        hi_done, lo_done, y_scaled = (phase_sem("experts", k) for k in ("w_hi_done", "w_lo_done", "y_scaled"))

        def high(act, names):
            act.wait_ge(ffn_loaded[l], 16 * len(loads))
            for k in names:
                act.activation(h[k][:, 0, :], w[k], ACT.Copy, scale=W_SCALE).then_inc(hi_done, 1)

        def vector(dve):
            for i, k in enumerate(h):
                dve.wait_ge(hi_done, i + 1)
                dve.scalar_tensor_tensor(h[k][:, 1, :], w[k], W_SCALE, h[k][:, 0, :], ALU.mult, ALU.subtract).then_inc(lo_done, 1)
            dve.tensor_scalar(y_scale[:], gates[:, 4 + l:5 + l], 1.0 / (W_SCALE * HID_SCALE), None, ALU.mult).then_inc(y_scaled, 1)
        names = list(h)
        return dict(scalar=lambda act: high(act, names[:1])), dict(scalar=lambda act: high(act, names[1:]), vector=vector)

    def ffn_load_phase(l):
        def sync(sp):
            for dst, src in ffn_weights(l)[1]:
                sp.dma_start(dst, src).then_inc(ffn_loaded[l], 16)
        return dict(sync=sync)

    def router(l):
        E, top = EXPERTS[l], TOP[l]
        halves = halves_of(l)
        unscale = 1.0 / (W_SCALE * X_SCALE)
        w, loads = ffn_weights(l)
        work.restart()
        logits = work.take([B, E], F32)
        e = work.take([B, E], F32)
        rest = work.take([B, E], F32)
        gate = work.take([B, E], F32)
        part = work.take([B, 3, E], BF16)
        best = work.take([B, 8], F32)
        red = work.take([3, B], F32)
        logit_ready, exp_ready, step, part_ready, turned, turned_out = (
            phase_sem("router", n) for n in ("logit_ready", "exp_ready", "step", "part_ready", "turned", "turned_out"))

        def tensor(pe):
            pe.wait_ge(ffn_loaded[l], 16 * len(loads))
            for b in range(B):
                for i, (x, r) in enumerate(((0, 0), (0, 1), (1, 0))):
                    last = pe.matmul(PS[0][:, E * b:E * b + E], x16[:, x, 128 * b:128 * b + 128], halves["router"][:, r, :],
                                     start=(i == 0), stop=(i == 2))
            last.then_inc(logit_ready, 1)
            pe.wait_ge(part_ready, 1)
            for i in range(NG4):
                wait(pe, turned_out, i - 1)
                for k in range(4):
                    b = 4 * i + k
                    last = pe.transpose(PS[1 + i % 2][:].bitcast(BF16)[0:3 * E, 128 * k:128 * k + 128],
                                        part[:, b, :, :].rearrange("p a e -> p (a e)"), ident_b[:])
                last.then_inc(turned, 1)

        def scalar(act):
            act.wait_ge(step, 3)
            act.activation(e, logits, ACT.Exp).then_inc(exp_ready, 1)
            for i in range(NG4):
                act.wait_ge(turned, i + 1)
                act.copy(gateT[0:3 * E, 512 * i:512 * i + 512], PS[1 + i % 2][:].bitcast(BF16)[0:3 * E, 0:512]).then_inc(turned_out, 1)

        def vector(dve):
            n = [0]

            def chain(ins):
                n[0] += 1
                ins.then_inc(step, 1)
                dve.wait_ge(step, n[0])
            dve.wait_ge(logit_ready, 1)
            ps = PS[0][:, 0:B * E].rearrange("p (b e) -> p b e", e=E)
            if l == 3:
                chain(dve.scalar_tensor_tensor(logits, ps, unscale, br_row[:].unsqueeze(1).to_broadcast([128, B, E]), ALU.mult, ALU.add))
            else:
                chain(dve.tensor_scalar(logits, ps, unscale, None, ALU.mult))
            chain(dve.tensor_reduce(red[:, 0, :], logits, AX, ALU.max))
            chain(dve.tensor_tensor(logits, logits, red[:, 0, :].unsqueeze(2).to_broadcast([128, B, E]), ALU.subtract))
            dve.wait_ge(exp_ready, 1)
            dve.tensor_reduce(red[:, 1, :], e, AX, ALU.add)
            for b in range(B):
                last = dve.max(best[:, b, :], e[:, b, :])
            chain(last)
            dve.reciprocal(red[:, 2, :], red[:, 1, :])
            chain(dve.memset(best[:, :, top:8], -1.0))
            for b in range(B):
                last = dve.match_replace(rest[:, b, :], best[:, b, :], e[:, b, :], -1.0)
            chain(last)
            chain(dve.scalar_tensor_tensor(gate, rest, 0.0, e, ALU.is_lt, ALU.mult))
            chain(dve.tensor_tensor(gate, gate, red[:, 2, :].unsqueeze(2).to_broadcast([128, B, E]), ALU.mult))
            chain(dve.tensor_copy(part[:, :, 0, :], gate))
            chain(dve.tensor_tensor(gate, gate, part[:, :, 0, :], ALU.subtract))
            chain(dve.tensor_copy(part[:, :, 1, :], gate))
            chain(dve.tensor_tensor(gate, gate, part[:, :, 1, :], ALU.subtract))
            dve.tensor_copy(part[:, :, 2, :], gate).then_inc(part_ready, 1)
            if l == 3:
                chain(dve.tensor_scalar(b2_rows[:], b2_rows[:], W_SCALE * HID_SCALE, None, ALU.mult))
                chain(dve.tensor_copy(b2_part[:, 0, :], b2_rows[:]))
                chain(dve.tensor_tensor(b2_rest[:], b2_rows[:], b2_part[:, 0, :], ALU.subtract))
                chain(dve.tensor_copy(b2_part[:, 1, :], b2_rest[:]))
                chain(dve.tensor_tensor(b2_rest[:], b2_rest[:], b2_part[:, 1, :], ALU.subtract))
                chain(dve.tensor_copy(b2_part[:, 2, :], b2_rest[:]))

        return dict(tensor=tensor, scalar=scalar, vector=vector)

    def experts(l):
        n, E = TILES[l], EXPERTS[l]
        w, loads = ffn_weights(l)
        halves = halves_of(l)
        func = ACT.Silu if l == 0 else ACT.Gelu
        LAG = 3
        work.restart()
        act_out = work.take([3, 512], F32)
        prod = work.take([3, 512], F32)
        hid = work.take([3, 512], F32)
        NH = 5 if n % 4 == 1 else 4
        hid16 = work.take([NH, 2, 512], FP16)
        y32 = work.take([512], F32)
        up_ready, act_done, prod_done, hid_done, hi_done, lo_dve, lo_pool, down_done, y_stored, yb_ready, x_done = (
            phase_sem("experts", k) for k in ("up_ready", "act_done", "prod_done", "hid_done", "hi_done", "lo_dve", "lo_pool",
                                              "down_done", "y_stored", "yb_ready", "x_done"))
        lo_on_dve = [t % 2 == 0 for t in range(n)]
        per_group = {True: sum(lo_on_dve), False: n - sum(lo_on_dve)}

        def before(t, m):
            return m if t >= m else t + n - max(x for x in range(n) if x % m == t)

        def gate_of(t):
            return {0: t, 1: t - 1 if t else None, 3: t // 4}[l]

        def gate_bank(t):
            return PS[4 + ((t // 4) % 2 if l == 3 else t % 2)]

        def low_count(g, t):
            return g * per_group[lo_on_dve[t]] + lo_on_dve[:t + 1].count(lo_on_dve[t])

        def ok(g):
            return not isinstance(g, int) or 0 <= g < NG4

        def rounds(eng, group):
            group(0)
            if NG4 > 1:
                with eng.Fori(1, NG4) as g:
                    group(g)
            group(NG4)

        def behind(g, t, lag):
            g, t = (g, t - lag) if t >= lag else (g - 1, t - lag + n)
            return (g, t) if ok(g) else None

        def tensor(pe):
            def product(dst, a, b, start=True, stop=True):
                for i, (x, y) in enumerate(((0, 0), (0, 1), (1, 0))):
                    last = pe.matmul(dst, a(x), b(y), start=(start and i == 0), stop=(stop and i == 2))
                return last

            def down(g, t):
                pe.wait_ge(lo_dve if lo_on_dve[t] else lo_pool, low_count(g, t))
                if t == 0:
                    wait(pe, y_stored, g)
                    if l == 3:
                        for p in range(3):
                            pe.matmul(PS[6][:], b2_part[:, p, :], gateT[:, bass.ds(g * 512, 512)], start=(p == 0), stop=False)
                product(PS[6][:], lambda x: halves["down"][:, x, 128 * t:128 * t + 128], lambda y: hid16[:, t % NH, y, :],
                        start=(t == 0 and l != 3), stop=(t == n - 1)).then_inc(down_done, 1)

            def group(g):
                for t in range(n):
                    late = behind(g, t, LAG)
                    first = t == 0 and n % 2
                    if late and first:
                        down(*late)
                    if ok(g):
                        tok = bass.ds(g * 512, 512)
                        N = g * n + t
                        gt = gate_of(t)
                        if l == 0:
                            wait(pe, prod_done, N - before(t, 2) + 1)
                            product(PS[2 + t % 2][:], lambda x: halves["up2"][:, x, 128 * t:128 * t + 128], lambda y: x16[:, y, tok])
                        if gt is not None and (l != 3 or t % 4 == 0):
                            wait(pe, hid_done, N - 4 if l == 3 else N - before(t, 2) + 1)
                            pe.matmul(gate_bank(t)[:], gate_sel[:, 128 * gt:128 * gt + 128], gateT[:, tok], start=True, stop=True)
                        wait(pe, act_done, N - before(t, 2) + 1)
                        product(PS[t % 2][:], lambda x: halves["up"][:, x, 128 * t:128 * t + 128],
                                lambda y: x16[:, y, tok]).then_inc(up_ready, 1)
                    if late and not first:
                        down(*late)
                    if t == 6 and ok(g - 1):
                        pe.wait_ge(y_stored, g)
                        wait(pe, x_done, g - 1)
                        for k in range(4):
                            last = pe.transpose(PS[7][:, 128 * k:128 * k + 128], y32[:, 128 * k:128 * k + 128], ident[:])
                        last.then_inc(yb_ready, 1)
            rounds(pe, group)

        def scalar(act):
            def group(g):
                for t in range(n):
                    if t == LAG and ok(g - 1):
                        act.wait_ge(down_done, g * n)
                        wait(act, yb_ready, g - 1)
                        act.activation(y32, PS[6][:], ACT.Copy, scale=y_scale[:]).then_inc(y_stored, 1)
                    if ok(g):
                        N = g * n + t
                        act.wait_ge(up_ready, N + 1)
                        wait(act, prod_done if l == 0 else hid_done, N - before(t, 3) + 1)
                        act.activation(act_out[:, t % 3, :], PS[t % 2][:], func, scale=1.0 / (W_SCALE * X_SCALE),
                                       **(dict(bias=w["b1"][:, t:t + 1]) if l == 3 else {})).then_inc(act_done, 1)
                    late = behind(g, t, 1)
                    if late:
                        N = late[0] * n + late[1]
                        act.wait_ge(hid_done, N + 1)
                        wait(act, down_done, N - before(late[1], NH) + 1)
                        act.copy(hid16[:, late[1] % NH, 0, :], hid[:, late[1] % 3, :]).then_inc(hi_done, 1)
            rounds(act, group)

        def low_half(eng, g, t):
            N = g * n + t
            eng.wait_ge(hi_done, N + 1)
            eng.tensor_tensor(hid16[:, t % NH, 1, :], hid[:, t % 3, :], hid16[:, t % NH, 0, :], ALU.subtract).then_inc(
                lo_dve if lo_on_dve[t] else lo_pool, 1)

        def vector(dve):
            def group(g):
                for t in range(n):
                    if ok(g):
                        N = g * n + t
                        dve.wait_ge(act_done, N + 1)
                        src = act_out[:, t % 3, :]
                        if l == 0:
                            wait(dve, hid_done, N - before(t, 2) + 1)
                            dve.tensor_tensor(prod[:, t % 3, :], src, PS[2 + t % 2][:], ALU.mult).then_inc(prod_done, 1)
                            dve.wait_ge(prod_done, N + 1)
                            src = prod[:, t % 3, :]
                        prev = behind(g, t, before(t, 3))
                        if prev:
                            dve.wait_ge(lo_dve if lo_on_dve[prev[1]] else lo_pool, low_count(*prev))
                        if gate_of(t) is None:
                            last = dve.tensor_scalar(hid[:, t % 3, :], src, HID_SCALE, None, ALU.mult)
                        else:
                            last = dve.tensor_tensor(hid[:, t % 3, :], src, gate_bank(t)[:], ALU.mult)
                        last.then_inc(hid_done, 1)
                    late = behind(g, t, 1)
                    if late and lo_on_dve[late[1]]:
                        low_half(dve, *late)
                    if t == 7 and ok(g - 1):
                        dve.wait_ge(yb_ready, g)
                        xs = X[:, bass.ds((g - 1) * 4, 4), :]
                        dve.tensor_tensor(xs, xs, PS[7][:].rearrange("p (b d) -> p b d", b=4), ALU.add).then_inc(x_done, 1)
                        dve.wait_ge(x_done, g)
                        for k in range(4):
                            dve.bn_stats(stats[:, bass.ds((g - 1) * 4 + k, 1), :], X[:, bass.ds((g - 1) * 4 + k, 1), :])
            rounds(dve, group)

        def gpsimd(pool):
            def group(g):
                for t in range(n):
                    if ok(g) and not lo_on_dve[t]:
                        low_half(pool, g, t)
            rounds(pool, group)

        return dict(tensor=tensor, scalar=scalar, vector=vector, gpsimd=gpsimd)

    def token_mix():
        w, loads = ffn_weights(2)
        work.restart()
        faded = work.take([2, 512], F32)
        mixed = work.take([2, 2, 512], F32)
        r_gate = work.take([2, 512], F32)
        relu = work.take([512], F32)
        squared = work.take([2, 512], F32)
        y32 = work.take([2, 512], F32)
        mu, rest = w["mu"][:, 0:2], w["mu"][:, 2:4]
        mu_ready, faded_done, mixed_done, rk_ready, r_done, relu_done, sq_done, v_ready, y_done, yb_ready, x_done = (
            sem(f"T_{k}") for k in ("mu_ready", "faded_done", "mixed_done", "rk_ready", "r_done", "relu_done",
                                    "sq_done", "v_ready", "y_done", "yb_ready", "x_done"))

        def ok(g):
            return not isinstance(g, int) or 0 <= g < NG4

        def rounds(eng, step):
            for g in range(4):
                step(g, g % 2)
            if NG4 > 4:
                with eng.Fori(2, NG4 // 2) as r:
                    step(2 * r, 0)
                    step(2 * r + 1, 1)
            step(NG4, 0)
            step(NG4 + 1, 1)

        def tensor(pe):
            pe.wait_ge(ffn_loaded[2], 16 * len(loads))

            def step(g, p):
                if ok(g):
                    pe.wait_ge(mixed_done, g + 1)
                    wait(pe, r_done, g - 1)
                    wait(pe, relu_done, g - 1)
                    pe.matmul(PS[p][:], w["wr"], mixed[:, p, 0, :], start=True, stop=True)
                    pe.matmul(PS[2 + p][:], w["wk"], mixed[:, p, 1, :], start=True, stop=True).then_inc(rk_ready, 1)
                if ok(g - 1):
                    pe.wait_ge(sq_done, g)
                    wait(pe, y_done, g - 2)
                    pe.matmul(PS[5 - p][:], w["wv"], squared[:, 1 - p, :], start=True, stop=True).then_inc(v_ready, 1)
                if ok(g - 2):
                    pe.wait_ge(y_done, g - 1)
                    wait(pe, x_done, g - 3)
                    for k in range(4):
                        last = pe.transpose(PS[6 + p][:, 128 * k:128 * k + 128], y32[:, p, 128 * k:128 * k + 128], ident[:])
                    last.then_inc(yb_ready, 1)
            rounds(pe, step)

        def scalar(act):
            def step(g, p):
                if ok(g):
                    act.wait_ge(rk_ready, g + 1)
                    wait(act, y_done, g - 1)
                    act.activation(r_gate[:, p, :], PS[p][:], ACT.Sigmoid).then_inc(r_done, 1)
            rounds(act, step)

        def vector(dve):
            dve.wait_ge(ffn_loaded[2], 16 * len(loads))
            dve.tensor_scalar(rest, mu, -1.0, 1.0, ALU.mult, ALU.add).then_inc(mu_ready, 1)
            dve.wait_ge(mu_ready, 1)

            def step(g, p):
                if ok(g):
                    x = xnT[:, bass.ds(g * 512, 512)]
                    xs = x.rearrange("p (b t) -> p b t", b=4)
                    wait(dve, mixed_done, g)
                    for i in range(2):
                        last = dve.tensor_scalar(faded[:, i, :], x, rest[:, i:i + 1], None, ALU.mult)
                    last.then_inc(faded_done, 1)
                    dve.wait_ge(faded_done, g + 1)
                    wait(dve, rk_ready, g - 1)
                    for i in range(2):
                        m = mixed[:, p, i, :].rearrange("p (b t) -> p b t", b=4)
                        f = faded[:, i, :].rearrange("p (b t) -> p b t", b=4)
                        dve.tensor_scalar(m[:, :, 0:1], xs[:, :, 0:1], mu[:, i:i + 1], None, ALU.mult)
                        last = dve.scalar_tensor_tensor(m[:, :, 1:128], xs[:, :, 1:128], mu[:, i:i + 1], f[:, :, 0:127], ALU.mult, ALU.add)
                    last.then_inc(mixed_done, 1)
                if ok(g - 1):
                    q = 1 - p
                    dve.wait_ge(rk_ready, g)
                    wait(dve, sq_done, g - 1)
                    dve.tensor_scalar(relu, PS[2 + q][:], 0.0, None, ALU.max).then_inc(relu_done, 1)
                    dve.wait_ge(relu_done, g)
                    wait(dve, v_ready, g - 2)
                    dve.tensor_tensor(squared[:, q, :], relu, relu, ALU.mult).then_inc(sq_done, 1)
                    dve.wait_ge(v_ready, g)
                    dve.wait_ge(r_done, g)
                    wait(dve, yb_ready, g - 2)
                    dve.scalar_tensor_tensor(y32[:, q, :], PS[5 - p][:], gates[:, 6:7], r_gate[:, q, :], ALU.mult, ALU.mult).then_inc(y_done, 1)
                if ok(g - 2):
                    dve.wait_ge(yb_ready, g - 1)
                    xs = X[:, bass.ds((g - 2) * 4, 4), :]
                    dve.tensor_tensor(xs, xs, PS[6 + p][:].rearrange("p (b d) -> p b d", b=4), ALU.add).then_inc(x_done, 1)
                    dve.wait_ge(x_done, g - 1)
                    for k in range(4):
                        dve.bn_stats(stats[:, bass.ds((g - 2) * 4 + k, 1), :], X[:, bass.ds((g - 2) * 4 + k, 1), :])
            rounds(dve, step)

        return dict(tensor=tensor, scalar=scalar, vector=vector)

    def feed_forward(l):
        return [token_mix()] if l == 2 else [router(l), experts(l)]

    att_loaded = [sem(f"att_loaded{l}") for l in range(4)]

    def att_loads(l):
        W_att.restart()
        inner = H * HEAD_DIMS[l]
        nchunk = inner // 128
        dst = {n: W_att.take([inner], F32) for n in ("wq", "wk", "wv")}
        dst["wo"] = W_att.take([nchunk * D], F32)
        loads = [(dst[n], A[f"L{l}_{n}"]) for n in ("wq", "wk", "wv", "wo")]
        if l == 0:
            loads += [(W_att.take([D], F32), A["L0_wq_turn"]), (W_att.take([D], F32), A["L0_wk_turn"])]
        loads.append((cols[:, l, 0:3], A[f"L{l}_cols"][:, 0:3]))
        if l == 2:
            loads.append((cols[:, l, 4:6], A["L2_cols"][:, 3:5]))
        else:
            loads.append((bv_row[:], bcast_rows(A[f"L{l}_bv"], 128)))
        return loads, 16 * len(loads)

    def att_scales(l):
        def vector(dve):
            dve.wait_ge(att_loaded[l], att_loads(l)[1])
            if l == 2:
                dve.tensor_tensor(cols[:, l, 6:7], gates[:, l:l + 1], gates[:, 8:9], ALU.mult).then_inc(scale_ready[l], 1)
            else:
                dve.tensor_copy(cols[:, l, 6:7], gates[:, l:l + 1]).then_inc(scale_ready[l], 1)
            dve.wait_ge(scale_ready[l], 1)
            dve.tensor_tensor(cols[:, l, 3:4], cols[:, l, 2:3], cols[:, l, 6:7], ALU.mult).then_inc(scale_ready[l], 1)
        return dict(vector=vector)

    scale_ready = [sem(f"scale_ready{l}") for l in range(4)]
    att_w_hi, att_w_lo = sem("att_w_hi"), sem("att_w_lo")

    phases = [dict(tensor=setup_tensor, scalar=setup_scalar, vector=setup_vector, sync=setup_sync)]

    def att_load_phase(l):
        def sync(sp):
            for dst, src in att_loads(l)[0]:
                sp.dma_start(dst, src).then_inc(att_loaded[l], 16)
        return dict(sync=sync)

    plan, ran = [], []
    for l in range(4):
        plan += [("att", l), ("ffn", l)]
    phases[0] = merge(phases[0], att_load_phase(0 if isinstance(upto, int) else upto[0][1]) if isinstance(upto, int) or upto[0][0] == "att" else ffn_load_phase(upto[0][1]))
    for kind, l in (plan[:upto] if isinstance(upto, int) else upto):
        if kind == "att":
            first = merge(att_scales(l), ffn_load_phase(l))
            while ran:
                first = merge(first, clear(ran.pop()))
            phases.append(first)
            if l == 2:
                phases.append(layer_norm("first"))
                phases.append(merge(layer_norm("second"), split_att_weights()))
            else:
                phases.append(layer_norm())
            phases.append(attention(l))
            ran.append("att")
        else:
            norm = layer_norm(halves=(l != 2))
            if ran:
                norm = merge(norm, clear(ran.pop()))
            if l != 2:
                first, others = split_weights(l)
                norm = merge(merge(first, norm), others)
            phases.append(norm)
            phases += feed_forward(l)
            if l != 2:
                ran += ["router", "experts"]
            if l < 3 and (isinstance(upto, int) or ("att", l + 1) in upto):
                phases[-1] = merge(phases[-1], att_load_phase(l + 1))

    stored = sem("stored")

    def store(sp):
        sp.dma_start(out.rearrange("b t d -> t b d"), X[:]).then_inc(stored, 16)
        sp.wait_ge(stored, 16)

    block = ctx.enter_context(nc.Block())

    def run(eng, name):
        for ph in phases:
            if name in ph:
                ph[name](eng)
            meet(eng)

    @block.sync
    def _(sp):
        run(sp, "sync")
        store(sp)

    @block.tensor
    def _(pe):
        run(pe, "tensor")

    @block.scalar
    def _(act):
        run(act, "scalar")

    @block.vector
    def _(dve):
        run(dve, "vector")

    @block.gpsimd
    def _(pool):
        run(pool, "gpsimd")


def merge(a, b):
    out = dict(a)
    for k, f in b.items():
        out[k] = (lambda e, p=a[k], q=f: (p(e), q(e))) if k in a else f
    return out


def bcast_rows(v, n):
    return v.rearrange("(a n) -> a n", a=1).to_broadcast([n, v.shape[0]])


def arrays_of(inputs):
    a = {k: np.asarray(v) for k, v in inputs.items()}
    B = a["x"].shape[0]
    f = {"x": a["x"], "ctx": a["ctx_1024"], "g_xattn": a["g_xattn"], "g_ffn": a["g_ffn"], "L2_gate": a["L2_xattn_gate"]}
    z = np.zeros((128,), np.float32)

    def turned(w):
        return w.reshape(64, 2, 128)[:, ::-1, :].reshape(128, 128)
    for l in (0, 1, 3):
        if l == 3:
            w = a["L3_xattn_in_proj_weight"]
            bb = a["L3_xattn_in_proj_bias"]
            wq, wk, wv, wo = w[0:128], w[128:256], w[256:384], a["L3_xattn_out_w"]
            bq, bk, bv, bo = bb[0:128], bb[128:256], bb[256:384], a["L3_xattn_out_b"]
        else:
            wq, wk, wv, wo = (a[f"L{l}_xattn_W{n}"] for n in "qkvo")
            bq, bk, bv, bo = (a[f"L1_xattn_b{n}"] for n in "qkvo") if l == 1 else (z, z, z, z)
        f[f"L{l}_wq"], f[f"L{l}_wk"], f[f"L{l}_wv"], f[f"L{l}_wo"] = wq.T, wk.T, wv.T, wo.T
        if l == 0:
            f["L0_wq_turn"], f["L0_wk_turn"] = turned(wq).T, turned(wk).T
        f[f"L{l}_cols"] = np.stack([bq, bk, bo], 1)
        f[f"L{l}_bv"] = bv
    f["L2_wq"] = a["L2_xattn_w_q"]
    f["L2_wk"] = a["L2_xattn_w_kv"][:, 0:1024]
    f["L2_wv"] = a["L2_xattn_w_kv"][:, 1024:2048]
    f["L2_wo"] = a["L2_xattn_w_out"].reshape(8, 128, 128).transpose(1, 0, 2).reshape(128, 1024)
    f["L2_cols"] = np.stack([z, z, a["L2_xattn_b_out"], a["L2_xattn_ln_gamma"], a["L2_xattn_ln_beta"]], 1)
    f["F0_up"], f["F0_up2"] = (a[f"L0_ffn_{n}"].transpose(1, 0, 2).reshape(128, 1408) for n in ("w1", "w3"))
    f["F0_down"] = rows_by_tile(a["L0_ffn_w2"].reshape(1408, 128))
    f["F0_router"] = a["L0_ffn_w_router"].T
    up = np.concatenate([a["L1_ffn_shared_up"], a["L1_ffn_routed_up"]], 0)
    down = np.concatenate([a["L1_ffn_shared_down"], a["L1_ffn_routed_down"]], 0)
    f["F1_up"] = up.reshape(1152, 128).T
    f["F1_down"] = rows_by_tile(down.transpose(0, 2, 1).reshape(1152, 128))
    f["F1_router"] = a["L1_ffn_router_w"].T
    f["F2_wr"], f["F2_wk"], f["F2_wv"] = (a[f"L2_ffn_W_{n}"].T for n in "rkv")
    f["F2_mu"] = np.stack([a["L2_ffn_mu_r"], a["L2_ffn_mu_k"]], 1)
    f["F3_up"] = a["L3_ffn_W1"].transpose(1, 0, 2).reshape(128, 4096)
    f["F3_down"] = rows_by_tile(a["L3_ffn_W2"].reshape(4096, 128))
    f["F3_router"], f["F3_br"] = a["L3_ffn_Wr"], a["L3_ffn_br"]
    f["F3_b1"] = a["L3_ffn_b1"].reshape(32, 128).T
    f["F3_b2"] = np.concatenate([np.tile(a["L3_ffn_b2"], (3, 1)), np.zeros((104, 128), np.float32)], 0)
    f.update(shape_constants(B))
    return {k: np.ascontiguousarray(v) for k, v in f.items()}


def rows_by_tile(w):
    return w.reshape(-1, 128, 128).transpose(1, 0, 2).reshape(128, -1)


def kernel(**inputs):
    import concourse.bacc as _bacc
    from concourse.bass_utils import run_bass_kernel_spmd as _run

    nc = _bacc.Bacc("TRN2", target_bir_lowering=False, num_devices=1)
    arrays = {f"in_{k}": v for k, v in arrays_of(inputs).items()}
    A = {k[3:]: nc.dram_tensor(k, v.shape, mybir.dt.from_np(v.dtype), kind="ExternalInput").ap() for k, v in arrays.items()}
    B = inputs["x"].shape[0]
    out = nc.dram_tensor("out_x", (B, S, D), F32, kind="ExternalOutput").ap()
    program(nc, A, out, B)
    r = _run(nc, [arrays], core_ids=[0])
    return r.results[0]["out_x"]
```
